# Optimizing a Trainium2 kernel written in Bass

```python
import numpy as np
import jax
import jax.numpy as jnp

def _softmax(x, axis=-1):
    return jax.nn.softmax(x, axis=axis)

def _gelu(x):
    return jax.nn.gelu(x, approximate=True)

def _silu(x):
    return jax.nn.silu(x)

def _sigmoid(x):
    return jax.nn.sigmoid(x)

def _layernorm(x, axis=-1, eps=1e-05):
    m = jnp.mean(x, axis=axis, keepdims=True)
    v = jnp.var(x, axis=axis, keepdims=True)
    return (x - m) / jnp.sqrt(v + eps)

def _scatter_add(tgt, idx, src, axis=0):
    return tgt.at[idx].add(src)

def _segment_sum(src, seg, n):
    return jax.ops.segment_sum(src, seg, n)
kernel_name = 'mk_vit_tower_d1_tok_img768_r4_237689'

def setup_inputs(seed: int=0):
    np.random.seed(seed)
    _w = jnp.asarray

    def _rec_inputs():
        import jax
        import jax.numpy as jnp
        _rk = jax.random.key(seed)
        x = -0.000147625 + 0.999875 * jax.random.normal(jax.random.fold_in(_rk, 1), (64, 3, 224, 224), jnp.float32)
        return x
    x = _rec_inputs()

    def _L0_tok_setup():
        import jax, jax.numpy as jnp
        import numpy as np
        N_PATCHES = 14

        def _patchify(images, n_patches):
            n, c, h, w = images.shape
            ps = h // n_patches
            x = images.reshape(n, c, n_patches, ps, n_patches, ps)
            x = x.transpose(0, 2, 4, 1, 3, 5)
            return x.reshape(n, n_patches * n_patches, c * ps * ps)
        key = jax.random.key(seed)
        k1, k2, k3 = jax.random.split(key, 3)
        batch, c, h, w = (64, 3, 224, 224)
        input_dim = c * (h // N_PATCHES) * (w // N_PATCHES)
        hidden_d = 192
        images = jax.random.normal(k1, (batch, c, h, w), dtype=jnp.float32)
        W = jax.random.normal(k2, (hidden_d, input_dim), dtype=jnp.float32) * input_dim ** (-0.5)
        b = jax.random.normal(k3, (hidden_d,), dtype=jnp.float32) * 0.01
        return {'images': images, 'W': W, 'b': b}
    _L0_tok_all = _L0_tok_setup()
    _L0_tok_in = {k: v for k, v in _L0_tok_all.items() if k in ('W', 'b')}
    del _L0_tok_all

    def _L0_attn_setup():
        import jax, jax.numpy as jnp
        import numpy as np
        ALPHA = 0.35

        def _round_ln_pow2(x):
            y = jnp.floor(jnp.log2(x))
            up = x - 2.0 ** y > 2.0 ** (y + 1.0) - x
            return 2.0 ** (y + up.astype(x.dtype))
        key = jax.random.key(seed)
        k1, k2, k3, k4, k5 = jax.random.split(key, 5)
        B, N, C = (64, 197, 192)
        return {'x': jax.random.normal(k1, (B, N, C), dtype=jnp.float32), 'qkv_weight': jax.random.normal(k2, (3 * C, C), dtype=jnp.float32) * 0.02, 'qkv_bias': jax.random.normal(k3, (3 * C,), dtype=jnp.float32) * 0.02, 'proj_weight': jax.random.normal(k4, (C, C), dtype=jnp.float32) * 0.02, 'proj_bias': jax.random.normal(k5, (C,), dtype=jnp.float32) * 0.02}
    _L0_attn_all = _L0_attn_setup()
    _L0_attn_in = {k: v for k, v in _L0_attn_all.items() if k in ('qkv_weight', 'qkv_bias', 'proj_weight', 'proj_bias')}
    del _L0_attn_all

    def _L0_ffn_setup():
        import jax, jax.numpy as jnp
        import numpy as np
        B, N, C, H, E = (8, 256, 192, 768, 4)
        key = jax.random.key(seed)
        ks = jax.random.split(key, 8)
        s_in = 1.0 / np.sqrt(C)
        s_h = 1.0 / np.sqrt(H)
        return {'x': jax.random.normal(ks[0], (B, N, C), dtype=jnp.float32), 'gate_w': jax.random.normal(ks[1], (C, E), dtype=jnp.float32) * 0.01, 'gate_b': jnp.zeros((E,), dtype=jnp.float32), 'gate_center': jnp.zeros((E,), dtype=jnp.float32), 'w1': jax.random.uniform(ks[2], (E, C, H), jnp.float32, -s_in, s_in), 'b1': jax.random.uniform(ks[3], (E, H), jnp.float32, -s_in, s_in), 'w2': jax.random.uniform(ks[4], (E, H, C), jnp.float32, -s_h, s_h), 'b2': jax.random.uniform(ks[5], (E, C), jnp.float32, -s_h, s_h)}
    _L0_ffn_all = _L0_ffn_setup()
    _L0_ffn_in = {k: v for k, v in _L0_ffn_all.items() if k in ('gate_w', 'gate_b', 'gate_center', 'w1', 'b1', 'w2', 'b2')}
    del _L0_ffn_all
    return {'x': x, 'L0_tok_W': _L0_tok_in['W'], 'L0_tok_b': _L0_tok_in['b'], 'L0_attn_qkv_weight': _L0_attn_in['qkv_weight'], 'L0_attn_qkv_bias': _L0_attn_in['qkv_bias'], 'L0_attn_proj_weight': _L0_attn_in['proj_weight'], 'L0_attn_proj_bias': _L0_attn_in['proj_bias'], 'L0_ffn_gate_w': _L0_ffn_in['gate_w'], 'L0_ffn_gate_b': _L0_ffn_in['gate_b'], 'L0_ffn_gate_center': _L0_ffn_in['gate_center'], 'L0_ffn_w1': _L0_ffn_in['w1'], 'L0_ffn_b1': _L0_ffn_in['b1'], 'L0_ffn_w2': _L0_ffn_in['w2'], 'L0_ffn_b2': _L0_ffn_in['b2']}

def reference(x, L0_tok_W, L0_tok_b, L0_attn_qkv_weight, L0_attn_qkv_bias, L0_attn_proj_weight, L0_attn_proj_bias, L0_ffn_gate_w, L0_ffn_gate_b, L0_ffn_gate_center, L0_ffn_w1, L0_ffn_b1, L0_ffn_w2, L0_ffn_b2):
    import jax
    import jax.numpy as jnp

    def _L0_tok_ref(images, W, b):
        import jax, jax.numpy as jnp
        import numpy as np
        N_PATCHES = 14

        def _patchify(images, n_patches):
            n, c, h, w = images.shape
            ps = h // n_patches
            x = images.reshape(n, c, n_patches, ps, n_patches, ps)
            x = x.transpose(0, 2, 4, 1, 3, 5)
            return x.reshape(n, n_patches * n_patches, c * ps * ps)
        patches = _patchify(images, N_PATCHES)
        tokens = jnp.einsum('npd,hd->nph', patches, W) + b
        return tokens

    def _L0_attn_ref(x, qkv_weight, qkv_bias, proj_weight, proj_bias):
        import jax, jax.numpy as jnp
        import numpy as np
        ALPHA = 0.35

        def _round_ln_pow2(x):
            y = jnp.floor(jnp.log2(x))
            up = x - 2.0 ** y > 2.0 ** (y + 1.0) - x
            return 2.0 ** (y + up.astype(x.dtype))
        B, N, C = x.shape
        num_heads = 12
        head_dim = C // num_heads
        scale = head_dim ** (-0.5)
        global_max_x = jnp.abs(x).max(axis=(0, 1))
        max_weight = jnp.abs(qkv_weight).max(axis=0)
        channel_scale = _round_ln_pow2(global_max_x ** ALPHA / max_weight ** (1.0 - ALPHA))
        x_smoothed = x / channel_scale[None, None, :]
        weight_smoothed = qkv_weight * channel_scale[None, :]
        h = jnp.einsum('bnc,mc->bnm', x_smoothed, weight_smoothed) + qkv_bias
        qkv = h.reshape(B, N, 3, num_heads, head_dim).transpose(2, 0, 3, 1, 4)
        q, k, v = (qkv[0], qkv[1], qkv[2])
        attn = jnp.einsum('bhnd,bhmd->bhnm', q, k) * scale
        attn = jax.nn.softmax(attn, axis=-1)
        out = jnp.einsum('bhnm,bhmd->bhnd', attn, v)
        out = out.transpose(0, 2, 1, 3).reshape(B, N, C)
        out = jnp.einsum('bnc,mc->bnm', out, proj_weight) + proj_bias
        return out

    def _L0_ffn_ref(x, gate_w, gate_b, gate_center, w1, b1, w2, b2):
        import jax, jax.numpy as jnp
        import numpy as np
        B, N, C, H, E = (8, 256, 192, 768, 4)
        b, n, c = x.shape
        scores = jnp.einsum('bnc,ce->bne', x, gate_w) + gate_b
        p_experts = jax.nn.softmax(scores - gate_center, axis=-1)
        expert = jnp.argmax(p_experts, axis=-1).reshape(-1)
        xt = x.reshape(-1, c)
        h = jax.nn.gelu(jnp.einsum('tc,ech->eth', xt, w1) + b1[:, None, :], approximate=False)
        out_all = jnp.einsum('eth,ehc->etc', h, w2) + b2[:, None, :]
        out = jnp.take_along_axis(out_all, expert[None, :, None], axis=0)[0]
        return out.reshape(b, n, c)
    h = _L0_tok_ref(x, L0_tok_W, L0_tok_b)
    h = h + _L0_attn_ref(_layernorm(h, axis=-1), L0_attn_qkv_weight, L0_attn_qkv_bias, L0_attn_proj_weight, L0_attn_proj_bias)
    h = h + _L0_ffn_ref(_layernorm(h, axis=-1), L0_ffn_gate_w, L0_ffn_gate_b, L0_ffn_gate_center, L0_ffn_w1, L0_ffn_b1, L0_ffn_w2, L0_ffn_b2)
    return h

_drawn_inputs = setup_inputs


def setup_inputs(seed=0):
    import zlib

    import numpy as np

    out = dict(_drawn_inputs(seed))
    spreads = {'L0_ffn_gate_b': (0.0, 0.1), 'L0_ffn_gate_center': (0.0, 0.1)}
    factors = {'L0_tok_b': 4.771,
     'L0_attn_qkv_weight': 4.754,
     'L0_attn_qkv_bias': 4.452,
     'L0_attn_proj_weight': 4.19,
     'L0_ffn_b1': 3.875,
     'L0_ffn_b2': 2.794}
    for name, (base, spread) in spreads.items():
        noise = np.random.default_rng([zlib.crc32(name.encode()), seed]).standard_normal(out[name].shape)
        drawn = base * np.exp(spread * noise) if base else spread * noise
        out[name] = jnp.asarray(drawn.astype(out[name].dtype))
    for name, factor in factors.items():
        out[name] = (out[name] * factor).astype(out[name].dtype)
    return out
```

```python
from contextlib import ExitStack

import concourse.bass as bass
from concourse import mybir

F32 = mybir.dt.float32
BF16 = mybir.dt.bfloat16
I32 = mybir.dt.int32
ALU = mybir.AluOpType
ACT = mybir.ActivationFunctionType
AX = mybir.AxisListType

P = 128
IMAGES, CHANNELS, SIDE = 64, 3, 224
GRID = 14
PATCH = SIDE // GRID
TOK = GRID * GRID
ALL = IMAGES * TOK
D_IN = CHANNELS * PATCH * PATCH
C = 192
HEADS, HD = 12, 16
HID, EXPERTS = 768, 4
KIN = D_IN // P
KH = HID // P
EPS = 1e-5

NT = ALL // P
GT = 7
GROUP = GT * P
GROUPS = NT // GT
LAG = 3

HALF = TOK // 2
UNITS = 12
TLAG = 4
SPLIT_ROWS = 6 * HD
Q_PARTS = (0, 0, 0, 1, 1, 2)
K_PARTS = (0, 1, 2, 0, 1, 0)
SCALE = float(HD) ** -0.5
STACK = 16 * 24
PROB_SLOTS = 6
FIRST_SLOTS = 6
ROUNDS = (IMAGES - FIRST_SLOTS) // 4

ROW = C + 4
MEAN, VAR, RSTD, TOKEN = C, C + 1, C + 2, C + 3
REGION = ALL + P
SPARE = EXPERTS * REGION
TILES = (ALL + EXPERTS * (P - 1)) // P
TILES += TILES % 2


def settled(eng, passed):
    eng.sem_inc(passed, 1)


def at_least(eng, semaphore, value):
    if not isinstance(value, int) or value > 0:
        eng.wait_ge(semaphore, value)


def at_least(eng, semaphore, value):
    if not isinstance(value, int) or value > 0:
        eng.wait_ge(semaphore, value)


def vit_block(nc, a):
    with ExitStack() as ctx:
        def sb(stack, name, shape, dt=F32):
            return stack.enter_context(nc.sbuf_tensor(name, shape, dt))

        def ps(stack, name, shape, dt=F32):
            return stack.enter_context(nc.psum_tensor(name, shape, dt))

        def sem(name):
            return ctx.enter_context(nc.semaphore(name))

        h_dram = nc.dram_tensor("h_tokens", [ALL, C], F32, kind="Internal").ap()
        rows_dram = nc.dram_tensor("rows_by_expert", [SPARE + P, ROW], F32, kind="Internal").ap()

        ident = sb(ctx, "ident", [P, P])
        tile_expert = sb(ctx, "tile_expert", [P, TILES], I32)
        tile_row = sb(ctx, "tile_row", [P, TILES], I32)
        with ExitStack() as st:
            xT = sb(st, "xT", [P, 2, ALL])
            absmax = sb(st, "absmax", [P, GROUPS, 2])
            phase_a(nc, a, sb, ps, sem, xT, ident, absmax, h_dram)
            phase_b(nc, a, sb, ps, sem, xT, ident, absmax, h_dram, rows_dram, tile_expert, tile_row)
        phase_c(nc, a, sb, ps, sem, ident, rows_dram, tile_expert, tile_row)


def phase_a(nc, a, sb, ps, sem, xT, ident, absmax, h_dram):
    with ExitStack() as st:
        patches = sb(st, "patches", [P, 2, KIN, GROUP])
        wt = sb(st, "wt", [P, KIN, C])
        bias = sb(st, "bias_tok", [P, C])
        h = sb(st, "h_a", [P, 2, GT, C])
        stats = sb(st, "stats_a", [P, 4, 6])
        mv = sb(st, "mv_a", [P, 4, 2])
        rstd = sb(st, "rstd_a", [P, 4, 1])
        vare = sb(st, "vare_a", [P, 4, 1])
        expo = sb(st, "expo_a", [P, 1])
        x = sb(st, "x_a", [P, 4, 2 * P])
        p_h = [ps(st, f"p_h{i}", [P, C]) for i in range(2)]
        p_x = [ps(st, f"p_x{i}", [P, 2, P]) for i in range(2)]

        loaded_w = sem("a_loaded_w")
        loaded = [sem(f"a_loaded{i}") for i in range(2)]
        const0, const = sem("a_const0"), sem("a_const")
        embedded, h_done, stats_done, mv_done, rstd_done, x_done = (
            sem("a_" + n) for n in ("embedded", "h_done", "stats_done", "mv_done", "rstd_done", "x_done"))
        turned, xT_done, max_done = sem("a_turned"), sem("a_xT_done"), sem("a_max_done")
        stored = [sem(f"a_stored{i}") for i in range(2)]

        waited_dve, waited_pool, vare_done = sem("a_waited_dve"), sem("a_waited_pool"), sem("a_vare_done")
        block = st.enter_context(nc.Block())
        patches_in = a["patches"].rearrange("(k p) t -> p k t", p=P)
        h_out = h_dram.rearrange("(n p) c -> p n c", p=P)

        def over_pairs(eng, body):
            body(0, True)
            with eng.Fori(1, GROUPS // 2) as i:
                body(i, False)

        @block.sync
        def _(sp):
            sp.dma_start(bias[:], a["tok_b"].partition_broadcast(P)).then_inc(loaded_w, 16)
            sp.dma_start(wt[:], a["tok_w"].rearrange("(k p) c -> p k c", p=P)).then_inc(loaded_w, 16)

            def body(i, first):
                for g in range(2):
                    if not first:
                        sp.wait_ge(embedded, (2 * i + g - 1) * GT)
                    for part in range(2):
                        ks = slice(3 * part, 3 * part + 3)
                        sp.dma_start(patches[:, g, ks, :],
                                     patches_in[:, ks, bass.ds((2 * i + g) * GROUP, GROUP)]).then_inc(loaded[g], 16)
            over_pairs(sp, body)

        @block.gpsimd
        def _(pool):
            nc.gpsimd.memset(ident[:], 0.0).then_inc(const0, 1)
            pool.wait_ge(const0, 1)
            nc.gpsimd.affine_select(out=ident[:], in_=ident[:], compare_op=ALU.not_equal, fill=1.0,
                                    base=0, pattern=[[-1, P]], channel_multiplier=1).then_inc(const, 1)
            nc.gpsimd.memset(x[:, :, C:2 * P], 1.0).then_inc(const, 1)
            nc.gpsimd.memset(expo[:], -0.5).then_inc(const, 1)
            pool.wait_ge(const, 3)

            def body(i, first):
                for t in range(2 * GT):
                    pool.wait_ge(mv_done, 2 * GT * i + t + 1)
                    settled(pool, waited_pool)
                    nc.gpsimd.tensor_scalar(vare[:, t % 2], mv[:, t % 2, 1:2], EPS, None, ALU.add).then_inc(vare_done, 1)
                    pool.wait_ge(vare_done, 2 * GT * i + t + 1)
                    nc.gpsimd.tensor_tensor(rstd[:, t % 2], vare[:, t % 2], expo[:], ALU.pow).then_inc(rstd_done, 1)
                    if t % GT == GT - 1:
                        g = t // GT
                        pool.wait_ge(h_done, (2 * i + g + 1) * GT)
                        pool.dma_start(h_out[:, bass.ds((2 * i + g) * GT, GT), :], h[:, g]).then_inc(stored[g], 16)
            over_pairs(pool, body)
            for g in range(2):
                pool.wait_ge(stored[g], 16 * (GROUPS // 2))

        @block.tensor
        def _(pe):
            pe.wait_ge(loaded_w, 32)
            pe.wait_ge(const, 2)

            def turn(n, slot):
                pe.wait_ge(x_done, n + 1)
                for c in range(2):
                    last = nc.tensor.transpose(p_x[slot % 2][:, c, :], x[:, slot % 4, c * P:(c + 1) * P], ident[:])
                last.then_inc(turned, 1)

            def body(i, first):
                for t in range(2 * GT):
                    n = 2 * GT * i + t
                    if t % GT == 0:
                        pe.wait_ge(loaded[t // GT], 32 * (i + 1))
                    if not first or t >= 2:
                        pe.wait_ge(h_done, n - 1)
                    for k in range(KIN):
                        last = nc.tensor.matmul(p_h[t % 2][:], patches[:, t // GT, k, (t % GT) * P:(t % GT + 1) * P],
                                                wt[:, k, :], start=(k == 0), stop=(k == KIN - 1))
                    last.then_inc(embedded, 1)
                    if not first or t >= LAG:
                        if not first or t >= LAG + 2:
                            pe.wait_ge(xT_done, n - LAG - 1)
                        turn(n - LAG, (t - LAG) % 2)
            over_pairs(pe, body)
            for k in range(LAG):
                n = NT - LAG + k
                pe.wait_ge(xT_done, n - 1)
                turn(n, n % 2)

        @block.vector
        def _(dve):
            dve.wait_ge(loaded_w, 32)
            dve.wait_ge(const, 2)

            def aggregate(n, s):
                dve.wait_ge(stats_done, n + 1)
                settled(dve, waited_dve)
                nc.vector.bn_aggr(mv[:, s], stats[:, s]).then_inc(mv_done, 1)

            def normalise(n, s, t, free):
                dve.wait_ge(rstd_done, n + 1)
                if free:
                    dve.wait_ge(turned, n - 1)
                g, k = (t // GT) % 2, t % GT
                nc.vector.tensor_scalar(x[:, s, 0:C], h[:, g, k], mv[:, s, 0:1], rstd[:, s], ALU.subtract,
                                        ALU.mult).then_inc(x_done, 1)

            def largest(g):
                dve.wait_ge(xT_done, (g + 1) * GT)
                nc.vector.tensor_reduce(absmax[:, bass.ds(g, 1), :].rearrange("p g c -> p (g c)"),
                                        xT[:, :, bass.ds(g * GROUP, GROUP)], AX.X, ALU.max,
                                        apply_absolute_value=True).then_inc(max_done, 1)

            def body(i, first):
                for t in range(2 * GT):
                    n = 2 * GT * i + t
                    s = t % 2
                    dve.wait_ge(embedded, n + 1)
                    if not first and t % GT == 0:
                        dve.wait_ge(stored[t // GT], 16 * i)
                    nc.vector.tensor_tensor(h[:, t // GT, t % GT], p_h[t % 2][:], bias[:], ALU.add).then_inc(h_done, 1)
                    if not first or t >= 1:
                        aggregate(n - 1, 1 - s)
                    if not first or t >= 2:
                        normalise(n - 2, s, (t - 2) % (2 * GT), not first or t >= 4)
                    dve.wait_ge(h_done, n + 1)
                    nc.vector.bn_stats(stats[:, s], h[:, t // GT, t % GT]).then_inc(stats_done, 1)
                    if not first and t == 6:
                        largest(2 * i - 1)
                    if t == 13:
                        largest(2 * i)
            over_pairs(dve, body)
            s = (NT - 1) % 2
            aggregate(NT - 1, s)
            normalise(NT - 2, 1 - s, 2 * GT - 2, True)
            normalise(NT - 1, s, 2 * GT - 1, True)
            largest(GROUPS - 1)
            dve.wait_ge(max_done, GROUPS)

        @block.scalar
        def _(act):
            def take(n, slot):
                act.wait_ge(turned, n + 1)
                nc.scalar.copy(xT[:, :, bass.ds(n * P, P)], p_x[slot][:]).then_inc(xT_done, 1)

            def body(i, first):
                for t in range(2 * GT):
                    if not first or t >= LAG:
                        take(2 * GT * i + t - LAG, (t - LAG) % 2)
            over_pairs(act, body)
            for n in range(NT - LAG, NT):
                take(n, n % 2)
            act.wait_ge(xT_done, NT)


def phase_b(nc, a, sb, ps, sem, xT, ident, absmax, h_dram, rows_dram, tile_expert, tile_row):
    with ExitStack() as st:
        wqkv = sb(st, "wqkv", [P, 2, 3 * C])
        wproj = sb(st, "wproj", [P, 3, C])
        gate_w = sb(st, "gate_w", [P, 2, EXPERTS])
        gate_b = sb(st, "gate_b", [P, EXPERTS])
        gate_c = sb(st, "gate_c", [P, EXPERTS])
        identb = sb(st, "identb", [P, P], BF16)
        smooth = sb(st, "smooth", [P, 8, 2])
        xs = sb(st, "x_smoothed", [P, 2, 2, 2 * TOK])
        rest = sb(st, "rest", [P, 2 * TOK])
        part = sb(st, "part", [P, 3, 3, 2 * TOK], BF16)
        qs = sb(st, "q_stack", [P, 2, HEADS, 2 * TOK], BF16)
        ks = sb(st, "k_stack", [P, 2, HEADS, 2 * TOK], BF16)
        vs = sb(st, "values", [P, 4, 2, HEADS, 2 * HD])
        probs = sb(st, "probs", [P, PROB_SLOTS, 2 * TOK])
        mx = sb(st, "mx", [P, 2, 2, HEADS])
        negm = sb(st, "negm", [P, 2, 2, HEADS], BF16)
        negmT = sb(st, "negmT", [2 * HEADS, TOK], BF16)
        o_raw = sb(st, "o_raw", [P, 3, TOK])
        recip = sb(st, "recip", [P, 2, HEADS])
        recip_rows = sb(st, "recip_rows", [P, 2, HEADS, 2 * HD])
        o = sb(st, "o_norm", [P, 3, TOK])
        hb = sb(st, "h_b", [P, 4, 2, C])
        rows = sb(st, "rows_b", [P, 2, 2, ROW])
        stats = sb(st, "stats_b", [P, 2, 6])
        vare = sb(st, "vare_b", [P, 2])
        expo = sb(st, "expo_b", [P, 3, 2])
        z = sb(st, "z_b", [P, 2, 2 * P])
        zT = sb(st, "zT_b", [P, 2, TOK])
        before = sb(st, "before", [P, P])
        ones = sb(st, "ones", [P, P])
        sum_rows = sb(st, "sum_rows", [P, 4])
        prefer = sb(st, "prefer", [P, EXPERTS])
        region = sb(st, "region", [P, EXPERTS])
        lane = sb(st, "lane", [P, 1])
        count_i = sb(st, "count_i", [P, TILES], I32)
        token_i = sb(st, "token_i", [P, 2, 2], I32)
        padding = sb(st, "padding", [P, ROW])
        score = sb(st, "score", [P, 2, EXPERTS])
        best = sb(st, "best", [P, 2])
        liked = sb(st, "liked", [P, 2, EXPERTS])
        likedest = sb(st, "likedest", [P, 2])
        chosen = sb(st, "chosen", [P, 2, EXPERTS])
        place = sb(st, "place", [P, 2, EXPERTS])
        where_f = sb(st, "where_f", [P, 2])
        where_i = sb(st, "where_i", [P, 2, 2], I32)
        base = sb(st, "base", [P, EXPERTS])
        pad_i = sb(st, "pad_i", [P, EXPERTS], I32)
        table = sb(st, "table", [P, 4, TILES])
        few = sb(st, "few", [P, 5, EXPERTS])
        few_i = sb(st, "few_i", [P, 2, EXPERTS], I32)

        p_s = [ps(st, f"p_s{i}", [P, 512]) for i in range(2)]
        p_t = [ps(st, f"p_t{i}", [P, 512]) for i in range(2)]
        p_o = [ps(st, f"p_o{i}", [P, 512]) for i in range(2)]
        p_qkv = ps(st, "p_qkv", [P, 512])
        p_misc = ps(st, "p_misc", [P, 512])
        p_negmT = p_misc[0:2 * HEADS, 0:HALF].bitcast(BF16)
        p_zT = p_misc[:, 0:2 * TOK]
        p_gate, p_sums = p_misc[0:HALF, 400:400 + 2 * EXPERTS], p_misc[0:HALF, 416:416 + 2 * HEADS]
        p_recip = p_misc[:, 0:2 * TOK]
        p_proj, p_place = p_misc[0:HALF, 0:2 * C], p_misc[0:HALF, 400:400 + 2 * EXPERTS]
        p_total = p_misc[:, 400 + 2 * EXPERTS:400 + 3 * EXPERTS]
        p_recip2 = p_o[1][:, 256:256 + TOK]

        w_loaded, const, smoothed, x_smooth, step, powers = (
            sem("b_" + n) for n in ("w_loaded", "const", "smoothed", "x_smooth", "step", "powers"))
        h_loaded = [sem(f"b_h_loaded{i}") for i in range(4)]
        s_done, max_done, t_done, exp_done = (sem("b_" + n) for n in ("scores", "max", "scoresT", "exp"))
        pv_done, o_taken, sums_done, recip_done, recipT_done, norm_done = (
            sem("b_" + n) for n in ("pv", "o_taken", "sums", "recip", "recipT", "norm"))
        negm1_done, negm_done, negmT_done, negmT_taken, negm_placed = (
            sem("b_" + n) for n in ("negm1", "negm", "negmT", "negmT_taken", "negm_placed"))
        qk_done, first_done, rest_done, second_done, third_done = (
            sem("b_" + n) for n in ("qk", "part1", "rest", "part2", "part3"))
        v_done, v_taken, stacked = sem("b_v"), sem("b_v_taken"), sem("b_stacked")
        proj_done, h2_done, stats_done, mv_done, vare_done, rstd_done, z_done, zT_done, zT_taken = (
            sem("b_" + n) for n in ("proj", "h2", "stats", "mv", "vare", "rstd", "z", "zT", "zT_taken"))
        gate_done, chosen_done, ranked, placed, token_done, padded = (
            sem("b_" + n) for n in ("gate", "chosen", "ranked", "placed", "token", "padded"))
        scattered = [sem(f"b_scattered{i}") for i in range(2)]
        pad_ready, tables, waited_pool, waited_sp, waited_dve = (
            sem("b_" + n) for n in ("pad_ready", "tables", "waited_pool", "waited_sp", "waited_dve"))
        block = st.enter_context(nc.Block())

        FILLS = 19
        MAXIMA_STEPS = 3
        CHOOSE, PLACE = 6, 5
        HALVES = [slice(HALF * t, HALF * (t + 1)) for t in range(2)]

        def over_slots(eng, slot):
            for n in range(FIRST_SLOTS):
                slot(n, n, n // 2, n // 4)
            with eng.Fori(0, ROUNDS) as i:
                for k in range(FIRST_SLOTS, FIRST_SLOTS + 4):
                    slot(4 * i + k, k, 2 * i + k // 2, i + k // 4)
            for n in range(FIRST_SLOTS + 4 * ROUNDS, IMAGES + 3):
                slot(n, n, n // 2, n // 4)

        def live(k, behind):
            return 0 <= k - behind < IMAGES

        def makes_pair(k):
            return k % 2 == 0 and k + 2 < IMAGES

        def unit(u, turned):
            if not turned:
                return u // 6, 2 * (u % 6)
            return (u // 2) % 2, 4 * (u // 4) + 2 * (u % 2)

        @block.sync
        def _(sp):
            sp.dma_start(wqkv[:], a["qkv_w"].rearrange("(k p) c -> p k c", p=P)).then_inc(w_loaded, 16)
            sp.dma_start(wproj[:], a["proj_w"].rearrange("(k p) c -> p k c", p=P)).then_inc(w_loaded, 16)
            sp.dma_start(gate_w[:], a["gate_w"].rearrange("(k p) e -> p k e", p=P)).then_inc(w_loaded, 16)
            for dst, name in ((gate_b, "gate_b"), (gate_c, "gate_c")):
                sp.dma_start(dst[:], a[name].partition_broadcast(P)).then_inc(w_loaded, 16)

            def stack(p, b):
                sp.wait_ge(third_done, 3 * (p + 1))
                settled(sp, waited_sp)
                for r in range(6):
                    rws = slice(HD * r, HD * (r + 1))
                    for dst, parts, col, low in ((qs, Q_PARTS, 0, 0), (ks, K_PARTS, 1, 64)):
                        sp.dma_start(dst[rws, b, 0:8, :], part[:, parts[r], col, :]).then_inc(stacked, 16)
                        sp.dma_start(dst[rws, b, 8:12, :], part[low:low + 64, parts[r], 2, :]).then_inc(stacked, 16)

            def slot(n, k, pair, quad):
                if k == 0:
                    stack(0, 0)
                if k % 2 == 1 and k < IMAGES - 1:
                    if k >= 3:
                        sp.wait_ge(t_done, UNITS * (n - 1))
                        settled(sp, waited_sp)
                    sp.wait_ge(stacked, STACK * (pair + 1))
                    stack(pair + 1, (k // 2 + 1) % 2)
                if live(k, 0):
                    if k >= 4:
                        sp.wait_ge(h2_done, n - 3)
                    sp.dma_start(hb[0:HALF, k % 4], h_dram[bass.ds(n * TOK, TOK), :]
                                 .rearrange("(t p) c -> p t c", p=HALF)).then_inc(h_loaded[k % 4], 16)
            over_slots(sp, slot)

        @block.gpsimd
        def _(pool):
            filled = [0]

            def alone(ins):
                filled[0] += 1
                ins.then_inc(const, 1)
                pool.wait_ge(const, filled[0])

            alone(nc.gpsimd.tensor_copy(identb[:], ident[:]))
            alone(nc.gpsimd.memset(ks[96:98], 1.0))
            alone(nc.gpsimd.memset(vs[:], 0.0))
            alone(nc.gpsimd.memset(vs[0:HALF, :, :, :, HD:2 * HD], 1.0))
            alone(nc.gpsimd.memset(probs[96:128], 0.0))
            alone(nc.gpsimd.memset(z[:, :, C:2 * P], 1.0))
            for i, power in enumerate((-0.5, 0.35, -0.65)):
                alone(nc.gpsimd.memset(expo[:, i], power))
            alone(nc.gpsimd.memset(ones[:], 1.0))
            alone(nc.gpsimd.affine_select(out=before[:], in_=ones[:], compare_op=ALU.is_gt, fill=0.0,
                                          base=0, pattern=[[1, P]], channel_multiplier=-1))
            alone(nc.gpsimd.memset(sum_rows[:], 0.0))
            alone(nc.gpsimd.affine_select(out=sum_rows[:], in_=sum_rows[:], compare_op=ALU.not_equal, fill=1.0,
                                          base=-HD, pattern=[[-2 * HD, 4]], channel_multiplier=1))
            alone(nc.gpsimd.iota(count_i[:], pattern=[[1, TILES]], base=0, channel_multiplier=0))
            alone(nc.gpsimd.tensor_copy(table[:, 0], count_i[:]))
            alone(nc.gpsimd.iota(token_i[:], pattern=[[TOK, 2], [HALF, 2]], base=-2 * TOK, channel_multiplier=1))
            for b in range(2):
                alone(nc.gpsimd.tensor_copy(rows[:, b, :, TOKEN], token_i[:, b]))
            alone(nc.gpsimd.iota(token_i[:, 0, 0:1], pattern=[[0, 1]], base=0, channel_multiplier=1))
            assert filled[0] == FILLS

            pool.wait_ge(step, MAXIMA_STEPS)
            nc.gpsimd.tensor_tensor(smooth[:, 2, :], smooth[:, 0, :], expo[:, 1], ALU.pow).then_inc(powers, 1)
            nc.gpsimd.tensor_tensor(smooth[:, 3, :], smooth[:, 1, :], expo[:, 2], ALU.pow).then_inc(powers, 1)

            def split(p, u):
                j = 3 * p + u
                pool.wait_ge(rest_done, j + 1)
                settled(pool, waited_pool)
                nc.gpsimd.tensor_scalar(part[:, 1, u, :], rest[:], 1.0, None, ALU.mult).then_inc(second_done, 1)
                pool.wait_ge(second_done, j + 1)
                nc.gpsimd.tensor_tensor(part[:, 2, u, :], rest[:], part[:, 1, u, :],
                                        ALU.subtract).then_inc(third_done, 1)

            def deviation(m, b):
                pool.wait_ge(mv_done, 2 * m + 2)
                settled(pool, waited_pool)
                nc.gpsimd.tensor_scalar(vare[0:HALF], rows[0:HALF, b, :, VAR], EPS, None, ALU.add)\
                    .then_inc(vare_done, 1)
                pool.wait_ge(vare_done, m + 1)
                nc.gpsimd.tensor_tensor(rows[0:HALF, b, :, RSTD], vare[0:HALF], expo[0:HALF, 0], ALU.pow)\
                    .then_inc(rstd_done, 1)
                nc.gpsimd.tensor_scalar(rows[0:HALF, b, :, TOKEN], rows[0:HALF, b, :, TOKEN], 2.0 * TOK, None,
                                        ALU.add).then_inc(token_done, 1)

            def scatter(m, b):
                pool.wait_ge(placed, PLACE * m + PLACE - 1)
                pool.wait_ge(rstd_done, m + 1)
                pool.wait_ge(token_done, m + 1)
                settled(pool, waited_pool)
                for t in range(2):
                    nc.gpsimd.indirect_dma_start(
                        out=rows_dram, out_offset=bass.IndirectOffsetOnAxis(ap=where_i[0:HALF, b, t:t + 1], axis=0),
                        in_=rows[0:HALF, b, t, :], in_offset=None).then_inc(scattered[b], 16)

            for u in range(3):
                split(0, u)

            def slot(n, k, pair, quad):
                if live(k, 3):
                    deviation(n - 3, (k - 3) % 2)
                if makes_pair(k):
                    for u in range(3):
                        split(pair + 1, u)
                if live(k, 3):
                    scatter(n - 3, (k - 3) % 2)
            over_slots(pool, slot)

            pool.wait_ge(pad_ready, 2)
            for e in range(EXPERTS):
                nc.gpsimd.indirect_dma_start(
                    out=rows_dram, out_offset=bass.IndirectOffsetOnAxis(ap=pad_i[:, e:e + 1], axis=0),
                    in_=padding[:], in_offset=None).then_inc(padded, 16)
            pool.dma_start(rows_dram[SPARE:SPARE + P, :], padding[:]).then_inc(padded, 16)
            for b in range(2):
                pool.wait_ge(scattered[b], 32 * IMAGES // 2)
            pool.wait_ge(padded, 16 * (EXPERTS + 1))

        @block.vector
        def _(dve):
            dve.wait_ge(w_loaded, 80)
            dve.wait_ge(const, FILLS)
            n_steps = [0]

            def then(ins):
                n_steps[0] += 1
                ins.then_inc(step, 1)
                dve.wait_ge(step, n_steps[0])

            gx, mw, gp, wp, r, pw, cs, inv = (smooth[:, i, :] for i in range(8))
            then(nc.vector.tensor_reduce(gx, absmax[:].rearrange("p g c -> p c g"), AX.X, ALU.max))
            then(nc.vector.tensor_reduce(mw, wqkv[:], AX.X, ALU.max, apply_absolute_value=True))
            then(nc.vector.memset(smooth[C - P:P, 0:2, 1:2], 1.0))
            assert n_steps[0] == MAXIMA_STEPS
            dve.wait_ge(powers, 2)
            then(nc.vector.tensor_tensor(r, gp, wp, ALU.mult))
            then(nc.vector.tensor_scalar(pw.bitcast(I32), r.bitcast(I32), 0x7F800000, None, ALU.bitwise_and))
            then(nc.vector.scalar_tensor_tensor(out=cs, in0=pw, scalar=1.5, in1=r, op0=ALU.mult, op1=ALU.is_lt))
            then(nc.vector.scalar_tensor_tensor(out=cs, in0=cs, scalar=1.0, in1=pw, op0=ALU.add, op1=ALU.mult))
            then(nc.vector.reciprocal(inv, cs))
            for c in range(2):
                nc.vector.tensor_scalar(wqkv[:, c], wqkv[:, c], cs[:, c:c + 1], None, ALU.mult).then_inc(smoothed, 1)
            then(nc.vector.tensor_tensor(gate_b[:], gate_b[:], gate_c[:], ALU.subtract))
            for e in range(EXPERTS):
                then(nc.vector.memset(prefer[:, e:e + 1], float(EXPERTS - e)))
                then(nc.vector.memset(region[:, e:e + 1], float(e * REGION)))
            then(nc.vector.tensor_copy(base[:], region[:]))
            then(nc.vector.tensor_copy(lane[:], token_i[:, 0, 0:1]))

            def smooth_x(p, b):
                at_least(dve, v_done, 2 * p - 2)
                for c in range(2):
                    nc.vector.tensor_scalar(xs[:, b, c], xT[:, c, bass.ds(2 * TOK * p, 2 * TOK)], inv[:, c:c + 1],
                                            None, ALU.mult).then_inc(x_smooth, 1)

            def leave(p, u):
                j = 3 * p + u
                dve.wait_ge(first_done, j + 1)
                at_least(dve, third_done, j)
                nc.vector.tensor_tensor(rest[:], p_qkv[:, 0:2 * TOK], part[:, 0, u, :],
                                        ALU.subtract).then_inc(rest_done, 1)

            smooth_x(0, 0)
            for u in range(3):
                leave(0, u)

            def biggest(n, k, u):
                half, head = unit(u, False)
                dve.wait_ge(s_done, UNITS * n + u + 1)
                nc.vector.tensor_reduce(mx[0:HALF, k % 2, half, head:head + 2],
                                        p_s[u % 2][0:HALF, 0:2 * TOK].rearrange("p (h t) -> p h t", h=2),
                                        AX.X, ALU.max).then_inc(max_done, 1)

            def negate(n, b):
                dve.wait_ge(max_done, UNITS * (n + 1))
                at_least(dve, negmT_done, n)
                nc.vector.tensor_scalar(negm[0:HALF, :, 0, :], mx[0:HALF, b], -1.0, None, ALU.mult).then_inc(negm1_done, 1)
                dve.wait_ge(negm1_done, n + 1)
                nc.vector.scalar_tensor_tensor(out=negm[0:HALF, :, 1, :], in0=mx[0:HALF, b], scalar=-1.0,
                                               in1=negm[0:HALF, :, 0, :], op0=ALU.mult, op1=ALU.subtract)\
                    .then_inc(negm_done, 1)

            def invert(m):
                dve.wait_ge(sums_done, m + 1)
                nc.vector.reciprocal(recip[0:HALF], p_sums.rearrange("p (t h) -> p t h", t=2)).then_inc(recip_done, 1)
                dve.wait_ge(recip_done, 2 * m + 1)
                at_least(dve, recipT_done, m)
                nc.vector.tensor_copy(recip_rows[0:HALF], recip[0:HALF].rearrange("p t (h o) -> p t h o", o=1)
                                      .broadcast_to([HALF, 2, HEADS, 2 * HD])).then_inc(recip_done, 1)

            def multiply(m):
                dve.wait_ge(recipT_done, m + 1)
                at_least(dve, proj_done, m)
                nc.vector.tensor_tensor(o[:, 0:2].rearrange("p g t -> p (g t)"), p_recip,
                                        o_raw[:, 0:2].rearrange("p g t -> p (g t)"), ALU.mult).then_inc(norm_done, 1)
                nc.vector.tensor_tensor(o[:, 2], p_recip2, o_raw[:, 2], ALU.mult).then_inc(norm_done, 1)

            def residual(m, b, earlier, hbuf, loads):
                dve.wait_ge(proj_done, m + 1)
                dve.wait_ge(h_loaded[hbuf], loads)
                at_least(dve, scattered[b], 32 * earlier)
                nc.vector.tensor_tensor(rows[0:HALF, b, :, 0:C], p_proj
                                        .rearrange("p (t c) -> p t c", t=2), hb[0:HALF, hbuf], ALU.add).then_inc(h2_done, 1)
                dve.wait_ge(h2_done, m + 1)
                for t in range(2):
                    nc.vector.bn_stats(stats[0:HALF, t], rows[0:HALF, b, t, 0:C]).then_inc(stats_done, 1)
                dve.wait_ge(stats_done, 2 * m + 2)
                settled(dve, waited_dve)
                for t in range(2):
                    nc.vector.bn_aggr(rows[0:HALF, b, t, MEAN:VAR + 1], stats[0:HALF, t]).then_inc(mv_done, 1)

            def normalise(m, b):
                dve.wait_ge(rstd_done, m + 1)
                at_least(dve, zT_done, m)
                for t in range(2):
                    nc.vector.tensor_scalar(z[0:HALF, t, 0:C], rows[0:HALF, b, t, 0:C],
                                            rows[0:HALF, b, t, MEAN:MEAN + 1], rows[0:HALF, b, t, RSTD:RSTD + 1],
                                            ALU.subtract, ALU.mult).then_inc(z_done, 1)

            def over_halves(t, n):
                return t.rearrange("p (o e) -> p o e", o=1).broadcast_to([n, 2, EXPERTS])

            def over_experts(t):
                return t.rearrange("p (t o) -> p t o", o=1).broadcast_to([HALF, 2, EXPERTS])

            def choose(m, k):
                H = slice(0, HALF)
                made = [CHOOSE * m]

                def link(ins):
                    made[0] = made[0] + 1
                    ins.then_inc(chosen_done, 1)
                    return made[0]

                dve.wait_ge(gate_done, m + 1)
                if live(k, 2):
                    dve.wait_ge(sums_done, m + 2)
                dve.wait_ge(chosen_done, link(nc.vector.tensor_tensor(
                    score[H], p_gate.rearrange("p (t e) -> p t e", t=2), over_halves(gate_b[H], HALF), ALU.add)))
                dve.wait_ge(chosen_done, link(nc.vector.tensor_reduce(best[H], score[H], AX.X, ALU.max)))
                dve.wait_ge(chosen_done, link(nc.vector.tensor_tensor(liked[H], score[H], over_experts(best[H]), ALU.is_ge)))
                dve.wait_ge(chosen_done, link(nc.vector.tensor_tensor(liked[H], liked[H], over_halves(prefer[H], HALF), ALU.mult)))
                dve.wait_ge(chosen_done, link(nc.vector.tensor_reduce(likedest[H], liked[H], AX.X, ALU.max)))
                at_least(dve, ranked, m)
                link(nc.vector.tensor_tensor(chosen[H], liked[H], over_experts(likedest[H]), ALU.is_equal))

            def put(m, b):
                H = slice(0, HALF)
                made = [PLACE * m]

                def link(ins):
                    made[0] = made[0] + 1
                    ins.then_inc(placed, 1)
                    return made[0]

                dve.wait_ge(ranked, m + 1)
                dve.wait_ge(placed, link(nc.vector.tensor_tensor(
                    place[H], p_place.rearrange("p (t e) -> p t e", t=2), over_halves(base[H], HALF), ALU.add)))
                dve.wait_ge(placed, link(nc.vector.tensor_tensor(place[H], place[H], chosen[H], ALU.mult)))
                dve.wait_ge(placed, link(nc.vector.tensor_reduce(where_f[H], place[H], AX.X, ALU.add)))
                link(nc.vector.tensor_copy(where_i[H, b], where_f[H]))
                link(nc.vector.tensor_tensor(base[:], p_total, base[:], ALU.add))

            def slot(n, k, pair, quad):
                for u in range(UNITS):
                    if makes_pair(k) and u == 0:
                        smooth_x(pair + 1, (k // 2 + 1) % 2)
                    if live(k, 0):
                        biggest(n, k, u)
                    if live(k, 3):
                        m, b = n - 3, (k - 3) % 2
                        if u == 0:
                            residual(m, b, pair + (k - 3) // 2 - k // 2, (k - 3) % 4,
                                     16 * (quad + (k - 3) // 4 - k // 4 + 1))
                        if u == 2:
                            normalise(m, b)
                        if u == 7:
                            choose(m, k)
                        if u == 11:
                            put(m, b)
                    if makes_pair(k) and u in (2, 5, 8):
                        leave(pair + 1, (u - 2) // 3)
                    if live(k, 2):
                        if u == 7:
                            invert(n - 2)
                        if u == 9:
                            multiply(n - 2)
                if live(k, 0):
                    negate(n, k % 2)
            over_slots(dve, slot)

            dve.wait_ge(placed, PLACE * IMAGES)
            then(nc.vector.memset(padding[:, 0:TOKEN], 0.0))
            nc.vector.tensor_scalar(padding[:, TOKEN:ROW], lane[:], float(ALL), None, ALU.add).then_inc(pad_ready, 1)
            nc.vector.tensor_scalar(pad_i[:], base[:], lane[:], None, ALU.add).then_inc(pad_ready, 1)
            tiles_f, ends, gaps = few[:, 0], few[:, 1], few[:, 2]
            then(nc.vector.tensor_tensor(few[:, 3], base[:], region[:], ALU.subtract))
            then(nc.vector.tensor_scalar(few_i[:, 0], few[:, 3], float(P - 1), None, ALU.add))
            then(nc.vector.tensor_scalar(few_i[:, 1], few_i[:, 0], 7, None, ALU.arith_shift_right))
            then(nc.vector.tensor_copy(tiles_f, few_i[:, 1]))
            then(nc.vector.tensor_copy(ends[:, 0:1], tiles_f[:, 0:1]))
            for e in range(1, EXPERTS):
                then(nc.vector.tensor_tensor(ends[:, e:e + 1], ends[:, e - 1:e], tiles_f[:, e:e + 1], ALU.add))
            then(nc.vector.tensor_scalar(gaps, tiles_f, -float(P), float(REGION), ALU.mult, ALU.add))
            number, expert, row, past = (table[:, i] for i in range(4))
            then(nc.vector.tensor_scalar(row, number, float(P), None, ALU.mult))
            then(nc.vector.memset(expert, 0.0))
            for e in range(EXPERTS - 1):
                then(nc.vector.tensor_scalar(past, number, ends[:, e:e + 1], None, ALU.is_ge))
                then(nc.vector.tensor_tensor(expert, expert, past, ALU.add))
                then(nc.vector.scalar_tensor_tensor(out=row, in0=past, scalar=gaps[:, e:e + 1], in1=row,
                                                    op0=ALU.mult, op1=ALU.add))
            then(nc.vector.tensor_scalar(past, number, ends[:, 3:4], None, ALU.is_lt))
            then(nc.vector.scalar_tensor_tensor(out=row, in0=row, scalar=-float(SPARE), in1=past,
                                                op0=ALU.add, op1=ALU.mult))
            nc.vector.tensor_scalar(tile_row[:], row, float(SPARE), None, ALU.add).then_inc(tables, 1)
            nc.vector.tensor_copy(tile_expert[:], expert).then_inc(tables, 1)
            dve.wait_ge(tables, 2)

        @block.scalar
        def _(act):
            def first_part(p, u):
                act.wait_ge(qk_done, 3 * p + u + 1)
                if u == 0:
                    at_least(act, stacked, STACK * p)
                nc.scalar.copy(part[:, 0, u, :], p_qkv[:, 0:2 * TOK]).then_inc(first_done, 1)

            for u in range(3):
                first_part(0, u)

            def exps(n, v):
                act.wait_ge(t_done, UNITS * n + v + 1)
                nc.scalar.activation(probs[0:HALF, v % PROB_SLOTS, :], p_t[v % 2][0:HALF, 0:2 * TOK], ACT.Exp,
                                     scale=SCALE).then_inc(exp_done, 1)

            def lay_max(m, k):
                act.wait_ge(negmT_done, m + 1)
                at_least(act, negm_placed, 16 * m)
                nc.scalar.copy(negmT[:], p_negmT).then_inc(negmT_taken, 1)
                act.wait_ge(negmT_taken, m + 1)
                col = TOK * (k % 2)
                act.dma_start(qs[96:98, (k // 2) % 2, :, col:col + TOK], negmT[:]).then_inc(negm_placed, 16)

            def take_outputs(m, bank):
                act.wait_ge(pv_done, 6 * m + 4 + 2 * bank)
                at_least(act, norm_done, 2 * m)
                if bank == 0:
                    nc.scalar.copy(o_raw[:, 0:2].rearrange("p g t -> p (g t)"), p_o[0][:, 0:2 * TOK]).then_inc(o_taken, 1)
                else:
                    nc.scalar.copy(o_raw[:, 2], p_o[1][:, 0:TOK]).then_inc(o_taken, 1)

            def slot(n, k, pair, quad):
                for u in range(UNITS):
                    if u < TLAG and live(k, 2):
                        exps(n - 2, u - TLAG + UNITS)
                    if u >= TLAG and live(k, 1):
                        exps(n - 1, u - TLAG)
                    if u == 1 and live(k, 1):
                        lay_max(n - 1, k - 1)
                    if makes_pair(k) and u in (2, 5, 8):
                        first_part(pair + 1, (u - 2) // 3)
                    if live(k, 2) and u in (3, 5):
                        take_outputs(n - 2, u // 5)
                    if live(k, 3) and u == 4:
                        act.wait_ge(zT_done, n - 2)
                        at_least(act, gate_done, n - 3)
                        nc.scalar.copy(zT[:], p_zT.rearrange("p (c t) -> p c t", c=2)).then_inc(zT_taken, 1)
                    if live(k, 0) and u == 11:
                        act.wait_ge(v_done, n + 1)
                        nc.scalar.copy(vs[0:HALF, k % 4, :, :, 0:HD],
                                       p_qkv[0:HALF, 0:2 * C].rearrange("p (t h d) -> p t h d", t=2, d=HD))\
                            .then_inc(v_taken, 1)
            over_slots(act, slot)

        @block.tensor
        def _(pe):
            pe.wait_ge(smoothed, 2)
            pe.wait_ge(const, FILLS)

            def queries_keys(p, b, u):
                pe.wait_ge(x_smooth, 2 * p + 2)
                at_least(pe, rest_done, 3 * p + u)
                if u == 0:
                    at_least(pe, v_taken, 2 * p - 2)
                for c in range(2):
                    last = nc.tensor.matmul(p_qkv[:, 0:2 * TOK], wqkv[:, c, P * u:P * (u + 1)],
                                            xs[:, b, c], start=(c == 0), stop=(c == 1))
                last.then_inc(qk_done, 1)

            def values(n, k, pair):
                if makes_pair(k):
                    pe.wait_ge(rest_done, 3 * pair + 6)
                else:
                    pe.wait_ge(v_taken, n)
                at = TOK * (k % 2)
                for t in range(2):
                    for c in range(2):
                        last = nc.tensor.matmul(p_qkv[0:HALF, C * t:C * (t + 1)],
                                                xs[:, (k // 2) % 2, c, at + HALF * t:at + HALF * (t + 1)],
                                                wqkv[:, c, 2 * C:3 * C], start=(c == 0), stop=(c == 1))
                last.then_inc(v_done, 1)

            def scores(n, k, u, pair):
                half, head = unit(u, False)
                b, at = (k // 2) % 2, TOK * (k % 2)
                if u == 0 and k % 2 == 0:
                    pe.wait_ge(stacked, STACK * (pair + 1))
                at_least(pe, max_done, UNITS * n + u - 1)
                for i in range(2):
                    last = nc.tensor.matmul(p_s[u % 2][0:HALF, TOK * i:TOK * (i + 1)],
                                            qs[0:SPLIT_ROWS, b, head + i, at + HALF * half:at + HALF * (half + 1)],
                                            ks[0:SPLIT_ROWS, b, head + i, at:at + TOK], start=True, stop=True)
                last.then_inc(s_done, 1)

            def scores_turned(n, k, v):
                half, head = unit(v, True)
                b, at = (k // 2) % 2, TOK * (k % 2)
                if v == 0:
                    pe.wait_ge(negm_placed, 16 * (n + 1))
                at_least(pe, exp_done, UNITS * n + v - 1)
                for i in range(2):
                    last = nc.tensor.matmul(p_t[v % 2][0:HALF, TOK * i:TOK * (i + 1)],
                                            ks[0:SPLIT_ROWS + 2, b, head + i, at + HALF * half:at + HALF * (half + 1)],
                                            qs[0:SPLIT_ROWS + 2, b, head + i, at:at + TOK], start=True, stop=True)
                last.then_inc(t_done, 1)

            def outputs(m, k, s):
                g, half = s // 2, s % 2
                pe.wait_ge(exp_done, UNITS * m + 2 * s + 2)
                if s == 0:
                    pe.wait_ge(v_taken, m + 1)
                    at_least(pe, o_taken, 2 * m - 1)
                if s == 4:
                    at_least(pe, norm_done, 2 * m)
                for j in range(4):
                    last = nc.tensor.matmul(p_o[g // 2][32 * j:32 * j + 32, TOK * (g % 2):TOK * (g % 2 + 1)],
                                            vs[:, k % 4, half, 4 * g + j, :],
                                            probs[:, (2 * s + j // 2) % PROB_SLOTS, TOK * (j % 2):TOK * (j % 2 + 1)],
                                            start=(half == 0), stop=(half == 1), skip_group_check=True)
                last.then_inc(pv_done, 1)

            def free_misc(n, k):
                if live(k, 3):
                    pe.wait_ge(h2_done, n - 2)
                if live(k, 4):
                    pe.wait_ge(placed, PLACE * (n - 3))

            def turn_max(m):
                pe.wait_ge(negm_done, m + 1)
                at_least(pe, negmT_taken, m)
                for t in range(2):
                    last = nc.tensor.transpose(p_negmT[:, HALVES[t]],
                                               negm[0:HALF, t].rearrange("p a h -> p (a h)"), identb[0:HALF, 0:HALF])
                last.then_inc(negmT_done, 1)

            def add_sums(m):
                pe.wait_ge(o_taken, 2 * m + 2)
                at_least(pe, recip_done, 2 * m)
                for t in range(2):
                    for g in range(3):
                        last = nc.tensor.matmul(p_sums[:, HEADS * t + 4 * g:HEADS * t + 4 * g + 4],
                                                o_raw[:, g, HALVES[t]], sum_rows[:], start=True, stop=True)
                last.then_inc(sums_done, 1)

            def turn_recip(m):
                pe.wait_ge(recip_done, 2 * m + 2)
                at_least(pe, chosen_done, CHOOSE * m)
                for g in range(3):
                    for t in range(2):
                        out = p_recip[:, TOK * g + HALF * t:TOK * g + HALF * (t + 1)] if g < 2 else p_recip2[:, HALVES[t]]
                        last = nc.tensor.transpose(out, recip_rows[0:HALF, t, 4 * g:4 * g + 4, :]
                                                   .rearrange("p h o -> p (h o)"), ident[0:HALF, 0:HALF])
                last.then_inc(recipT_done, 1)

            def project(m):
                pe.wait_ge(norm_done, 2 * m + 2)
                for t in range(2):
                    for g in range(3):
                        last = nc.tensor.matmul(p_proj[:, C * t:C * (t + 1)], o[:, g, HALVES[t]],
                                                wproj[:, g, :], start=(g == 0), stop=(g == 2))
                last.then_inc(proj_done, 1)

            def turn_z(m, k):
                pe.wait_ge(z_done, 2 * m + 2)
                if live(k, 1):
                    pe.wait_ge(negmT_taken, m + 3)
                for t in range(2):
                    for c in range(2):
                        last = nc.tensor.transpose(p_zT[:, TOK * c + HALF * t:TOK * c + HALF * (t + 1)],
                                                   z[0:HALF, t, P * c:P * (c + 1)], ident[0:HALF, 0:HALF])
                last.then_inc(zT_done, 1)

            def gate(m):
                pe.wait_ge(zT_taken, m + 1)
                for t in range(2):
                    for c in range(2):
                        last = nc.tensor.matmul(p_gate[:, EXPERTS * t:EXPERTS * (t + 1)], zT[:, c, HALVES[t]],
                                                gate_w[:, c, :], start=(c == 0), stop=(c == 1))
                last.then_inc(gate_done, 1)

            def rank(m):
                pe.wait_ge(chosen_done, CHOOSE * (m + 1))
                at_least(pe, placed, PLACE * m)
                H = slice(0, HALF)
                nc.tensor.matmul(p_place[:, 0:EXPERTS], before[H, H], chosen[H, 0], start=True, stop=True)
                nc.tensor.matmul(p_place[:, EXPERTS:2 * EXPERTS], before[H, H], chosen[H, 1], start=True, stop=False)
                nc.tensor.matmul(p_place[:, EXPERTS:2 * EXPERTS], ones[H, H], chosen[H, 0], start=False, stop=True)
                nc.tensor.matmul(p_total, ones[H, :], chosen[H, 0], start=True, stop=False)
                nc.tensor.matmul(p_total, ones[H, :], chosen[H, 1], start=False, stop=True).then_inc(ranked, 1)

            for u in range(3):
                queries_keys(0, 0, u)

            def slot(n, k, pair, quad):
                for u in range(UNITS):
                    if live(k, 0):
                        scores(n, k, u, pair)
                    if u < TLAG and live(k, 2):
                        scores_turned(n - 2, k - 2, u - TLAG + UNITS)
                    if u >= TLAG and live(k, 1):
                        scores_turned(n - 1, k - 1, u - TLAG)
                    if u % 2 == 1:
                        s = (u - TLAG - 3) // 2
                        if s >= 0 and live(k, 1):
                            outputs(n - 1, k - 1, s)
                        if s < 0 and live(k, 2):
                            outputs(n - 2, k - 2, s + 6)
                    if u == 1:
                        free_misc(n, k)
                        if live(k, 1):
                            turn_max(n - 1)
                    if makes_pair(k) and u in (1, 4, 7):
                        queries_keys(pair + 1, (k // 2 + 1) % 2, (u - 1) // 3)
                    if live(k, 3) and u == 3:
                        turn_z(n - 3, k)
                    if live(k, 3) and u == 6:
                        gate(n - 3)
                    if live(k, 2) and u == 6:
                        add_sums(n - 2)
                    if live(k, 2) and u == 8:
                        turn_recip(n - 2)
                    if live(k, 0) and u == 10:
                        values(n, k, pair)
                    if live(k, 2) and u == 10:
                        project(n - 2)
                    if live(k, 3) and u == 10:
                        rank(n - 3)
            over_slots(pe, slot)


def phase_c(nc, a, sb, ps, sem, ident, rows_dram, tile_expert, tile_row):
    with ExitStack() as st:
        w1 = sb(st, "w1", [P, EXPERTS, 2, HID])
        w2 = sb(st, "w2", [P, EXPERTS, KH, C])
        b2 = sb(st, "b2", [P, EXPERTS, C])
        rows = sb(st, "rows_c", [P, 4, ROW])
        z = sb(st, "z_c", [P, 2, 2 * P])
        zT = sb(st, "zT_c", [P, 2, 2, P])
        hid = sb(st, "hid", [P, 2, HID])
        hidT = sb(st, "hidT", [P, 2, KH, P])
        y = sb(st, "y", [P, 2, C])
        result = sb(st, "result", [P, 2, C])
        token = sb(st, "token", [P, 4, 1], I32)
        p_z = ps(st, "p_z", [P, 2, P])
        p_h = [ps(st, f"p_hid{i}", [P, 512]) for i in range(2)]
        p_hT = [ps(st, f"p_hidT{i}", [P, 512]) for i in range(2)]
        p_y = [ps(st, f"p_y{i}", [P, 512]) for i in range(2)]
        HH = HID // 2

        w_loaded, ones_done = sem("c_w_loaded"), sem("c_ones")
        loaded = [sem(f"c_rows{i}") for i in range(4)]
        z_done, zT_done, zT_taken, h_done, gelu_done, hT_done, hT_taken = (
            sem("c_" + n) for n in ("z", "zT", "zT_taken", "hid", "gelu", "hidT", "hidT_taken"))
        y_done, biased, token_done, result_done = (sem("c_" + n) for n in ("y", "biased", "token", "result"))
        stored = [sem(f"c_stored{i}") for i in range(2)]
        waited_dve = sem("c_waited_dve")
        waited_pool = sem("c_waited_pool")
        block = st.enter_context(nc.Block())

        def over_steps(eng, step):
            for t in range(4):
                step(t, t, t // 2, 0)
            with eng.Fori(1, TILES // 4) as i:
                for k in range(4, 8):
                    step(4 * i + k - 4, k, 2 * i + k // 2 - 2, i)
            for t in range(TILES // 4 * 4, TILES + 2):
                step(t, t, t // 2, t // 4)

        def live(k, behind):
            return 0 <= k - behind < TILES

        @block.sync
        def _(sp):
            for e in range(EXPERTS):
                sp.dma_start(w1[:, e], a["w1"][e].rearrange("(k p) h -> p k h", p=P)).then_inc(w_loaded, 16)
                sp.dma_start(w2[:, e], a["w2"][e].rearrange("(k p) c -> p k c", p=P)).then_inc(w_loaded, 16)
            sp.dma_start(b2[:].rearrange("p e c -> p (e c)"), a["b2"].partition_broadcast(P)).then_inc(w_loaded, 16)

            def step(t, k, half, rnd):
                if live(k, 0):
                    if k >= 4:
                        sp.wait_ge(result_done, t - 3)
                    first = sp.value_load(tile_row[0:1, bass.ds(t, 1)], min_val=0, max_val=SPARE)
                    sp.dma_start(rows[:, k % 4, :], rows_dram[bass.ds(first, P), :]).then_inc(loaded[k % 4], 16)
            over_steps(sp, step)

        @block.gpsimd
        def _(pool):
            nc.gpsimd.memset(z[:, :, C:2 * P], 1.0).then_inc(ones_done, 1)

            def step(t, k, half, rnd):
                if live(k, 2):
                    pool.wait_ge(result_done, t - 1)
                    pool.wait_ge(token_done, t - 1)
                    settled(pool, waited_pool)
                    nc.gpsimd.indirect_dma_start(
                        out=a["out"], out_offset=bass.IndirectOffsetOnAxis(ap=token[:, (k - 2) % 4, :], axis=0),
                        in_=result[:, k % 2, :], in_offset=None, bounds_check=ALL - 1, oob_is_err=False)\
                        .then_inc(stored[k % 2], 16)
            over_steps(pool, step)
            for b in range(2):
                pool.wait_ge(stored[b], 16 * TILES // 2)

        @block.vector
        def _(dve):
            dve.wait_ge(w_loaded, 16 * (2 * EXPERTS + 1))
            dve.wait_ge(ones_done, 1)

            def normalise(t, k, half, rnd):
                b4 = k % 4
                dve.wait_ge(loaded[b4], 16 * (rnd + 1))
                at_least(dve, zT_done, t - 1)
                row = rows[:, b4, :]
                nc.vector.tensor_scalar(z[:, k % 2, 0:C], row[:, 0:C], row[:, MEAN:MEAN + 1], row[:, RSTD:RSTD + 1],
                                        ALU.subtract, ALU.mult).then_inc(z_done, 1)
                at_least(dve, stored[k % 2], 16 * (half - 1))
                nc.vector.tensor_copy(token[:, b4, :], row[:, TOKEN:ROW]).then_inc(token_done, 1)

            def take_turned(t, b, part):
                dve.wait_ge(hT_done, 2 * t + part + 1)
                at_least(dve, y_done, t - 1)
                nc.vector.tensor_copy(hidT[:, b, 3 * part:3 * part + 3, :].rearrange("p k t -> p (k t)"),
                                      p_hT[part][:, 0:HH]).then_inc(hT_taken, 1)

            def finish(t, k, half):
                dve.wait_ge(y_done, t + 1)
                expert = dve.value_load(tile_expert[0:1, bass.ds(t, 1)], min_val=0, max_val=EXPERTS - 1)
                nc.vector.tensor_tensor(y[:, k % 2], p_y[k % 2][:, 0:C], b2[:, bass.ds(expert, 1), :]
                                        .rearrange("p e c -> p (e c)"), ALU.add).then_inc(biased, 1)
                dve.wait_ge(biased, t + 1)
                at_least(dve, stored[k % 2], 16 * half)
                nc.vector.tensor_tensor(result[:, k % 2], y[:, k % 2], rows[:, k % 4, 0:C], ALU.add).then_inc(result_done, 1)

            def step(t, k, half, rnd):
                if k == 0:
                    normalise(t, k, half, rnd)
                if live(k, -1):
                    normalise(t + 1, k + 1, half + (k + 1) // 2 - k // 2, rnd + (k + 1) // 4 - k // 4)
                if live(k, 1):
                    for part in range(2):
                        take_turned(t - 1, (k - 1) % 2, part)
                if live(k, 2):
                    finish(t - 2, k - 2, half - 1)
            over_steps(dve, step)

        @block.scalar
        def _(act):
            def take_z(t, b):
                act.wait_ge(zT_done, t + 1)
                at_least(act, h_done, 2 * t - 2)
                nc.scalar.copy(zT[:, b], p_z[:]).then_inc(zT_taken, 1)

            def step(t, k, half, rnd):
                if k == 0:
                    take_z(t, 0)
                if live(k, 0):
                    for part in range(2):
                        act.wait_ge(h_done, 2 * t + part + 1)
                        at_least(act, hT_done, 2 * t - 2)
                        nc.scalar.activation(hid[:, k % 2, HH * part:HH * (part + 1)], p_h[part][:, 0:HH],
                                             ACT.Gelu).then_inc(gelu_done, 1)
                        if part == 0 and live(k, -1):
                            take_z(t + 1, (k + 1) % 2)
            over_steps(act, step)

        @block.tensor
        def _(pe):
            pe.wait_ge(w_loaded, 16 * (2 * EXPERTS + 1))

            def turn_z(t, b):
                pe.wait_ge(z_done, t + 1)
                at_least(pe, zT_taken, t)
                for c in range(2):
                    last = nc.tensor.transpose(p_z[:, c, :], z[:, b, P * c:P * (c + 1)], ident[:])
                last.then_inc(zT_done, 1)

            def first_layer(t, b, part, expert):
                pe.wait_ge(zT_taken, t + 1)
                at_least(pe, gelu_done, 2 * t + part - 1)
                for c in range(2):
                    last = nc.tensor.matmul(p_h[part][:, 0:HH], zT[:, b, c, :],
                                            w1[:, bass.ds(expert, 1), c, HH * part:HH * (part + 1)]
                                            .rearrange("p e h -> p (e h)"), start=(c == 0), stop=(c == 1))
                last.then_inc(h_done, 1)

            def turn_hidden(t, b, part):
                pe.wait_ge(gelu_done, 2 * t + part + 1)
                at_least(pe, hT_taken, 2 * t + part - 1)
                for m in range(3):
                    at = HH * part + P * m
                    last = nc.tensor.transpose(p_hT[part][:, P * m:P * (m + 1)], hid[:, b, at:at + P], ident[:])
                last.then_inc(hT_done, 1)

            def second_layer(t, b, expert):
                at_least(pe, result_done, t - 1)
                for m in range(KH):
                    if m % 3 == 0:
                        pe.wait_ge(hT_taken, 2 * t + m // 3 + 1)
                    last = nc.tensor.matmul(p_y[b][:, 0:C], hidT[:, b, m, :],
                                            w2[:, bass.ds(expert, 1), m, :].rearrange("p e c -> p (e c)"),
                                            start=(m == 0), stop=(m == KH - 1))
                last.then_inc(y_done, 1)

            def step(t, k, half, rnd):
                if k == 0:
                    turn_z(t, 0)
                if live(k, -1):
                    turn_z(t + 1, (k + 1) % 2)
                if live(k, 0):
                    expert = pe.value_load(tile_expert[0:1, bass.ds(t, 1)], min_val=0, max_val=EXPERTS - 1)
                    first_layer(t, k % 2, 0, expert)
                if live(k, 1):
                    for part in range(2):
                        turn_hidden(t - 1, (k - 1) % 2, part)
                if live(k, 0):
                    first_layer(t, k % 2, 1, expert)
                if live(k, 1):
                    last_expert = pe.value_load(tile_expert[0:1, bass.ds(t - 1, 1)], min_val=0, max_val=EXPERTS - 1)
                    second_layer(t - 1, (k - 1) % 2, last_expert)
            over_steps(pe, step)


def kernel(x, L0_tok_W, L0_tok_b, L0_attn_qkv_weight, L0_attn_qkv_bias, L0_attn_proj_weight, L0_attn_proj_bias,
           L0_ffn_gate_w, L0_ffn_gate_b, L0_ffn_gate_center, L0_ffn_w1, L0_ffn_b1, L0_ffn_w2, L0_ffn_b2):
    import numpy as np
    from concourse import bacc
    from concourse.bass_utils import run_bass_kernel_spmd

    x = np.asarray(x).reshape(IMAGES, CHANNELS, GRID, PATCH, GRID, PATCH)
    patches = np.ascontiguousarray(x.transpose(1, 3, 5, 0, 2, 4).reshape(D_IN, ALL))

    def with_bias(w, b):
        out = np.zeros((2 * P, w.shape[1]), np.float32)
        out[:C] = w
        out[C] = b
        return out

    def by_dim(first, heads):
        return [first + h * HD + d for d in range(HD) for h in heads]

    order = (by_dim(0, range(8)) + by_dim(C, range(8)) + by_dim(0, range(8, 12)) + by_dim(C, range(8, 12))
             + list(range(2 * C, 3 * C)))
    qkv_w = with_bias(np.asarray(L0_attn_qkv_weight).T[:, order], np.asarray(L0_attn_qkv_bias)[order])
    proj_w = np.zeros((HEADS, 2 * HD, C), np.float32)
    proj_w[:, :HD] = np.asarray(L0_attn_proj_weight).T.reshape(HEADS, HD, C)
    proj_w[0, HD] = np.asarray(L0_attn_proj_bias)
    w1 = np.stack([with_bias(w, b) for w, b in zip(np.asarray(L0_ffn_w1), np.asarray(L0_ffn_b1))])
    gate_w = np.zeros((2 * P, EXPERTS), np.float32)
    gate_w[:C] = np.asarray(L0_ffn_gate_w)
    arrays = {
        "patches": patches,
        "tok_w": np.ascontiguousarray(np.asarray(L0_tok_W).T),
        "tok_b": np.asarray(L0_tok_b),
        "qkv_w": qkv_w,
        "proj_w": proj_w.reshape(3 * P, C),
        "gate_w": gate_w,
        "gate_b": np.asarray(L0_ffn_gate_b),
        "gate_c": np.asarray(L0_ffn_gate_center),
        "w1": w1,
        "w2": np.asarray(L0_ffn_w2),
        "b2": np.asarray(L0_ffn_b2).reshape(-1),
    }
    nc = bacc.Bacc("TRN2", target_bir_lowering=False, num_devices=1)
    a = {n: nc.dram_tensor("in_" + n, v.shape, F32, kind="ExternalInput").ap() for n, v in arrays.items()}
    a["out"] = nc.dram_tensor("out", [ALL, C], F32, kind="ExternalOutput").ap()
    vit_block(nc, a)
    r = run_bass_kernel_spmd(nc, [{"in_" + n: v for n, v in arrays.items()}], core_ids=[0])
    return r.results[0]["out"].reshape(IMAGES, TOK, C)
```

```python
from contextlib import ExitStack

import concourse.bass as bass
from concourse import mybir

F32 = mybir.dt.float32
BF16 = mybir.dt.bfloat16
I32 = mybir.dt.int32
ALU = mybir.AluOpType
ACT = mybir.ActivationFunctionType
AX = mybir.AxisListType

P = 128
IMAGES, CHANNELS, SIDE = 64, 3, 224
GRID = 14
PATCH = SIDE // GRID
TOK = GRID * GRID
ALL = IMAGES * TOK
D_IN = CHANNELS * PATCH * PATCH
C = 192
HEADS, HD = 12, 16
HID, EXPERTS = 768, 4
KIN = D_IN // P
KH = HID // P
EPS = 1e-5

NT = ALL // P
GT = 7
GROUP = GT * P
GROUPS = NT // GT
LAG = 3

HALF = TOK // 2
UNITS = 12
TLAG = 6
SPLIT_ROWS = 6 * HD
Q_PARTS = (0, 0, 0, 1, 1, 2)
K_PARTS = (0, 1, 2, 0, 1, 0)
SCALE = float(HD) ** -0.5
STACK = 16 * 12
PROB_SLOTS = 6
FIRST_SLOTS = 6
ROUNDS = (IMAGES - FIRST_SLOTS) // 4

ROW = C + 4
MEAN, VAR, RSTD, TOKEN = C, C + 1, C + 2, C + 3
REGION = ALL + P
SPARE = EXPERTS * REGION
TILES = (ALL + EXPERTS * (P - 1)) // P
RING = 6
TILES = -(-TILES // RING) * RING


def settled(eng, passed):
    eng.sem_inc(passed, 1)


def at_least(eng, semaphore, value):
    if not isinstance(value, int) or value > 0:
        eng.wait_ge(semaphore, value)


def at_least(eng, semaphore, value):
    if not isinstance(value, int) or value > 0:
        eng.wait_ge(semaphore, value)


def at_least(eng, semaphore, value):
    if not isinstance(value, int) or value > 0:
        eng.wait_ge(semaphore, value)


def at_least(eng, semaphore, value):
    if not isinstance(value, int) or value > 0:
        eng.wait_ge(semaphore, value)


def at_least(eng, semaphore, value):
    if not isinstance(value, int) or value > 0:
        eng.wait_ge(semaphore, value)


def at_least(eng, semaphore, value):
    if not isinstance(value, int) or value > 0:
        eng.wait_ge(semaphore, value)


def at_least(eng, semaphore, value):
    if not isinstance(value, int) or value > 0:
        eng.wait_ge(semaphore, value)


def at_least(eng, semaphore, value):
    if not isinstance(value, int) or value > 0:
        eng.wait_ge(semaphore, value)


def at_least(eng, semaphore, value):
    if not isinstance(value, int) or value > 0:
        eng.wait_ge(semaphore, value)


def at_least(eng, semaphore, value):
    if not isinstance(value, int) or value > 0:
        eng.wait_ge(semaphore, value)


def at_least(eng, semaphore, value):
    if not isinstance(value, int) or value > 0:
        eng.wait_ge(semaphore, value)


def at_least(eng, semaphore, value):
    if not isinstance(value, int) or value > 0:
        eng.wait_ge(semaphore, value)


def vit_block(nc, a):
    with ExitStack() as ctx:
        def sb(stack, name, shape, dt=F32):
            return stack.enter_context(nc.sbuf_tensor(name, shape, dt))

        def ps(stack, name, shape, dt=F32):
            return stack.enter_context(nc.psum_tensor(name, shape, dt))

        def sem(name):
            return ctx.enter_context(nc.semaphore(name))

        h_dram = nc.dram_tensor("h_tokens", [ALL, C], F32, kind="Internal").ap()
        rows_dram = nc.dram_tensor("rows_by_expert", [SPARE + P, ROW], F32, kind="Internal").ap()

        ident = sb(ctx, "ident", [P, P])
        tile_expert = sb(ctx, "tile_expert", [P, TILES], I32)
        tile_row = sb(ctx, "tile_row", [P, TILES], I32)
        with ExitStack() as st:
            xT = sb(st, "xT", [P, 2, ALL])
            absmax = sb(st, "absmax", [P, GROUPS, 2])
            phase_a(nc, a, sb, ps, sem, xT, ident, absmax, h_dram)
            phase_b(nc, a, sb, ps, sem, xT, ident, absmax, h_dram, rows_dram, tile_expert, tile_row)
        phase_c(nc, a, sb, ps, sem, ident, rows_dram, tile_expert, tile_row)


def phase_a(nc, a, sb, ps, sem, xT, ident, absmax, h_dram):
    with ExitStack() as st:
        patches = sb(st, "patches", [P, 2, KIN, GROUP])
        wt = sb(st, "wt", [P, KIN, C])
        bias = sb(st, "bias_tok", [P, C])
        h = sb(st, "h_a", [P, 2, GT, C])
        stats = sb(st, "stats_a", [P, 4, 6])
        mv = sb(st, "mv_a", [P, 4, 2])
        rstd = sb(st, "rstd_a", [P, 4, 1])
        vare = sb(st, "vare_a", [P, 4, 1])
        expo = sb(st, "expo_a", [P, 1])
        x = sb(st, "x_a", [P, 4, 2 * P])
        p_h = [ps(st, f"p_h{i}", [P, C]) for i in range(2)]
        p_x = [ps(st, f"p_x{i}", [P, 2, P]) for i in range(2)]

        loaded_w = sem("a_loaded_w")
        loaded = [sem(f"a_loaded{i}") for i in range(2)]
        const0, const = sem("a_const0"), sem("a_const")
        embedded, h_done, stats_done, mv_done, rstd_done, x_done = (
            sem("a_" + n) for n in ("embedded", "h_done", "stats_done", "mv_done", "rstd_done", "x_done"))
        turned, xT_done, max_done = sem("a_turned"), sem("a_xT_done"), sem("a_max_done")
        stored = [sem(f"a_stored{i}") for i in range(2)]

        waited_dve, waited_pool, vare_done = sem("a_waited_dve"), sem("a_waited_pool"), sem("a_vare_done")
        block = st.enter_context(nc.Block())
        patches_in = a["patches"].rearrange("(k p) t -> p k t", p=P)
        h_out = h_dram.rearrange("(n p) c -> p n c", p=P)

        def over_pairs(eng, body):
            body(0, True)
            with eng.Fori(1, GROUPS // 2) as i:
                body(i, False)

        @block.sync
        def _(sp):
            sp.dma_start(bias[:], a["tok_b"].partition_broadcast(P)).then_inc(loaded_w, 16)
            sp.dma_start(wt[:], a["tok_w"].rearrange("(k p) c -> p k c", p=P)).then_inc(loaded_w, 16)

            def body(i, first):
                for g in range(2):
                    if not first:
                        sp.wait_ge(embedded, (2 * i + g - 1) * GT)
                    for part in range(2):
                        ks = slice(3 * part, 3 * part + 3)
                        sp.dma_start(patches[:, g, ks, :],
                                     patches_in[:, ks, bass.ds((2 * i + g) * GROUP, GROUP)]).then_inc(loaded[g], 16)
            over_pairs(sp, body)

        @block.gpsimd
        def _(pool):
            nc.gpsimd.memset(ident[:], 0.0).then_inc(const0, 1)
            pool.wait_ge(const0, 1)
            nc.gpsimd.affine_select(out=ident[:], in_=ident[:], compare_op=ALU.not_equal, fill=1.0,
                                    base=0, pattern=[[-1, P]], channel_multiplier=1).then_inc(const, 1)
            nc.gpsimd.memset(x[:, :, C:2 * P], 1.0).then_inc(const, 1)
            nc.gpsimd.memset(expo[:], -0.5).then_inc(const, 1)
            pool.wait_ge(const, 3)

            def body(i, first):
                for t in range(2 * GT):
                    pool.wait_ge(mv_done, 2 * GT * i + t + 1)
                    settled(pool, waited_pool)
                    nc.gpsimd.tensor_scalar(vare[:, t % 2], mv[:, t % 2, 1:2], EPS, None, ALU.add).then_inc(vare_done, 1)
                    pool.wait_ge(vare_done, 2 * GT * i + t + 1)
                    nc.gpsimd.tensor_tensor(rstd[:, t % 2], vare[:, t % 2], expo[:], ALU.pow).then_inc(rstd_done, 1)
                    if t % GT == GT - 1:
                        g = t // GT
                        pool.wait_ge(h_done, (2 * i + g + 1) * GT)
                        pool.dma_start(h_out[:, bass.ds((2 * i + g) * GT, GT), :], h[:, g]).then_inc(stored[g], 16)
            over_pairs(pool, body)
            for g in range(2):
                pool.wait_ge(stored[g], 16 * (GROUPS // 2))

        @block.tensor
        def _(pe):
            pe.wait_ge(loaded_w, 32)
            pe.wait_ge(const, 2)

            def turn(n, slot):
                pe.wait_ge(x_done, n + 1)
                for c in range(2):
                    last = nc.tensor.transpose(p_x[slot % 2][:, c, :], x[:, slot % 4, c * P:(c + 1) * P], ident[:])
                last.then_inc(turned, 1)

            def body(i, first):
                for t in range(2 * GT):
                    n = 2 * GT * i + t
                    if t % GT == 0:
                        pe.wait_ge(loaded[t // GT], 32 * (i + 1))
                    if not first or t >= 2:
                        pe.wait_ge(h_done, n - 1)
                    for k in range(KIN):
                        last = nc.tensor.matmul(p_h[t % 2][:], patches[:, t // GT, k, (t % GT) * P:(t % GT + 1) * P],
                                                wt[:, k, :], start=(k == 0), stop=(k == KIN - 1))
                    last.then_inc(embedded, 1)
                    if not first or t >= LAG:
                        if not first or t >= LAG + 2:
                            pe.wait_ge(xT_done, n - LAG - 1)
                        turn(n - LAG, (t - LAG) % 2)
            over_pairs(pe, body)
            for k in range(LAG):
                n = NT - LAG + k
                pe.wait_ge(xT_done, n - 1)
                turn(n, n % 2)

        @block.vector
        def _(dve):
            dve.wait_ge(loaded_w, 32)
            dve.wait_ge(const, 2)

            def aggregate(n, s):
                dve.wait_ge(stats_done, n + 1)
                settled(dve, waited_dve)
                nc.vector.bn_aggr(mv[:, s], stats[:, s]).then_inc(mv_done, 1)

            def normalise(n, s, t, free):
                dve.wait_ge(rstd_done, n + 1)
                if free:
                    dve.wait_ge(turned, n - 1)
                g, k = (t // GT) % 2, t % GT
                nc.vector.tensor_scalar(x[:, s, 0:C], h[:, g, k], mv[:, s, 0:1], rstd[:, s], ALU.subtract,
                                        ALU.mult).then_inc(x_done, 1)

            def largest(g):
                dve.wait_ge(xT_done, (g + 1) * GT)
                nc.vector.tensor_reduce(absmax[:, bass.ds(g, 1), :].rearrange("p g c -> p (g c)"),
                                        xT[:, :, bass.ds(g * GROUP, GROUP)], AX.X, ALU.max,
                                        apply_absolute_value=True).then_inc(max_done, 1)

            def body(i, first):
                for t in range(2 * GT):
                    n = 2 * GT * i + t
                    s = t % 2
                    dve.wait_ge(embedded, n + 1)
                    if not first and t % GT == 0:
                        dve.wait_ge(stored[t // GT], 16 * i)
                    nc.vector.tensor_tensor(h[:, t // GT, t % GT], p_h[t % 2][:], bias[:], ALU.add).then_inc(h_done, 1)
                    if not first or t >= 1:
                        aggregate(n - 1, 1 - s)
                    if not first or t >= 2:
                        normalise(n - 2, s, (t - 2) % (2 * GT), not first or t >= 4)
                    dve.wait_ge(h_done, n + 1)
                    nc.vector.bn_stats(stats[:, s], h[:, t // GT, t % GT]).then_inc(stats_done, 1)
                    if not first and t == 6:
                        largest(2 * i - 1)
                    if t == 13:
                        largest(2 * i)
            over_pairs(dve, body)
            s = (NT - 1) % 2
            aggregate(NT - 1, s)
            normalise(NT - 2, 1 - s, 2 * GT - 2, True)
            normalise(NT - 1, s, 2 * GT - 1, True)
            largest(GROUPS - 1)
            dve.wait_ge(max_done, GROUPS)

        @block.scalar
        def _(act):
            def take(n, slot):
                act.wait_ge(turned, n + 1)
                nc.scalar.copy(xT[:, :, bass.ds(n * P, P)], p_x[slot][:]).then_inc(xT_done, 1)

            def body(i, first):
                for t in range(2 * GT):
                    if not first or t >= LAG:
                        take(2 * GT * i + t - LAG, (t - LAG) % 2)
            over_pairs(act, body)
            for n in range(NT - LAG, NT):
                take(n, n % 2)
            act.wait_ge(xT_done, NT)


def phase_b(nc, a, sb, ps, sem, xT, ident, absmax, h_dram, rows_dram, tile_expert, tile_row):
    with ExitStack() as st:
        wqkv = sb(st, "wqkv", [P, 2, 3 * C])
        wproj = sb(st, "wproj", [P, 3, C])
        gate_w = sb(st, "gate_w", [P, 2, EXPERTS])
        gate_b = sb(st, "gate_b", [P, EXPERTS])
        gate_c = sb(st, "gate_c", [P, EXPERTS])
        identb = sb(st, "identb", [P, P], BF16)
        smooth = sb(st, "smooth", [P, 8, 2])
        xs = sb(st, "x_smoothed", [P, 2, 2, 2 * TOK])
        rest = sb(st, "rest", [P, 2, 2 * TOK])
        part = sb(st, "part", [P, 3, 3, 2 * TOK], BF16)
        qs = sb(st, "q_stack", [P, 2, HEADS, 2 * TOK], BF16)
        ks = sb(st, "k_stack", [P, 2, HEADS, 2 * TOK], BF16)
        vs = sb(st, "values", [P, 4, 2, HEADS, 2 * HD])
        probs = sb(st, "probs", [P, PROB_SLOTS, 2 * TOK])
        mx = sb(st, "mx", [P, 2, 2, HEADS])
        negm = sb(st, "negm", [P, 2, 2, HEADS], BF16)
        negmT = sb(st, "negmT", [2 * HEADS, TOK], BF16)
        o_raw = sb(st, "o_raw", [P, 3, TOK])
        recip = sb(st, "recip", [P, 2, HEADS])
        recip_rows = sb(st, "recip_rows", [P, 2, HEADS, 2 * HD])
        o = sb(st, "o_norm", [P, 3, TOK])
        hb = sb(st, "h_b", [P, 4, 2, C])
        rows = sb(st, "rows_b", [P, 2, 2, ROW])
        stats = sb(st, "stats_b", [P, 2, 6])
        vare = sb(st, "vare_b", [P, 2])
        expo = sb(st, "expo_b", [P, 3, 2])
        z = sb(st, "z_b", [P, 2, 2 * P])
        zT = sb(st, "zT_b", [P, 2, TOK])
        before = sb(st, "before", [P, P], BF16)
        ones = sb(st, "ones", [P, P], BF16)
        sum_rows = sb(st, "sum_rows", [P, 4])
        prefer = sb(st, "prefer", [P, EXPERTS])
        region = sb(st, "region", [P, EXPERTS])
        lane = sb(st, "lane", [P, 1])
        count_i = sb(st, "count_i", [P, TILES], I32)
        token_i = sb(st, "token_i", [P, 2, 2], I32)
        padding = sb(st, "padding", [P, ROW])
        score = sb(st, "score", [P, 2, EXPERTS])
        best = sb(st, "best", [P, 2])
        liked = sb(st, "liked", [P, 2, EXPERTS])
        likedest = sb(st, "likedest", [P, 2])
        chosen = sb(st, "chosen", [P, 2, EXPERTS], BF16)
        place = sb(st, "place", [P, 2, EXPERTS])
        where_f = sb(st, "where_f", [P, 2])
        where_i = sb(st, "where_i", [P, 2, 2], I32)
        base = sb(st, "base", [P, EXPERTS])
        pad_i = sb(st, "pad_i", [P, EXPERTS], I32)
        table = sb(st, "table", [P, 4, TILES])
        few = sb(st, "few", [P, 5, EXPERTS])
        few_i = sb(st, "few_i", [P, 2, EXPERTS], I32)

        p_s = [ps(st, f"p_s{i}", [P, 512]) for i in range(2)]
        p_t = [ps(st, f"p_t{i}", [P, 512]) for i in range(2)]
        p_o = [ps(st, f"p_o{i}", [P, 512]) for i in range(2)]
        p_qkv = ps(st, "p_qkv", [P, 512])
        p_misc = ps(st, "p_misc", [P, 512])
        p_zT = p_misc[:, 0:2 * TOK]
        p_gate, p_sums = p_misc[0:HALF, 400:400 + 2 * EXPERTS], p_misc[0:HALF, 416:416 + 2 * HEADS]
        p_recip = p_misc[:, 0:2 * TOK]
        p_proj, p_place = p_misc[0:HALF, 0:2 * C], p_misc[0:HALF, 400:400 + 2 * EXPERTS]
        p_total = p_misc[:, 400 + 2 * EXPERTS:400 + 3 * EXPERTS]
        p_recip2 = p_o[1][:, 300:300 + TOK]
        p_negmT = p_o[1][0:2 * HEADS, 200:200 + HALF].bitcast(BF16)

        w_loaded, const, smoothed, x_smooth, step, powers = (
            sem("b_" + n) for n in ("w_loaded", "const", "smoothed", "x_smooth", "step", "powers"))
        h_loaded = [sem(f"b_h_loaded{i}") for i in range(4)]
        s_done, max_done, t_done, exp_done = (sem("b_" + n) for n in ("scores", "max", "scoresT", "exp"))
        pv_done, o_taken, sums_done, recip_done, recipT_done, norm_done = (
            sem("b_" + n) for n in ("pv", "o_taken", "sums", "recip", "recipT", "norm"))
        negm1_done, negm_done, negmT_done, negmT_taken, negm_placed = (
            sem("b_" + n) for n in ("negm1", "negm", "negmT", "negmT_taken", "negm_placed"))
        qk_done, first_done, rest_done, second_done, third_done = (
            sem("b_" + n) for n in ("qk", "part1", "rest", "part2", "part3"))
        v_done, v_taken, stacked = sem("b_v"), sem("b_v_taken"), [sem(f"b_stacked{i}") for i in range(2)]
        proj_done, h2_done, stats_done, mv_done, vare_done, rstd_done, z_done, zT_done, zT_taken = (
            sem("b_" + n) for n in ("proj", "h2", "stats", "mv", "vare", "rstd", "z", "zT", "zT_taken"))
        gate_done, chosen_done, ranked, placed, token_done, padded = (
            sem("b_" + n) for n in ("gate", "chosen", "ranked", "placed", "token", "padded"))
        scattered = [sem(f"b_scattered{i}") for i in range(2)]
        pad_ready, tables, waited_pool, waited_sp, waited_dve = (
            sem("b_" + n) for n in ("pad_ready", "tables", "waited_pool", "waited_sp", "waited_dve"))
        block = st.enter_context(nc.Block())

        FILLS = 19
        MAXIMA_STEPS = 3
        CHOOSE, PLACE = 6, 5
        HALVES = [slice(HALF * t, HALF * (t + 1)) for t in range(2)]

        def over_slots(eng, slot):
            for n in range(FIRST_SLOTS):
                slot(n, n, n // 2, n // 4)
            with eng.Fori(0, ROUNDS) as i:
                for k in range(FIRST_SLOTS, FIRST_SLOTS + 4):
                    slot(4 * i + k, k, 2 * i + k // 2, i + k // 4)
            for n in range(FIRST_SLOTS + 4 * ROUNDS, IMAGES + 4):
                slot(n, n, n // 2, n // 4)

        def live(k, behind):
            return 0 <= k - behind < IMAGES

        def makes_pair(k):
            return k % 2 == 0 and k + 2 < IMAGES

        def unit(u, turned):
            if not turned:
                return u // 6, 2 * (u % 6)
            return (u // 2) % 2, 4 * (u // 4) + 2 * (u % 2)

        @block.sync
        def _(sp):
            sp.dma_start(wqkv[:], a["qkv_w"].rearrange("(k p) c -> p k c", p=P)).then_inc(w_loaded, 16)
            sp.dma_start(wproj[:], a["proj_w"].rearrange("(k p) c -> p k c", p=P)).then_inc(w_loaded, 16)
            sp.dma_start(gate_w[:], a["gate_w"].rearrange("(k p) e -> p k e", p=P)).then_inc(w_loaded, 16)
            for dst, name in ((gate_b, "gate_b"), (gate_c, "gate_c")):
                sp.dma_start(dst[:], a[name].partition_broadcast(P)).then_inc(w_loaded, 16)

            def stack(p, b, late):
                sp.wait_ge(third_done, 3 * p + 2 + late)
                settled(sp, waited_sp)
                for r in range(6):
                    rws = slice(HD * r, HD * (r + 1))
                    for dst, parts, col, low in ((qs, Q_PARTS, 0, 0), (ks, K_PARTS, 1, 64)):
                        if late:
                            sp.dma_start(dst[rws, b, 8:12, :], part[low:low + 64, parts[r], 2, :]).then_inc(stacked[1], 16)
                        else:
                            sp.dma_start(dst[rws, b, 0:8, :], part[:, parts[r], col, :]).then_inc(stacked[0], 16)

            def lay_max(m, k):
                sp.wait_ge(negmT_taken, m + 1)
                col = TOK * (k % 2)
                sp.dma_start(qs[96:98, (k // 2) % 2, :, col:col + TOK], negmT[:]).then_inc(negm_placed, 16)

            def slot(n, k, pair, quad):
                if k == 0:
                    for late in range(2):
                        stack(0, 0, late)
                if live(k, 1):
                    lay_max(n - 1, k - 1)
                if k % 2 == 1 and k < IMAGES - 1:
                    for late in range(2):
                        if k >= 3:
                            sp.wait_ge(t_done, UNITS * (n - 1) if late else UNITS * (n - 2) + 8)
                            settled(sp, waited_sp)
                        sp.wait_ge(stacked[late], STACK * (pair + 1))
                        settled(sp, waited_sp)
                        stack(pair + 1, (k // 2 + 1) % 2, late)
                if live(k, 0):
                    if k >= 4:
                        sp.wait_ge(h2_done, n - 3)
                    sp.dma_start(hb[0:HALF, k % 4], h_dram[bass.ds(n * TOK, TOK), :]
                                 .rearrange("(t p) c -> p t c", p=HALF)).then_inc(h_loaded[k % 4], 16)
            over_slots(sp, slot)

        @block.gpsimd
        def _(pool):
            filled = [0]

            def alone(ins):
                filled[0] += 1
                ins.then_inc(const, 1)
                pool.wait_ge(const, filled[0])

            alone(nc.gpsimd.tensor_copy(identb[:], ident[:]))
            alone(nc.gpsimd.memset(ks[96:98], 1.0))
            alone(nc.gpsimd.memset(vs[:], 0.0))
            alone(nc.gpsimd.memset(vs[0:HALF, :, :, :, HD:2 * HD], 1.0))
            alone(nc.gpsimd.memset(probs[96:128], 0.0))
            alone(nc.gpsimd.memset(z[:, :, C:2 * P], 1.0))
            for i, power in enumerate((-0.5, 0.35, -0.65)):
                alone(nc.gpsimd.memset(expo[:, i], power))
            alone(nc.gpsimd.memset(ones[:], 1.0))
            alone(nc.gpsimd.affine_select(out=before[:], in_=ones[:], compare_op=ALU.is_gt, fill=0.0,
                                          base=0, pattern=[[1, P]], channel_multiplier=-1))
            alone(nc.gpsimd.memset(sum_rows[:], 0.0))
            alone(nc.gpsimd.affine_select(out=sum_rows[:], in_=sum_rows[:], compare_op=ALU.not_equal, fill=1.0,
                                          base=-HD, pattern=[[-2 * HD, 4]], channel_multiplier=1))
            alone(nc.gpsimd.iota(count_i[:], pattern=[[1, TILES]], base=0, channel_multiplier=0))
            alone(nc.gpsimd.tensor_copy(table[:, 0], count_i[:]))
            alone(nc.gpsimd.iota(token_i[:], pattern=[[TOK, 2], [HALF, 2]], base=-2 * TOK, channel_multiplier=1))
            for b in range(2):
                alone(nc.gpsimd.tensor_copy(rows[:, b, :, TOKEN], token_i[:, b]))
            alone(nc.gpsimd.iota(token_i[:, 0, 0:1], pattern=[[0, 1]], base=0, channel_multiplier=1))
            assert filled[0] == FILLS

            pool.wait_ge(step, MAXIMA_STEPS)
            nc.gpsimd.tensor_tensor(smooth[:, 2, :], smooth[:, 0, :], expo[:, 1], ALU.pow).then_inc(powers, 1)
            nc.gpsimd.tensor_tensor(smooth[:, 3, :], smooth[:, 1, :], expo[:, 2], ALU.pow).then_inc(powers, 1)

            def split(p, u, b):
                j = 3 * p + u
                pool.wait_ge(rest_done, j + 1)
                settled(pool, waited_pool)
                nc.gpsimd.tensor_scalar(part[:, 1, u, :], rest[:, b], 1.0, None, ALU.mult).then_inc(second_done, 1)
                pool.wait_ge(second_done, j + 1)
                nc.gpsimd.tensor_tensor(part[:, 2, u, :], rest[:, b], part[:, 1, u, :],
                                        ALU.subtract).then_inc(third_done, 1)

            def deviation(m, b):
                pool.wait_ge(mv_done, 2 * m + 2)
                settled(pool, waited_pool)
                nc.gpsimd.tensor_scalar(vare[0:HALF], rows[0:HALF, b, :, VAR], EPS, None, ALU.add)\
                    .then_inc(vare_done, 1)
                pool.wait_ge(vare_done, m + 1)
                nc.gpsimd.tensor_tensor(rows[0:HALF, b, :, RSTD], vare[0:HALF], expo[0:HALF, 0], ALU.pow)\
                    .then_inc(rstd_done, 1)
                nc.gpsimd.tensor_scalar(rows[0:HALF, b, :, TOKEN], rows[0:HALF, b, :, TOKEN], 2.0 * TOK, None,
                                        ALU.add).then_inc(token_done, 1)

            def scatter(m, b):
                pool.wait_ge(placed, PLACE * (m + 1))
                pool.wait_ge(rstd_done, m + 1)
                pool.wait_ge(token_done, m + 1)
                settled(pool, waited_pool)
                for t in range(2):
                    nc.gpsimd.indirect_dma_start(
                        out=rows_dram, out_offset=bass.IndirectOffsetOnAxis(ap=where_i[0:HALF, b, t:t + 1], axis=0),
                        in_=rows[0:HALF, b, t, :], in_offset=None).then_inc(scattered[b], 16)

            for u in range(3):
                split(0, u, u % 2)

            def slot(n, k, pair, quad):
                if live(k, 3):
                    deviation(n - 3, (k - 3) % 2)
                for u in range(3):
                    if makes_pair(k):
                        split(pair + 1, u, (k // 2 + 1 + u) % 2)
                    if live(k, 4) and u == 0:
                        scatter(n - 4, k % 2)
            over_slots(pool, slot)

            pool.wait_ge(pad_ready, 2)
            for e in range(EXPERTS):
                nc.gpsimd.indirect_dma_start(
                    out=rows_dram, out_offset=bass.IndirectOffsetOnAxis(ap=pad_i[:, e:e + 1], axis=0),
                    in_=padding[:], in_offset=None).then_inc(padded, 16)
            pool.dma_start(rows_dram[SPARE:SPARE + P, :], padding[:]).then_inc(padded, 16)
            for b in range(2):
                pool.wait_ge(scattered[b], 32 * IMAGES // 2)
            pool.wait_ge(padded, 16 * (EXPERTS + 1))

        @block.vector
        def _(dve):
            dve.wait_ge(w_loaded, 80)
            dve.wait_ge(const, FILLS)
            n_steps = [0]

            def then(ins):
                n_steps[0] += 1
                ins.then_inc(step, 1)
                dve.wait_ge(step, n_steps[0])

            gx, mw, gp, wp, r, pw, cs, inv = (smooth[:, i, :] for i in range(8))
            then(nc.vector.tensor_reduce(gx, absmax[:].rearrange("p g c -> p c g"), AX.X, ALU.max))
            then(nc.vector.tensor_reduce(mw, wqkv[:], AX.X, ALU.max, apply_absolute_value=True))
            then(nc.vector.memset(smooth[C - P:P, 0:2, 1:2], 1.0))
            assert n_steps[0] == MAXIMA_STEPS
            dve.wait_ge(powers, 2)
            then(nc.vector.tensor_tensor(r, gp, wp, ALU.mult))
            then(nc.vector.tensor_scalar(pw.bitcast(I32), r.bitcast(I32), 0x7F800000, None, ALU.bitwise_and))
            then(nc.vector.scalar_tensor_tensor(out=cs, in0=pw, scalar=1.5, in1=r, op0=ALU.mult, op1=ALU.is_lt))
            then(nc.vector.scalar_tensor_tensor(out=cs, in0=cs, scalar=1.0, in1=pw, op0=ALU.add, op1=ALU.mult))
            then(nc.vector.reciprocal(inv, cs))
            for c in range(2):
                nc.vector.tensor_scalar(wqkv[:, c], wqkv[:, c], cs[:, c:c + 1], None, ALU.mult).then_inc(smoothed, 1)
            then(nc.vector.tensor_tensor(gate_b[:], gate_b[:], gate_c[:], ALU.subtract))
            for e in range(EXPERTS):
                then(nc.vector.memset(prefer[:, e:e + 1], float(EXPERTS - e)))
                then(nc.vector.memset(region[:, e:e + 1], float(e * REGION)))
            then(nc.vector.tensor_copy(base[:], region[:]))
            then(nc.vector.tensor_copy(lane[:], token_i[:, 0, 0:1]))

            def smooth_x(p, b):
                at_least(dve, v_done, 2 * p - 2)
                for c in range(2):
                    nc.vector.tensor_scalar(xs[:, b, c], xT[:, c, bass.ds(2 * TOK * p, 2 * TOK)], inv[:, c:c + 1],
                                            None, ALU.mult).then_inc(x_smooth, 1)

            def leave(p, u, b):
                j = 3 * p + u
                dve.wait_ge(first_done, j + 1)
                at_least(dve, third_done, j - 1)
                nc.vector.tensor_tensor(rest[:, b], p_qkv[:, 0:2 * TOK], part[:, 0, u, :],
                                        ALU.subtract).then_inc(rest_done, 1)

            smooth_x(0, 0)
            for u in range(3):
                leave(0, u, u % 2)

            def biggest(n, k, u):
                half, head = unit(u, False)
                dve.wait_ge(s_done, UNITS * n + u + 1)
                nc.vector.tensor_reduce(mx[0:HALF, k % 2, half, head:head + 2],
                                        p_s[u % 2][0:HALF, 0:2 * TOK].rearrange("p (h t) -> p h t", h=2),
                                        AX.X, ALU.max).then_inc(max_done, 1)

            def negate(n, b):
                dve.wait_ge(max_done, UNITS * (n + 1))
                at_least(dve, negmT_done, n)
                nc.vector.tensor_scalar(negm[0:HALF, :, 0, :], mx[0:HALF, b], -1.0, None, ALU.mult).then_inc(negm1_done, 1)
                dve.wait_ge(negm1_done, n + 1)
                nc.vector.scalar_tensor_tensor(out=negm[0:HALF, :, 1, :], in0=mx[0:HALF, b], scalar=-1.0,
                                               in1=negm[0:HALF, :, 0, :], op0=ALU.mult, op1=ALU.subtract)\
                    .then_inc(negm_done, 1)

            def invert(m):
                dve.wait_ge(sums_done, m + 1)
                nc.vector.reciprocal(recip[0:HALF], p_sums.rearrange("p (t h) -> p t h", t=2)).then_inc(recip_done, 1)
                dve.wait_ge(recip_done, 2 * m + 1)
                at_least(dve, recipT_done, m)
                nc.vector.tensor_copy(recip_rows[0:HALF], recip[0:HALF].rearrange("p t (h o) -> p t h o", o=1)
                                      .broadcast_to([HALF, 2, HEADS, 2 * HD])).then_inc(recip_done, 1)

            def multiply(m):
                dve.wait_ge(recipT_done, m + 1)
                at_least(dve, proj_done, m)
                nc.vector.tensor_tensor(o[:, 0:2].rearrange("p g t -> p (g t)"), p_recip,
                                        o_raw[:, 0:2].rearrange("p g t -> p (g t)"), ALU.mult).then_inc(norm_done, 1)
                nc.vector.tensor_tensor(o[:, 2], p_recip2, o_raw[:, 2], ALU.mult).then_inc(norm_done, 1)

            def residual(m, b, earlier, hbuf, loads):
                dve.wait_ge(proj_done, m + 1)
                dve.wait_ge(h_loaded[hbuf], loads)
                at_least(dve, scattered[b], 32 * earlier)
                nc.vector.tensor_tensor(rows[0:HALF, b, :, 0:C], p_proj
                                        .rearrange("p (t c) -> p t c", t=2), hb[0:HALF, hbuf], ALU.add).then_inc(h2_done, 1)

            def statistics(m, b):
                dve.wait_ge(h2_done, m + 1)
                for t in range(2):
                    nc.vector.bn_stats(stats[0:HALF, t], rows[0:HALF, b, t, 0:C]).then_inc(stats_done, 1)
                dve.wait_ge(stats_done, 2 * m + 2)
                settled(dve, waited_dve)
                for t in range(2):
                    nc.vector.bn_aggr(rows[0:HALF, b, t, MEAN:VAR + 1], stats[0:HALF, t]).then_inc(mv_done, 1)

            def normalise(m, b):
                dve.wait_ge(rstd_done, m + 1)
                at_least(dve, zT_done, m)
                for t in range(2):
                    nc.vector.tensor_scalar(z[0:HALF, t, 0:C], rows[0:HALF, b, t, 0:C],
                                            rows[0:HALF, b, t, MEAN:MEAN + 1], rows[0:HALF, b, t, RSTD:RSTD + 1],
                                            ALU.subtract, ALU.mult).then_inc(z_done, 1)

            def over_halves(t, n):
                return t.rearrange("p (o e) -> p o e", o=1).broadcast_to([n, 2, EXPERTS])

            def over_experts(t):
                return t.rearrange("p (t o) -> p t o", o=1).broadcast_to([HALF, 2, EXPERTS])

            H = slice(0, HALF)

            def score_experts(m, k):
                dve.wait_ge(gate_done, m + 1)
                if live(k, 2):
                    dve.wait_ge(sums_done, m + 2)
                nc.vector.tensor_tensor(score[H], p_gate.rearrange("p (t e) -> p t e", t=2),
                                        over_halves(gate_b[H], HALF), ALU.add).then_inc(chosen_done, 1)

            def best_score(m):
                dve.wait_ge(chosen_done, CHOOSE * m + 1)
                nc.vector.tensor_reduce(best[H], score[H], AX.X, ALU.max).then_inc(chosen_done, 1)

            def like(m):
                dve.wait_ge(chosen_done, CHOOSE * m + 2)
                nc.vector.tensor_tensor(liked[H], score[H], over_experts(best[H]), ALU.is_ge).then_inc(chosen_done, 1)
                dve.wait_ge(chosen_done, CHOOSE * m + 3)
                nc.vector.tensor_tensor(liked[H], liked[H], over_halves(prefer[H], HALF), ALU.mult).then_inc(chosen_done, 1)

            def choose(m):
                dve.wait_ge(chosen_done, CHOOSE * m + 4)
                nc.vector.tensor_reduce(likedest[H], liked[H], AX.X, ALU.max).then_inc(chosen_done, 1)
                dve.wait_ge(chosen_done, CHOOSE * m + 5)
                at_least(dve, ranked, m)
                nc.vector.tensor_tensor(chosen[H], liked[H], over_experts(likedest[H]), ALU.is_equal).then_inc(chosen_done, 1)

            def rows_of_experts(m, k):
                dve.wait_ge(ranked, m + 1)
                if live(k, 3):
                    dve.wait_ge(proj_done, m + 2)
                nc.vector.tensor_tensor(place[H], p_place.rearrange("p (t e) -> p t e", t=2),
                                        over_halves(base[H], HALF), ALU.add).then_inc(placed, 1)
                dve.wait_ge(placed, PLACE * m + 1)
                nc.vector.tensor_tensor(base[:], p_total, base[:], ALU.add).then_inc(placed, 1)

            def row_of_chosen(m, b):
                nc.vector.tensor_tensor(place[H], place[H], chosen[H], ALU.mult).then_inc(placed, 1)
                dve.wait_ge(placed, PLACE * m + 3)
                nc.vector.tensor_reduce(where_f[H], place[H], AX.X, ALU.add).then_inc(placed, 1)
                dve.wait_ge(placed, PLACE * m + 4)
                nc.vector.tensor_copy(where_i[H, b], where_f[H]).then_inc(placed, 1)

            def slot(n, k, pair, quad):
                for u in range(UNITS):
                    if live(k, 3) and u == 0:
                        multiply(n - 3)
                    if live(k, 0):
                        biggest(n, k, u)
                    if makes_pair(k) and u in (3, 6, 9):
                        leave(pair + 1, (u - 3) // 3, (k // 2 + u // 3) % 2)
                    if live(k, 4) and u == 0:
                        choose(n - 4)
                    if makes_pair(k) and u == 0:
                        smooth_x(pair + 1, (k // 2 + 1) % 2)
                    if live(k, 3) and u == 2:
                        residual(n - 3, (k - 3) % 2, pair + (k - 3) // 2 - k // 2, (k - 3) % 4,
                                 16 * (quad + (k - 3) // 4 - k // 4 + 1))
                    if live(k, 4) and u == 2:
                        rows_of_experts(n - 4, k)
                    if live(k, 3) and u == 3:
                        statistics(n - 3, (k - 3) % 2)
                    if live(k, 4) and u == 4:
                        row_of_chosen(n - 4, k % 2)
                    if live(k, 3) and u == 5:
                        normalise(n - 3, (k - 3) % 2)
                    if live(k, 2) and u == 10:
                        invert(n - 2)
                    if live(k, 3) and u == 10:
                        score_experts(n - 3, k)
                    if live(k, 3) and u == 11:
                        best_score(n - 3)
                        like(n - 3)
                if live(k, 0):
                    negate(n, k % 2)
            over_slots(dve, slot)

            dve.wait_ge(placed, PLACE * IMAGES)
            then(nc.vector.memset(padding[:, 0:TOKEN], 0.0))
            nc.vector.tensor_scalar(padding[:, TOKEN:ROW], lane[:], float(ALL), None, ALU.add).then_inc(pad_ready, 1)
            nc.vector.tensor_scalar(pad_i[:], base[:], lane[:], None, ALU.add).then_inc(pad_ready, 1)
            tiles_f, ends, gaps = few[:, 0], few[:, 1], few[:, 2]
            then(nc.vector.tensor_tensor(few[:, 3], base[:], region[:], ALU.subtract))
            then(nc.vector.tensor_scalar(few_i[:, 0], few[:, 3], float(P - 1), None, ALU.add))
            then(nc.vector.tensor_scalar(few_i[:, 1], few_i[:, 0], 7, None, ALU.arith_shift_right))
            then(nc.vector.tensor_copy(tiles_f, few_i[:, 1]))
            then(nc.vector.tensor_copy(ends[:, 0:1], tiles_f[:, 0:1]))
            for e in range(1, EXPERTS):
                then(nc.vector.tensor_tensor(ends[:, e:e + 1], ends[:, e - 1:e], tiles_f[:, e:e + 1], ALU.add))
            then(nc.vector.tensor_scalar(gaps, tiles_f, -float(P), float(REGION), ALU.mult, ALU.add))
            number, expert, row, past = (table[:, i] for i in range(4))
            then(nc.vector.tensor_scalar(row, number, float(P), None, ALU.mult))
            then(nc.vector.memset(expert, 0.0))
            for e in range(EXPERTS - 1):
                then(nc.vector.tensor_scalar(past, number, ends[:, e:e + 1], None, ALU.is_ge))
                then(nc.vector.tensor_tensor(expert, expert, past, ALU.add))
                then(nc.vector.scalar_tensor_tensor(out=row, in0=past, scalar=gaps[:, e:e + 1], in1=row,
                                                    op0=ALU.mult, op1=ALU.add))
            then(nc.vector.tensor_scalar(past, number, ends[:, 3:4], None, ALU.is_lt))
            then(nc.vector.scalar_tensor_tensor(out=row, in0=row, scalar=-float(SPARE), in1=past,
                                                op0=ALU.add, op1=ALU.mult))
            nc.vector.tensor_scalar(tile_row[:], row, float(SPARE), None, ALU.add).then_inc(tables, 1)
            nc.vector.tensor_copy(tile_expert[:], expert).then_inc(tables, 1)
            dve.wait_ge(tables, 2)

        @block.scalar
        def _(act):
            def first_part(p, u):
                act.wait_ge(qk_done, 3 * p + u + 1)
                if u == 0:
                    for late in range(2):
                        at_least(act, stacked[late], STACK * p)
                nc.scalar.copy(part[:, 0, u, :], p_qkv[:, 0:2 * TOK]).then_inc(first_done, 1)

            for u in range(3):
                first_part(0, u)

            def exps(n, v):
                act.wait_ge(t_done, UNITS * n + v + 1)
                nc.scalar.activation(probs[0:HALF, v % PROB_SLOTS, :], p_t[v % 2][0:HALF, 0:2 * TOK], ACT.Exp,
                                     scale=SCALE).then_inc(exp_done, 1)

            def take_max(m):
                act.wait_ge(negmT_done, m + 1)
                at_least(act, negm_placed, 16 * m)
                nc.scalar.copy(negmT[:], p_negmT).then_inc(negmT_taken, 1)

            def take_outputs(m, bank):
                act.wait_ge(pv_done, 6 * m + 4 + 2 * bank)
                at_least(act, norm_done, 2 * m)
                if bank == 0:
                    nc.scalar.copy(o_raw[:, 0:2].rearrange("p g t -> p (g t)"), p_o[0][:, 0:2 * TOK]).then_inc(o_taken, 1)
                else:
                    nc.scalar.copy(o_raw[:, 2], p_o[1][:, 0:TOK]).then_inc(o_taken, 1)

            def slot(n, k, pair, quad):
                for u in range(UNITS):
                    if makes_pair(k) and u in (3, 6, 9):
                        first_part(pair + 1, (u - 3) // 3)
                    if u < TLAG and live(k, 2):
                        exps(n - 2, u - TLAG + UNITS)
                    if u >= TLAG and live(k, 1):
                        exps(n - 1, u - TLAG)
                    if u == 2 and live(k, 1):
                        take_max(n - 1)
                    if live(k, 2) and u in (TLAG - 2, TLAG + 1):
                        take_outputs(n - 2, (u - TLAG + 2) // 3)
                    if live(k, 3) and u == 8:
                        act.wait_ge(zT_done, n - 2)
                        at_least(act, gate_done, n - 3)
                        nc.scalar.copy(zT[:], p_zT.rearrange("p (c t) -> p c t", c=2)).then_inc(zT_taken, 1)
                    if live(k, 1) and u == 0:
                        act.wait_ge(v_done, n)
                        nc.scalar.copy(vs[0:HALF, (k - 1) % 4, :, :, 0:HD],
                                       p_qkv[0:HALF, 0:2 * C].rearrange("p (t h d) -> p t h d", t=2, d=HD))\
                            .then_inc(v_taken, 1)
            over_slots(act, slot)

        @block.tensor
        def _(pe):
            pe.wait_ge(smoothed, 2)
            pe.wait_ge(const, FILLS)

            def queries_keys(p, b, u):
                pe.wait_ge(x_smooth, 2 * p + 2)
                at_least(pe, rest_done, 3 * p + u)
                if u == 0:
                    at_least(pe, v_taken, 2 * p - 2)
                for c in range(2):
                    last = nc.tensor.matmul(p_qkv[:, 0:2 * TOK], wqkv[:, c, P * u:P * (u + 1)],
                                            xs[:, b, c], start=(c == 0), stop=(c == 1))
                last.then_inc(qk_done, 1)

            def values(n, k, pair):
                if makes_pair(k):
                    pe.wait_ge(rest_done, 3 * pair + 6)
                else:
                    pe.wait_ge(v_taken, n)
                at = TOK * (k % 2)
                for t in range(2):
                    for c in range(2):
                        last = nc.tensor.matmul(p_qkv[0:HALF, C * t:C * (t + 1)],
                                                xs[:, (k // 2) % 2, c, at + HALF * t:at + HALF * (t + 1)],
                                                wqkv[:, c, 2 * C:3 * C], start=(c == 0), stop=(c == 1))
                last.then_inc(v_done, 1)

            def scores(n, k, u, pair):
                half, head = unit(u, False)
                b, at = (k // 2) % 2, TOK * (k % 2)
                if u in (0, 4) and k % 2 == 0:
                    pe.wait_ge(stacked[u // 4], STACK * (pair + 1))
                at_least(pe, max_done, UNITS * n + u - 1)
                for i in range(2):
                    last = nc.tensor.matmul(p_s[u % 2][0:HALF, TOK * i:TOK * (i + 1)],
                                            qs[0:SPLIT_ROWS, b, head + i, at + HALF * half:at + HALF * (half + 1)],
                                            ks[0:SPLIT_ROWS, b, head + i, at:at + TOK], start=True, stop=True)
                last.then_inc(s_done, 1)

            def scores_turned(n, k, v):
                half, head = unit(v, True)
                b, at = (k // 2) % 2, TOK * (k % 2)
                if v == 0:
                    pe.wait_ge(negm_placed, 16 * (n + 1))
                at_least(pe, exp_done, UNITS * n + v - 1)
                for i in range(2):
                    last = nc.tensor.matmul(p_t[v % 2][0:HALF, TOK * i:TOK * (i + 1)],
                                            ks[0:SPLIT_ROWS + 2, b, head + i, at + HALF * half:at + HALF * (half + 1)],
                                            qs[0:SPLIT_ROWS + 2, b, head + i, at:at + TOK], start=True, stop=True)
                last.then_inc(t_done, 1)

            def outputs(m, k, s, more):
                g, half = s // 2, s % 2
                pe.wait_ge(exp_done, UNITS * m + 2 * s + 2)
                if s == 0:
                    pe.wait_ge(v_taken, m + 1)
                    at_least(pe, o_taken, 2 * m - 1)
                if s == 4:
                    at_least(pe, norm_done, 2 * m)
                    if more:
                        pe.wait_ge(negmT_taken, m + 2)
                for j in range(4):
                    last = nc.tensor.matmul(p_o[g // 2][32 * j:32 * j + 32, TOK * (g % 2):TOK * (g % 2 + 1)],
                                            vs[:, k % 4, half, 4 * g + j, :],
                                            probs[:, (2 * s + j // 2) % PROB_SLOTS, TOK * (j % 2):TOK * (j % 2 + 1)],
                                            start=(half == 0), stop=(half == 1), skip_group_check=True)
                last.then_inc(pv_done, 1)

            def turn_max(m, k):
                if live(k, 3):
                    pe.wait_ge(norm_done, 2 * m - 2)
                pe.wait_ge(negm_done, m + 1)
                at_least(pe, negmT_taken, m)
                for t in range(2):
                    last = nc.tensor.transpose(p_negmT[:, HALVES[t]],
                                               negm[0:HALF, t].rearrange("p a h -> p (a h)"), identb[0:HALF, 0:HALF])
                last.then_inc(negmT_done, 1)

            def add_sums(m):
                pe.wait_ge(o_taken, 2 * m + 2)
                at_least(pe, recip_done, 2 * m)
                for t in range(2):
                    for g in range(3):
                        last = nc.tensor.matmul(p_sums[:, HEADS * t + 4 * g:HEADS * t + 4 * g + 4],
                                                o_raw[:, g, HALVES[t]], sum_rows[:], start=True, stop=True)
                last.then_inc(sums_done, 1)

            def turn_recip(m, k):
                pe.wait_ge(recip_done, 2 * m + 2)
                if live(k, 3):
                    pe.wait_ge(chosen_done, CHOOSE * (m - 1) + 1)
                for g in range(3):
                    for t in range(2):
                        out = p_recip[:, TOK * g + HALF * t:TOK * g + HALF * (t + 1)] if g < 2 else p_recip2[:, HALVES[t]]
                        last = nc.tensor.transpose(out, recip_rows[0:HALF, t, 4 * g:4 * g + 4, :]
                                                   .rearrange("p h o -> p (h o)"), ident[0:HALF, 0:HALF])
                last.then_inc(recipT_done, 1)

            def project(m):
                pe.wait_ge(norm_done, 2 * m + 2)
                for t in range(2):
                    for g in range(3):
                        last = nc.tensor.matmul(p_proj[:, C * t:C * (t + 1)], o[:, g, HALVES[t]],
                                                wproj[:, g, :], start=(g == 0), stop=(g == 2))
                last.then_inc(proj_done, 1)

            def turn_z(m, k):
                pe.wait_ge(z_done, 2 * m + 2)
                pe.wait_ge(h2_done, m + 1)
                if live(k, 4):
                    pe.wait_ge(placed, PLACE * (m - 1) + 2)
                for t in range(2):
                    for c in range(2):
                        last = nc.tensor.transpose(p_zT[:, TOK * c + HALF * t:TOK * c + HALF * (t + 1)],
                                                   z[0:HALF, t, P * c:P * (c + 1)], ident[0:HALF, 0:HALF])
                last.then_inc(zT_done, 1)

            def gate(m):
                pe.wait_ge(zT_taken, m + 1)
                for t in range(2):
                    for c in range(2):
                        last = nc.tensor.matmul(p_gate[:, EXPERTS * t:EXPERTS * (t + 1)], zT[:, c, HALVES[t]],
                                                gate_w[:, c, :], start=(c == 0), stop=(c == 1))
                last.then_inc(gate_done, 1)

            def rank(m, k):
                pe.wait_ge(chosen_done, CHOOSE * (m + 1))
                if live(k, 3):
                    pe.wait_ge(norm_done, 2 * m + 4)
                H = slice(0, HALF)
                nc.tensor.matmul(p_place[:, 0:EXPERTS], before[H, H], chosen[H, 0], start=True, stop=True)
                nc.tensor.matmul(p_place[:, EXPERTS:2 * EXPERTS], before[H, H], chosen[H, 1], start=True, stop=False)
                nc.tensor.matmul(p_place[:, EXPERTS:2 * EXPERTS], ones[H, H], chosen[H, 0], start=False, stop=True)
                nc.tensor.matmul(p_total, ones[H, :], chosen[H, 0], start=True, stop=False)
                nc.tensor.matmul(p_total, ones[H, :], chosen[H, 1], start=False, stop=True).then_inc(ranked, 1)

            for u in range(3):
                queries_keys(0, 0, u)

            def slot(n, k, pair, quad):
                for u in range(UNITS):
                    if live(k, 0):
                        scores(n, k, u, pair)
                    if u < TLAG and live(k, 2):
                        scores_turned(n - 2, k - 2, u - TLAG + UNITS)
                    if u >= TLAG and live(k, 1):
                        scores_turned(n - 1, k - 1, u - TLAG)
                    if u % 2 == 1:
                        s = (u - TLAG - 3) // 2
                        if s >= 0 and live(k, 1):
                            outputs(n - 1, k - 1, s, False)
                        if s < 0 and live(k, 2):
                            outputs(n - 2, k - 2, s + 6, live(k, 1))
                    if live(k, 1) and u == 1:
                        turn_max(n - 1, k)
                    if live(k, 4) and u == 1:
                        rank(n - 4, k)
                    if live(k, 3) and u == 1:
                        project(n - 3)
                    if makes_pair(k) and u in (2, 5, 8):
                        queries_keys(pair + 1, (k // 2 + 1) % 2, (u - 2) // 3)
                    if live(k, 3) and u == 7:
                        turn_z(n - 3, k)
                    if live(k, 3) and u == 9:
                        gate(n - 3)
                    if live(k, 2) and u == 9:
                        add_sums(n - 2)
                    if live(k, 0) and u == 11:
                        values(n, k, pair)
                    if live(k, 2) and u == 11:
                        turn_recip(n - 2, k)
            over_slots(pe, slot)


def phase_c(nc, a, sb, ps, sem, ident, rows_dram, tile_expert, tile_row):
    with ExitStack() as st:
        w1 = sb(st, "w1", [P, EXPERTS, 2, HID])
        w2 = sb(st, "w2", [P, EXPERTS, KH, C])
        b2 = sb(st, "b2", [P, EXPERTS, C])
        rows = sb(st, "rows_c", [P, RING, ROW])
        z = sb(st, "z_c", [P, 2, 2 * P])
        zT = sb(st, "zT_c", [P, 2, 2, P])
        hid = sb(st, "hid", [P, 2, HID])
        hidT = sb(st, "hidT", [P, 2, KH, P])
        y = sb(st, "y", [P, 2, C])
        result = sb(st, "result", [P, 2, C])
        token = sb(st, "token", [P, RING, 1], I32)
        p_z = ps(st, "p_z", [P, 2, P])
        p_h = [ps(st, f"p_hid{i}", [P, 512]) for i in range(2)]
        p_hT = [ps(st, f"p_hidT{i}", [P, 512]) for i in range(2)]
        p_y = [ps(st, f"p_y{i}", [P, 512]) for i in range(2)]
        HH = HID // 2

        w_loaded, ones_done = sem("c_w_loaded"), sem("c_ones")
        loaded = [sem(f"c_rows{i}") for i in range(RING)]
        z_done, zT_done, zT_taken, h_done, gelu_done, hT_done, hT_taken = (
            sem("c_" + n) for n in ("z", "zT", "zT_taken", "hid", "gelu", "hidT", "hidT_taken"))
        y_done, biased, token_done, result_done = (sem("c_" + n) for n in ("y", "biased", "token", "result"))
        stored = [sem(f"c_stored{i}") for i in range(2)]
        waited_dve = sem("c_waited_dve")
        waited_pool = sem("c_waited_pool")
        block = st.enter_context(nc.Block())

        def over_steps(eng, step):
            for t in range(RING):
                step(t, t, t // 2, 0)
            with eng.Fori(1, TILES // RING - 1) as i:
                for k in range(RING, 2 * RING):
                    step(RING * i + k - RING, k, RING // 2 * i + (k - RING) // 2, i)
            for t in range(TILES - RING, TILES + 2):
                step(t, t, t // 2, t // RING)

        def live(k, behind):
            return 0 <= k - behind < TILES

        @block.sync
        def _(sp):
            for e in range(EXPERTS):
                sp.dma_start(w1[:, e], a["w1"][e].rearrange("(k p) h -> p k h", p=P)).then_inc(w_loaded, 16)
                sp.dma_start(w2[:, e], a["w2"][e].rearrange("(k p) c -> p k c", p=P)).then_inc(w_loaded, 16)
            sp.dma_start(b2[:].rearrange("p e c -> p (e c)"), a["b2"].partition_broadcast(P)).then_inc(w_loaded, 16)

            def step(t, k, half, rnd):
                if live(k, 0):
                    if k >= RING:
                        sp.wait_ge(result_done, t - RING + 1)
                    first = sp.value_load(tile_row[0:1, bass.ds(t, 1)], min_val=0, max_val=SPARE)
                    sp.dma_start(rows[:, k % RING, :], rows_dram[bass.ds(first, P), :]).then_inc(loaded[k % RING], 16)
            over_steps(sp, step)

        @block.gpsimd
        def _(pool):
            nc.gpsimd.memset(z[:, :, C:2 * P], 1.0).then_inc(ones_done, 1)

            def step(t, k, half, rnd):
                if live(k, 2):
                    pool.wait_ge(result_done, t - 1)
                    pool.wait_ge(token_done, t - 1)
                    settled(pool, waited_pool)
                    nc.gpsimd.indirect_dma_start(
                        out=a["out"], out_offset=bass.IndirectOffsetOnAxis(ap=token[:, (k - 2) % RING, :], axis=0),
                        in_=result[:, k % 2, :], in_offset=None, bounds_check=ALL - 1, oob_is_err=False)\
                        .then_inc(stored[k % 2], 16)
            over_steps(pool, step)
            for b in range(2):
                pool.wait_ge(stored[b], 16 * TILES // 2)

        @block.vector
        def _(dve):
            dve.wait_ge(w_loaded, 16 * (2 * EXPERTS + 1))
            dve.wait_ge(ones_done, 1)

            def normalise(t, k, half, rnd):
                slot = k % RING
                dve.wait_ge(loaded[slot], 16 * (rnd + 1))
                at_least(dve, zT_done, t - 1)
                row = rows[:, slot, :]
                nc.vector.tensor_scalar(z[:, k % 2, 0:C], row[:, 0:C], row[:, MEAN:MEAN + 1], row[:, RSTD:RSTD + 1],
                                        ALU.subtract, ALU.mult).then_inc(z_done, 1)
                at_least(dve, stored[k % 2], 16 * (half - RING // 2 + 1))
                nc.vector.tensor_copy(token[:, slot, :], row[:, TOKEN:ROW]).then_inc(token_done, 1)

            def take_turned(t, b, part):
                dve.wait_ge(hT_done, 2 * t + part + 1)
                at_least(dve, y_done, t - 1)
                nc.vector.tensor_copy(hidT[:, b, 3 * part:3 * part + 3, :].rearrange("p k t -> p (k t)"),
                                      p_hT[part][:, 0:HH]).then_inc(hT_taken, 1)

            def finish(t, k, half):
                dve.wait_ge(y_done, t + 1)
                expert = dve.value_load(tile_expert[0:1, bass.ds(t, 1)], min_val=0, max_val=EXPERTS - 1)
                nc.vector.tensor_tensor(y[:, k % 2], p_y[k % 2][:, 0:C], b2[:, bass.ds(expert, 1), :]
                                        .rearrange("p e c -> p (e c)"), ALU.add).then_inc(biased, 1)
                dve.wait_ge(biased, t + 1)
                at_least(dve, stored[k % 2], 16 * half)
                nc.vector.tensor_tensor(result[:, k % 2], y[:, k % 2], rows[:, k % RING, 0:C], ALU.add).then_inc(result_done, 1)

            def step(t, k, half, rnd):
                if k == 0:
                    normalise(t, k, half, rnd)
                if live(k, -1):
                    normalise(t + 1, k + 1, half + (k + 1) // 2 - k // 2, rnd + (k + 1) // RING - k // RING)
                if live(k, 1):
                    for part in range(2):
                        take_turned(t - 1, (k - 1) % 2, part)
                if live(k, 2):
                    finish(t - 2, k - 2, half - 1)
            over_steps(dve, step)

        @block.scalar
        def _(act):
            def take_z(t, b):
                act.wait_ge(zT_done, t + 1)
                at_least(act, h_done, 2 * t - 2)
                nc.scalar.copy(zT[:, b], p_z[:]).then_inc(zT_taken, 1)

            def step(t, k, half, rnd):
                if k == 0:
                    take_z(t, 0)
                if live(k, 0):
                    for part in range(2):
                        act.wait_ge(h_done, 2 * t + part + 1)
                        at_least(act, hT_done, 2 * t - 2)
                        nc.scalar.activation(hid[:, k % 2, HH * part:HH * (part + 1)], p_h[part][:, 0:HH],
                                             ACT.Gelu).then_inc(gelu_done, 1)
                        if part == 0 and live(k, -1):
                            take_z(t + 1, (k + 1) % 2)
            over_steps(act, step)

        @block.tensor
        def _(pe):
            pe.wait_ge(w_loaded, 16 * (2 * EXPERTS + 1))

            def turn_z(t, b):
                pe.wait_ge(z_done, t + 1)
                at_least(pe, zT_taken, t)
                for c in range(2):
                    last = nc.tensor.transpose(p_z[:, c, :], z[:, b, P * c:P * (c + 1)], ident[:])
                last.then_inc(zT_done, 1)

            def first_layer(t, b, part, expert):
                pe.wait_ge(zT_taken, t + 1)
                at_least(pe, gelu_done, 2 * t + part - 1)
                for c in range(2):
                    last = nc.tensor.matmul(p_h[part][:, 0:HH], zT[:, b, c, :],
                                            w1[:, bass.ds(expert, 1), c, HH * part:HH * (part + 1)]
                                            .rearrange("p e h -> p (e h)"), start=(c == 0), stop=(c == 1))
                last.then_inc(h_done, 1)

            def turn_hidden(t, b, part):
                pe.wait_ge(gelu_done, 2 * t + part + 1)
                at_least(pe, hT_taken, 2 * t + part - 1)
                for m in range(3):
                    at = HH * part + P * m
                    last = nc.tensor.transpose(p_hT[part][:, P * m:P * (m + 1)], hid[:, b, at:at + P], ident[:])
                last.then_inc(hT_done, 1)

            def second_layer(t, b, expert):
                at_least(pe, result_done, t - 1)
                for m in range(KH):
                    if m % 3 == 0:
                        pe.wait_ge(hT_taken, 2 * t + m // 3 + 1)
                    last = nc.tensor.matmul(p_y[b][:, 0:C], hidT[:, b, m, :],
                                            w2[:, bass.ds(expert, 1), m, :].rearrange("p e c -> p (e c)"),
                                            start=(m == 0), stop=(m == KH - 1))
                last.then_inc(y_done, 1)

            def step(t, k, half, rnd):
                if k == 0:
                    turn_z(t, 0)
                if live(k, -1):
                    turn_z(t + 1, (k + 1) % 2)
                if live(k, 0):
                    expert = pe.value_load(tile_expert[0:1, bass.ds(t, 1)], min_val=0, max_val=EXPERTS - 1)
                    first_layer(t, k % 2, 0, expert)
                if live(k, 1):
                    for part in range(2):
                        turn_hidden(t - 1, (k - 1) % 2, part)
                if live(k, 0):
                    first_layer(t, k % 2, 1, expert)
                if live(k, 1):
                    last_expert = pe.value_load(tile_expert[0:1, bass.ds(t - 1, 1)], min_val=0, max_val=EXPERTS - 1)
                    second_layer(t - 1, (k - 1) % 2, last_expert)
            over_steps(pe, step)


def kernel(x, L0_tok_W, L0_tok_b, L0_attn_qkv_weight, L0_attn_qkv_bias, L0_attn_proj_weight, L0_attn_proj_bias,
           L0_ffn_gate_w, L0_ffn_gate_b, L0_ffn_gate_center, L0_ffn_w1, L0_ffn_b1, L0_ffn_w2, L0_ffn_b2):
    import numpy as np
    from concourse import bacc
    from concourse.bass_utils import run_bass_kernel_spmd

    x = np.asarray(x).reshape(IMAGES, CHANNELS, GRID, PATCH, GRID, PATCH)
    patches = np.ascontiguousarray(x.transpose(1, 3, 5, 0, 2, 4).reshape(D_IN, ALL))

    def with_bias(w, b):
        out = np.zeros((2 * P, w.shape[1]), np.float32)
        out[:C] = w
        out[C] = b
        return out

    def by_dim(first, heads):
        return [first + h * HD + d for d in range(HD) for h in heads]

    order = (by_dim(0, range(8)) + by_dim(C, range(8)) + by_dim(0, range(8, 12)) + by_dim(C, range(8, 12))
             + list(range(2 * C, 3 * C)))
    qkv_w = with_bias(np.asarray(L0_attn_qkv_weight).T[:, order], np.asarray(L0_attn_qkv_bias)[order])
    proj_w = np.zeros((HEADS, 2 * HD, C), np.float32)
    proj_w[:, :HD] = np.asarray(L0_attn_proj_weight).T.reshape(HEADS, HD, C)
    proj_w[0, HD] = np.asarray(L0_attn_proj_bias)
    w1 = np.stack([with_bias(w, b) for w, b in zip(np.asarray(L0_ffn_w1), np.asarray(L0_ffn_b1))])
    gate_w = np.zeros((2 * P, EXPERTS), np.float32)
    gate_w[:C] = np.asarray(L0_ffn_gate_w)
    arrays = {
        "patches": patches,
        "tok_w": np.ascontiguousarray(np.asarray(L0_tok_W).T),
        "tok_b": np.asarray(L0_tok_b),
        "qkv_w": qkv_w,
        "proj_w": proj_w.reshape(3 * P, C),
        "gate_w": gate_w,
        "gate_b": np.asarray(L0_ffn_gate_b),
        "gate_c": np.asarray(L0_ffn_gate_center),
        "w1": w1,
        "w2": np.asarray(L0_ffn_w2),
        "b2": np.asarray(L0_ffn_b2).reshape(-1),
    }
    nc = bacc.Bacc("TRN2", target_bir_lowering=False, num_devices=1)
    a = {n: nc.dram_tensor("in_" + n, v.shape, F32, kind="ExternalInput").ap() for n, v in arrays.items()}
    a["out"] = nc.dram_tensor("out", [ALL, C], F32, kind="ExternalOutput").ap()
    vit_block(nc, a)
    r = run_bass_kernel_spmd(nc, [{"in_" + n: v for n, v in arrays.items()}], core_ids=[0])
    return r.results[0]["out"].reshape(IMAGES, TOK, C)
```

```python
from contextlib import ExitStack
from math import prod

import concourse.bass as bass
from concourse import mybir

F32 = mybir.dt.float32
BF16 = mybir.dt.bfloat16
I32 = mybir.dt.int32
F32R = mybir.dt.float32r
ALU = mybir.AluOpType
ACT = mybir.ActivationFunctionType
AX = mybir.AxisListType

P = 128
IMAGES, CHANNELS, SIDE = 64, 3, 224
GRID = 14
PATCH = SIDE // GRID
TOK = GRID * GRID
ALL = IMAGES * TOK
D_IN = CHANNELS * PATCH * PATCH
C = 192
HEADS, HD = 12, 16
HID, EXPERTS = 768, 4
KIN = D_IN // P
KH = HID // P
EPS = 1e-5

NT = ALL // P
GT = 7
GROUP = GT * P
GROUPS = NT // GT
LAG = 3

HALF = TOK // 2
UNITS = 12
TLAG = 6
SPLIT_ROWS = 6 * HD
Q_PARTS = (0, 0, 0, 1, 1, 2)
K_PARTS = (0, 1, 2, 0, 1, 0)
SCALE = float(HD) ** -0.5
STACK = 16 * 12
PROB_SLOTS = 4
FIRST_SLOTS = 6
ROUNDS = (IMAGES - FIRST_SLOTS) // 4

ROW = C + 4
MEAN, VAR, RSTD, TOKEN = C, C + 1, C + 2, C + 3
REGION = ALL + P
SPARE = EXPERTS * REGION
TILES = (ALL + EXPERTS * (P - 1)) // P
RAW_LOADS = 16 * (2 * EXPERTS + 1)
PRODUCTS = ((0, 0), (0, 1), (2, 0), (1, 2), (3, 3))
RING = 6
TILES = -(-TILES // RING) * RING


def settled(eng, passed):
    eng.sem_inc(passed, 1)


def at_least(eng, semaphore, value):
    if not isinstance(value, int) or value > 0:
        eng.wait_ge(semaphore, value)


def at_least(eng, semaphore, value):
    if not isinstance(value, int) or value > 0:
        eng.wait_ge(semaphore, value)


def at_least(eng, semaphore, value):
    if not isinstance(value, int) or value > 0:
        eng.wait_ge(semaphore, value)


def at_least(eng, semaphore, value):
    if not isinstance(value, int) or value > 0:
        eng.wait_ge(semaphore, value)


def at_least(eng, semaphore, value):
    if not isinstance(value, int) or value > 0:
        eng.wait_ge(semaphore, value)


def at_least(eng, semaphore, value):
    if not isinstance(value, int) or value > 0:
        eng.wait_ge(semaphore, value)


def at_least(eng, semaphore, value):
    if not isinstance(value, int) or value > 0:
        eng.wait_ge(semaphore, value)


def at_least(eng, semaphore, value):
    if not isinstance(value, int) or value > 0:
        eng.wait_ge(semaphore, value)


def at_least(eng, semaphore, value):
    if not isinstance(value, int) or value > 0:
        eng.wait_ge(semaphore, value)


def at_least(eng, semaphore, value):
    if not isinstance(value, int) or value > 0:
        eng.wait_ge(semaphore, value)


def at_least(eng, semaphore, value):
    if not isinstance(value, int) or value > 0:
        eng.wait_ge(semaphore, value)


def at_least(eng, semaphore, value):
    if not isinstance(value, int) or value > 0:
        eng.wait_ge(semaphore, value)


def at_least(eng, semaphore, value):
    if not isinstance(value, int) or value > 0:
        eng.wait_ge(semaphore, value)


def at_least(eng, semaphore, value):
    if not isinstance(value, int) or value > 0:
        eng.wait_ge(semaphore, value)


def at_least(eng, semaphore, value):
    if not isinstance(value, int) or value > 0:
        eng.wait_ge(semaphore, value)


def at_least(eng, semaphore, value):
    if not isinstance(value, int) or value > 0:
        eng.wait_ge(semaphore, value)


def at_least(eng, semaphore, value):
    if not isinstance(value, int) or value > 0:
        eng.wait_ge(semaphore, value)


def at_least(eng, semaphore, value):
    if not isinstance(value, int) or value > 0:
        eng.wait_ge(semaphore, value)


def at_least(eng, semaphore, value):
    if not isinstance(value, int) or value > 0:
        eng.wait_ge(semaphore, value)


def at_least(eng, semaphore, value):
    if not isinstance(value, int) or value > 0:
        eng.wait_ge(semaphore, value)


def at_least(eng, semaphore, value):
    if not isinstance(value, int) or value > 0:
        eng.wait_ge(semaphore, value)


def at_least(eng, semaphore, value):
    if not isinstance(value, int) or value > 0:
        eng.wait_ge(semaphore, value)


def at_least(eng, semaphore, value):
    if not isinstance(value, int) or value > 0:
        eng.wait_ge(semaphore, value)


def at_least(eng, semaphore, value):
    if not isinstance(value, int) or value > 0:
        eng.wait_ge(semaphore, value)


def at_least(eng, semaphore, value):
    if not isinstance(value, int) or value > 0:
        eng.wait_ge(semaphore, value)


def at_least(eng, semaphore, value):
    if not isinstance(value, int) or value > 0:
        eng.wait_ge(semaphore, value)


def at_least(eng, semaphore, value):
    if not isinstance(value, int) or value > 0:
        eng.wait_ge(semaphore, value)


def at_least(eng, semaphore, value):
    if not isinstance(value, int) or value > 0:
        eng.wait_ge(semaphore, value)


def at_least(eng, semaphore, value):
    if not isinstance(value, int) or value > 0:
        eng.wait_ge(semaphore, value)


def at_least(eng, semaphore, value):
    if not isinstance(value, int) or value > 0:
        eng.wait_ge(semaphore, value)


def at_least(eng, semaphore, value):
    if not isinstance(value, int) or value > 0:
        eng.wait_ge(semaphore, value)


def at_least(eng, semaphore, value):
    if not isinstance(value, int) or value > 0:
        eng.wait_ge(semaphore, value)


def at_least(eng, semaphore, value):
    if not isinstance(value, int) or value > 0:
        eng.wait_ge(semaphore, value)


def at_least(eng, semaphore, value):
    if not isinstance(value, int) or value > 0:
        eng.wait_ge(semaphore, value)


def at_least(eng, semaphore, value):
    if not isinstance(value, int) or value > 0:
        eng.wait_ge(semaphore, value)


def vit_block(nc, a):
    with ExitStack() as ctx:
        def sb(stack, name, shape, dt=F32):
            return stack.enter_context(nc.sbuf_tensor(name, shape, dt))

        def ps(stack, name, shape, dt=F32):
            return stack.enter_context(nc.psum_tensor(name, shape, dt))

        def sem(name):
            return ctx.enter_context(nc.semaphore(name))

        h_dram = nc.dram_tensor("h_tokens", [ALL, C], F32, kind="Internal").ap()
        rows_dram = nc.dram_tensor("rows_by_expert", [SPARE + P, ROW], F32, kind="Internal").ap()

        ident = sb(ctx, "ident", [P, P])
        tile_expert = sb(ctx, "tile_expert", [P, TILES], I32)
        tile_row = sb(ctx, "tile_row", [P, TILES], I32)
        shared = sb(ctx, "shared", [P, 2 * ALL])
        raw_loaded = sem("raw_loaded")
        with ExitStack() as st:
            wqkv = sb(st, "wqkv", [P, 4, 3 * C], F32R)
            smooth = sb(st, "smooth", [P, 8, 3])
            wproj = sb(st, "wproj", [P, 2, C])
            gate_w = sb(st, "gate_w", [P, 2, EXPERTS])
            gate_b = sb(st, "gate_b", [P, EXPERTS])
            gate_c = sb(st, "gate_c", [P, EXPERTS])
            xT = shared[:].rearrange("p (k t) -> p k t", k=2)
            absmax = sb(st, "absmax", [P, GROUPS, 2])
            phase_a(nc, a, sb, ps, sem, wqkv, smooth, wproj, gate_w, gate_b, gate_c, xT, ident, absmax, h_dram)
            phase_b(nc, a, sb, ps, sem, shared, raw_loaded, wqkv, smooth, wproj, gate_w, gate_b, gate_c, xT, ident,
                    absmax, h_dram, rows_dram, tile_expert, tile_row)
        phase_c(nc, a, sb, ps, sem, shared, raw_loaded, ident, rows_dram, tile_expert, tile_row)


def phase_a(nc, a, sb, ps, sem, wqkv, smooth, wproj, gate_w, gate_b, gate_c, xT, ident, absmax, h_dram):
    with ExitStack() as st:
        patches = sb(st, "patches", [P, 2, KIN, GROUP])
        wt = sb(st, "wt", [P, KIN, C])
        bias = sb(st, "bias_tok", [P, C])
        wqkv_raw = sb(st, "wqkv_raw", [P, 3, 3 * C])
        h = sb(st, "h_a", [P, 2, GT, C])
        stats = sb(st, "stats_a", [P, 4, 6])
        mv = sb(st, "mv_a", [P, 4, 2])
        rstd = sb(st, "rstd_a", [P, 4, 1])
        vare = sb(st, "vare_a", [P, 4, 1])
        expo = sb(st, "expo_a", [P, 1])
        x = sb(st, "x_a", [P, 4, 2 * P])
        p_h = [ps(st, f"p_h{i}", [P, C]) for i in range(2)]
        p_x = [ps(st, f"p_x{i}", [P, 2, P]) for i in range(2)]

        loaded_w = sem("a_loaded_w")
        attn_loaded, attn_high, attn_low = sem("a_attn_loaded"), sem("a_attn_high"), sem("a_attn_low")
        loaded = [sem(f"a_loaded{i}") for i in range(2)]
        const0, const = sem("a_const0"), sem("a_const")
        embedded, h_done, stats_done, mv_done, rstd_done, x_done = (
            sem("a_" + n) for n in ("embedded", "h_done", "stats_done", "mv_done", "rstd_done", "x_done"))
        turned, xT_done, max_done = sem("a_turned"), sem("a_xT_done"), sem("a_max_done")
        stored = [sem(f"a_stored{i}") for i in range(2)]

        waited_dve, waited_pool, vare_done = sem("a_waited_dve"), sem("a_waited_pool"), sem("a_vare_done")
        block = st.enter_context(nc.Block())
        patches_in = a["patches"].rearrange("(k p) t -> p k t", p=P)
        h_out = h_dram.rearrange("(n p) c -> p n c", p=P)

        def over_pairs(eng, body):
            body(0, True)
            with eng.Fori(1, GROUPS // 2) as i:
                body(i, False)

        @block.sync
        def _(sp):
            sp.dma_start(bias[:], a["tok_b"].partition_broadcast(P)).then_inc(loaded_w, 16)
            sp.dma_start(wt[:], a["tok_w"].rearrange("(k p) c -> p k c", p=P)).then_inc(loaded_w, 16)

            def body(i, first):
                for g in range(2):
                    if not first:
                        sp.wait_ge(embedded, (2 * i + g - 1) * GT)
                    for part in range(2):
                        ks = slice(3 * part, 3 * part + 3)
                        sp.dma_start(patches[:, g, ks, :],
                                     patches_in[:, ks, bass.ds((2 * i + g) * GROUP, GROUP)]).then_inc(loaded[g], 16)
                if first:
                    sp.dma_start(wqkv_raw[:], a["qkv_w"].rearrange("(k p) c -> p k c", p=P)).then_inc(attn_loaded, 16)
                    sp.dma_start(wproj[:], a["proj_w"].rearrange("(k p) c -> p k c", p=P)).then_inc(attn_loaded, 16)
                    sp.dma_start(gate_w[:], a["gate_w"].rearrange("(k p) e -> p k e", p=P)).then_inc(attn_loaded, 16)
                    for dst, name in ((gate_b, "gate_b"), (gate_c, "gate_c")):
                        sp.dma_start(dst[:], a[name].partition_broadcast(P)).then_inc(attn_loaded, 16)
            over_pairs(sp, body)

        @block.gpsimd
        def _(pool):
            nc.gpsimd.memset(ident[:], 0.0).then_inc(const0, 1)
            pool.wait_ge(const0, 1)
            nc.gpsimd.affine_select(out=ident[:], in_=ident[:], compare_op=ALU.not_equal, fill=1.0,
                                    base=0, pattern=[[-1, P]], channel_multiplier=1).then_inc(const, 1)
            nc.gpsimd.memset(expo[:], -0.5).then_inc(const, 1)
            pool.wait_ge(const, 2)

            def body(i, first):
                for t in range(2 * GT):
                    pool.wait_ge(mv_done, 2 * GT * i + t + 1)
                    settled(pool, waited_pool)
                    nc.gpsimd.tensor_scalar(vare[:, t % 2], mv[:, t % 2, 1:2], EPS, None, ALU.add).then_inc(vare_done, 1)
                    pool.wait_ge(vare_done, 2 * GT * i + t + 1)
                    nc.gpsimd.tensor_tensor(rstd[:, t % 2], vare[:, t % 2], expo[:], ALU.pow).then_inc(rstd_done, 1)
                    if t % GT == GT - 1:
                        g = t // GT
                        pool.wait_ge(h_done, (2 * i + g + 1) * GT)
                        pool.dma_start(h_out[:, bass.ds((2 * i + g) * GT, GT), :], h[:, g]).then_inc(stored[g], 16)
            over_pairs(pool, body)
            for g in range(2):
                pool.wait_ge(stored[g], 16 * (GROUPS // 2))

        @block.tensor
        def _(pe):
            pe.wait_ge(loaded_w, 32)
            pe.wait_ge(const, 1)

            def turn(n, slot):
                pe.wait_ge(x_done, 2 * n + 2)
                for c in range(2):
                    last = nc.tensor.transpose(p_x[slot % 2][:, c, :], x[:, slot % 4, c * P:(c + 1) * P], ident[:])
                last.then_inc(turned, 1)

            def body(i, first):
                for t in range(2 * GT):
                    n = 2 * GT * i + t
                    if t % GT == 0:
                        pe.wait_ge(loaded[t // GT], 32 * (i + 1))
                    if not first or t >= 2:
                        pe.wait_ge(h_done, n - 1)
                    for k in range(KIN):
                        last = nc.tensor.matmul(p_h[t % 2][:], patches[:, t // GT, k, (t % GT) * P:(t % GT + 1) * P],
                                                wt[:, k, :], start=(k == 0), stop=(k == KIN - 1))
                    last.then_inc(embedded, 1)
                    if not first or t >= LAG:
                        if not first or t >= LAG + 2:
                            pe.wait_ge(xT_done, n - LAG - 1)
                        turn(n - LAG, (t - LAG) % 2)
            over_pairs(pe, body)
            for k in range(LAG):
                n = NT - LAG + k
                pe.wait_ge(xT_done, n - 1)
                turn(n, n % 2)

        @block.vector
        def _(dve):
            dve.wait_ge(loaded_w, 32)

            def aggregate(n, s):
                dve.wait_ge(stats_done, n + 1)
                settled(dve, waited_dve)
                nc.vector.bn_aggr(mv[:, s], stats[:, s]).then_inc(mv_done, 1)

            def normalise(n, s, t, free):
                dve.wait_ge(rstd_done, n + 1)
                if free:
                    dve.wait_ge(turned, n - 1)
                g, k = (t // GT) % 2, t % GT
                for into, features in ((slice(0, C), slice(0, C)), (slice(C, 2 * P), slice(P, C))):
                    nc.vector.tensor_scalar(x[:, s, into], h[:, g, k, features], mv[:, s, 0:1], rstd[:, s],
                                            ALU.subtract, ALU.mult).then_inc(x_done, 1)

            def largest(g):
                dve.wait_ge(xT_done, (g + 1) * GT)
                nc.vector.tensor_reduce(absmax[:, bass.ds(g, 1), :].rearrange("p g c -> p (g c)"),
                                        xT[:, :, bass.ds(g * GROUP, GROUP)], AX.X, ALU.max,
                                        apply_absolute_value=True).then_inc(max_done, 1)

            def body(i, first):
                for t in range(2 * GT):
                    n = 2 * GT * i + t
                    s = t % 2
                    dve.wait_ge(embedded, n + 1)
                    if not first and t % GT == 0:
                        dve.wait_ge(stored[t // GT], 16 * i)
                    nc.vector.tensor_tensor(h[:, t // GT, t % GT], p_h[t % 2][:], bias[:], ALU.add).then_inc(h_done, 1)
                    if not first or t >= 1:
                        aggregate(n - 1, 1 - s)
                    if not first or t >= 2:
                        normalise(n - 2, s, (t - 2) % (2 * GT), not first or t >= 4)
                    dve.wait_ge(h_done, n + 1)
                    nc.vector.bn_stats(stats[:, s], h[:, t // GT, t % GT]).then_inc(stats_done, 1)
                    if not first and t == 6:
                        largest(2 * i - 1)
                    if t == 13:
                        largest(2 * i)
                    if first and t == 6:
                        dve.wait_ge(attn_loaded, 80)
                        nc.vector.tensor_reduce(smooth[:, 1, 0:2], wqkv_raw[:, 0:2], AX.X, ALU.max,
                                                apply_absolute_value=True).then_inc(attn_low, 1)
                        dve.wait_ge(attn_high, 3)
                        nc.vector.tensor_tensor(wqkv[:, 1], wqkv_raw[:, 0], wqkv[:, 0], ALU.subtract).then_inc(attn_low, 1)
                        nc.vector.tensor_tensor(wqkv[0:96, 3], wqkv_raw[0:96, 2], wqkv[0:96, 3], ALU.subtract)\
                            .then_inc(attn_low, 1)
            over_pairs(dve, body)
            s = (NT - 1) % 2
            aggregate(NT - 1, s)
            normalise(NT - 2, 1 - s, 2 * GT - 2, True)
            normalise(NT - 1, s, 2 * GT - 1, True)
            largest(GROUPS - 1)
            dve.wait_ge(max_done, GROUPS)
            dve.wait_ge(attn_low, 3)

        @block.scalar
        def _(act):
            def take(n, slot):
                act.wait_ge(turned, n + 1)
                nc.scalar.copy(xT[:, :, bass.ds(n * P, P)], p_x[slot][:]).then_inc(xT_done, 1)

            act.wait_ge(attn_loaded, 80)
            for into, chunk in ((0, 0), (2, 1), (3, 2)):
                nc.scalar.copy(wqkv[:, into], wqkv_raw[:, chunk]).then_inc(attn_high, 1)

            def body(i, first):
                for t in range(2 * GT):
                    if not first or t >= LAG:
                        take(2 * GT * i + t - LAG, (t - LAG) % 2)
            over_pairs(act, body)
            for n in range(NT - LAG, NT):
                take(n, n % 2)
            act.wait_ge(xT_done, NT)


def phase_b(nc, a, sb, ps, sem, shared, raw_loaded, wqkv, smooth, wproj, gate_w, gate_b, gate_c, xT, ident, absmax,
            h_dram, rows_dram, tile_expert, tile_row):
    with ExitStack() as st:
        identb = sb(st, "identb", [P, P], BF16)
        xs = sb(st, "x_smoothed", [P, 2, 4, 2 * TOK], F32R)
        rest = sb(st, "rest", [P, 2, 2 * TOK])
        part = sb(st, "part", [P, 3, 3, 2 * TOK], BF16)
        qs = sb(st, "q_stack", [P, 2, HEADS, 2 * TOK], BF16)
        ks = sb(st, "k_stack", [P, 2, HEADS, 2 * TOK], BF16)
        vs = sb(st, "values", [P, 2, 2, HEADS, 2 * HD])
        probs = sb(st, "probs", [P, PROB_SLOTS, 2 * TOK])
        mx = sb(st, "mx", [P, 2, 2, HEADS])
        negm = sb(st, "negm", [P, 2, 2, HEADS], BF16)
        negmT = sb(st, "negmT", [2 * HEADS, TOK], BF16)
        o_raw = sb(st, "o_raw", [P, 3, TOK])
        recip = sb(st, "recip", [P, 2, HEADS])
        o = sb(st, "o_norm", [P, 2, 2 * P])
        oT = sb(st, "oT", [P, 2, TOK])
        hb = sb(st, "h_b", [P, 4, 2, C])
        rows = sb(st, "rows_b", [P, 2, 2, ROW])
        stats = sb(st, "stats_b", [P, 2, 6])
        vare = sb(st, "vare_b", [P, 2])
        expo = sb(st, "expo_b", [P, 3, 2])
        z = sb(st, "z_b", [P, 2, 2 * P])
        zT = sb(st, "zT_b", [P, 2, TOK])
        before = sb(st, "before", [P, P], BF16)
        ones = sb(st, "ones", [P, P], BF16)
        pick = sb(st, "pick", [P, 4, HD + 1])
        prefer = sb(st, "prefer", [P, EXPERTS])
        region = sb(st, "region", [P, EXPERTS])
        lane = sb(st, "lane", [P, 1])
        count_i = sb(st, "count_i", [P, TILES], I32)
        token_i = sb(st, "token_i", [P, 2, 2], I32)
        padding = sb(st, "padding", [P, ROW])
        score = sb(st, "score", [P, 2, EXPERTS])
        best = sb(st, "best", [P, 2])
        liked = sb(st, "liked", [P, 2, EXPERTS])
        likedest = sb(st, "likedest", [P, 2])
        chosen = sb(st, "chosen", [P, 2, EXPERTS], BF16)
        place = sb(st, "place", [P, 2, EXPERTS])
        where_f = sb(st, "where_f", [P, 2])
        where_i = sb(st, "where_i", [P, 2, 2], I32)
        base = sb(st, "base", [P, EXPERTS])
        pad_i = sb(st, "pad_i", [P, EXPERTS], I32)
        table = sb(st, "table", [P, 4, TILES])
        few = sb(st, "few", [P, 5, EXPERTS])
        few_i = sb(st, "few_i", [P, 2, EXPERTS], I32)

        p_s = [ps(st, f"p_s{i}", [P, 512]) for i in range(2)]
        p_t = [ps(st, f"p_t{i}", [P, 512]) for i in range(2)]
        p_o = [ps(st, f"p_o{i}", [P, 512]) for i in range(2)]
        p_qkv = ps(st, "p_qkv", [P, 512])
        p_misc = ps(st, "p_misc", [P, 512])
        p_zT = p_misc[:, 0:2 * TOK]
        p_picked = p_misc[0:HALF, 0:2 * HEADS * (HD + 1)].rearrange("p (t h d) -> p t h d", t=2, h=HEADS)
        p_gate = p_misc[0:HALF, 416:416 + 2 * EXPERTS]
        p_oT = p_misc[:, 0:2 * TOK]
        p_proj, p_place = p_misc[0:HALF, 0:2 * C], p_misc[0:HALF, 400:400 + 2 * EXPERTS]
        p_total = p_misc[:, 400 + 2 * EXPERTS:400 + 3 * EXPERTS]
        p_negmT = p_o[1][0:2 * HEADS, 200:200 + HALF].bitcast(BF16)

        const, smoothed, x_high, x_low, x_ones, step, powers = (
            sem("b_" + n) for n in ("const", "smoothed", "x_high", "x_low", "x_ones", "step", "powers"))
        h_loaded = [sem(f"b_h_loaded{i}") for i in range(4)]
        s_done, max_done, t_done, exp_done = (sem("b_" + n) for n in ("scores", "max", "scoresT", "exp"))
        pv_done, o_taken, picked, recip_done, norm_done, oT_done, oT_taken = (
            sem("b_" + n) for n in ("pv", "o_taken", "picked", "recip", "norm", "oT", "oT_taken"))
        negm1_done, negm_done, negmT_done, negmT_taken, negm_placed = (
            sem("b_" + n) for n in ("negm1", "negm", "negmT", "negmT_taken", "negm_placed"))
        qk_done, first_done, rest_done, second_done, third_done = (
            sem("b_" + n) for n in ("qk", "part1", "rest", "part2", "part3"))
        v_done, v_taken, stacked = sem("b_v"), sem("b_v_taken"), [sem(f"b_stacked{i}") for i in range(2)]
        proj_done, h2_done, stats_done, mv_done, vare_done, rstd_done, z_done, zT_done, zT_taken = (
            sem("b_" + n) for n in ("proj", "h2", "stats", "mv", "vare", "rstd", "z", "zT", "zT_taken"))
        gate_done, chosen_done, ranked, placed, token_done, padded = (
            sem("b_" + n) for n in ("gate", "chosen", "ranked", "placed", "token", "padded"))
        scattered = [sem(f"b_scattered{i}") for i in range(2)]
        pad_ready, tables, waited_pool, waited_sp, waited_dve = (
            sem("b_" + n) for n in ("pad_ready", "tables", "waited_pool", "waited_sp", "waited_dve"))
        block = st.enter_context(nc.Block())

        FILLS = 20
        MAXIMA_STEPS = 1
        CHOOSE, PLACE = 6, 5
        HALVES = [slice(HALF * t, HALF * (t + 1)) for t in range(2)]

        def over_slots(eng, slot):
            for n in range(FIRST_SLOTS):
                slot(n, n, n // 2, n // 4)
            with eng.Fori(0, ROUNDS) as i:
                for k in range(FIRST_SLOTS, FIRST_SLOTS + 4):
                    slot(4 * i + k, k, 2 * i + k // 2, i + k // 4)
            for n in range(FIRST_SLOTS + 4 * ROUNDS, IMAGES + 4):
                slot(n, n, n // 2, n // 4)

        def live(k, behind):
            return 0 <= k - behind < IMAGES

        def makes_pair(k):
            return k % 2 == 0 and k + 2 < IMAGES

        def unit(u, turned):
            if not turned:
                return u // 6, 2 * (u % 6)
            return (u // 2) % 2, 4 * (u // 4) + 2 * (u % 2)

        @block.sync
        def _(sp):
            def stack(p, b, late):
                sp.wait_ge(third_done, 3 * p + 2 + late)
                settled(sp, waited_sp)
                for r in range(6):
                    rws = slice(HD * r, HD * (r + 1))
                    for dst, parts, col, low in ((qs, Q_PARTS, 0, 0), (ks, K_PARTS, 1, 64)):
                        if late:
                            sp.dma_start(dst[rws, b, 8:12, :], part[low:low + 64, parts[r], 2, :]).then_inc(stacked[1], 16)
                        else:
                            sp.dma_start(dst[rws, b, 0:8, :], part[:, parts[r], col, :]).then_inc(stacked[0], 16)

            def slot(n, k, pair, quad):
                if k == 0:
                    for late in range(2):
                        stack(0, 0, late)
                if k == IMAGES:
                    sp.wait_ge(x_high, 3 * IMAGES // 2)
                    sp.wait_ge(x_low, IMAGES)
                    w1_raw, w2_raw, b2 = shared_by_phase_c(shared)[0:3]
                    for e in range(EXPERTS):
                        sp.dma_start(w1_raw[:, e], a["w1"][e].rearrange("(k p) h -> p k h", p=P)).then_inc(raw_loaded, 16)
                    for e in range(EXPERTS):
                        sp.dma_start(w2_raw[:, e], a["w2"][e].rearrange("(k p) c -> p k c", p=P)).then_inc(raw_loaded, 16)
                    sp.dma_start(b2.rearrange("p e c -> p (e c)"), a["b2"].partition_broadcast(P)).then_inc(raw_loaded, 16)
                if k % 2 == 1 and k < IMAGES - 1:
                    for late in range(2):
                        if k >= 3:
                            sp.wait_ge(t_done, UNITS * (n - 1) if late else UNITS * (n - 2) + 8)
                            settled(sp, waited_sp)
                        sp.wait_ge(stacked[late], STACK * (pair + 1))
                        settled(sp, waited_sp)
                        stack(pair + 1, (k // 2 + 1) % 2, late)
                if live(k, 0):
                    if k >= 4:
                        sp.wait_ge(h2_done, n - 3)
                    sp.dma_start(hb[0:HALF, k % 4], h_dram[bass.ds(n * TOK, TOK), :]
                                 .rearrange("(t p) c -> p t c", p=HALF)).then_inc(h_loaded[k % 4], 16)
            over_slots(sp, slot)

        @block.gpsimd
        def _(pool):
            filled = [0]

            def alone(ins):
                filled[0] += 1
                ins.then_inc(const, 1)
                pool.wait_ge(const, filled[0])

            for i, power in enumerate((-0.5, 0.35, -0.65)):
                alone(nc.gpsimd.memset(expo[:, i], power))
            pool.wait_ge(step, MAXIMA_STEPS)
            nc.gpsimd.tensor_tensor(smooth[:, 2:4, 0:2], smooth[:, 0:2, 0:2], expo[:, 1:3], ALU.pow).then_inc(powers, 1)
            alone(nc.gpsimd.tensor_copy(identb[:], ident[:]))
            alone(nc.gpsimd.memset(z[:, :, C:2 * P], 1.0))
            alone(nc.gpsimd.memset(ones[:], 1.0))
            alone(nc.gpsimd.affine_select(out=before[:], in_=ones[:], compare_op=ALU.is_gt, fill=0.0,
                                          base=0, pattern=[[1, P]], channel_multiplier=-1))
            alone(nc.gpsimd.memset(o[:, :, C:2 * P], 1.0))
            alone(nc.gpsimd.memset(pick[:], 0.0))
            alone(nc.gpsimd.affine_select(out=pick[:], in_=pick[:], compare_op=ALU.not_equal, fill=1.0,
                                          base=0, pattern=[[-2 * HD, 4], [-1, HD + 1]], channel_multiplier=1))
            alone(nc.gpsimd.iota(count_i[:], pattern=[[1, TILES]], base=0, channel_multiplier=0))
            alone(nc.gpsimd.tensor_copy(table[:, 0], count_i[:]))
            alone(nc.gpsimd.iota(token_i[:], pattern=[[TOK, 2], [HALF, 2]], base=-2 * TOK, channel_multiplier=1))
            for b in range(2):
                alone(nc.gpsimd.tensor_copy(rows[:, b, :, TOKEN], token_i[:, b]))
            alone(nc.gpsimd.iota(token_i[:, 0, 0:1], pattern=[[0, 1]], base=0, channel_multiplier=1))

            def split(p, u, b):
                j = 3 * p + u
                pool.wait_ge(rest_done, j + 1)
                settled(pool, waited_pool)
                nc.gpsimd.tensor_scalar(part[:, 1, u, :], rest[:, b], 1.0, None, ALU.mult).then_inc(second_done, 1)
                pool.wait_ge(second_done, j + 1)
                nc.gpsimd.tensor_tensor(part[:, 2, u, :], rest[:, b], part[:, 1, u, :],
                                        ALU.subtract).then_inc(third_done, 1)

            def lay_max(m, k):
                pool.wait_ge(negmT_taken, m + 1)
                settled(pool, waited_pool)
                col = TOK * (k % 2)
                pool.dma_start(qs[96:98, (k // 2) % 2, :, col:col + TOK], negmT[:]).then_inc(negm_placed, 16)

            def deviation(m, b):
                pool.wait_ge(mv_done, 2 * m + 2)
                settled(pool, waited_pool)
                nc.gpsimd.tensor_scalar(vare[0:HALF], rows[0:HALF, b, :, VAR], EPS, None, ALU.add)\
                    .then_inc(vare_done, 1)
                pool.wait_ge(vare_done, m + 1)
                nc.gpsimd.tensor_tensor(rows[0:HALF, b, :, RSTD], vare[0:HALF], expo[0:HALF, 0], ALU.pow)\
                    .then_inc(rstd_done, 1)
                nc.gpsimd.tensor_scalar(rows[0:HALF, b, :, TOKEN], rows[0:HALF, b, :, TOKEN], 2.0 * TOK, None,
                                        ALU.add).then_inc(token_done, 1)

            def scatter(m, b):
                pool.wait_ge(placed, PLACE * (m + 1))
                pool.wait_ge(rstd_done, m + 1)
                pool.wait_ge(token_done, m + 1)
                settled(pool, waited_pool)
                for t in range(2):
                    nc.gpsimd.indirect_dma_start(
                        out=rows_dram, out_offset=bass.IndirectOffsetOnAxis(ap=where_i[0:HALF, b, t:t + 1], axis=0),
                        in_=rows[0:HALF, b, t, :], in_offset=None).then_inc(scattered[b], 16)

            for u in range(3):
                split(0, u, u % 2)
            pool.wait_ge(third_done, 3)
            alone(nc.gpsimd.memset(ks[96:98], 1.0))
            alone(nc.gpsimd.memset(vs[:], 0.0))
            alone(nc.gpsimd.memset(vs[0:HALF, :, :, :, HD:2 * HD], 1.0))
            alone(nc.gpsimd.memset(probs[96:128], 0.0))
            assert filled[0] == FILLS

            def slot(n, k, pair, quad):
                if live(k, 1):
                    lay_max(n - 1, k - 1)
                if live(k, 3):
                    deviation(n - 3, (k - 3) % 2)
                for u in range(3):
                    if makes_pair(k):
                        split(pair + 1, u, (k // 2 + 1 + u) % 2)
                    if live(k, 4) and u == 0:
                        scatter(n - 4, k % 2)
            over_slots(pool, slot)

            pool.wait_ge(pad_ready, 2)
            for e in range(EXPERTS):
                nc.gpsimd.indirect_dma_start(
                    out=rows_dram, out_offset=bass.IndirectOffsetOnAxis(ap=pad_i[:, e:e + 1], axis=0),
                    in_=padding[:], in_offset=None).then_inc(padded, 16)
            pool.dma_start(rows_dram[SPARE:SPARE + P, :], padding[:]).then_inc(padded, 16)
            for b in range(2):
                pool.wait_ge(scattered[b], 32 * IMAGES // 2)
            pool.wait_ge(padded, 16 * (EXPERTS + 1))

        @block.vector
        def _(dve):
            n_steps = [0]

            def then(ins):
                n_steps[0] += 1
                ins.then_inc(step, 1)
                dve.wait_ge(step, n_steps[0])

            gx, _, gp, wp, r, pw, cs, inv = (smooth[:, i, :] for i in range(8))
            then(nc.vector.tensor_reduce(gx[:, 0:2], absmax[:].rearrange("p g c -> p c g"), AX.X, ALU.max))
            dve.wait_ge(powers, 1)
            then(nc.vector.tensor_tensor(r[:, 0:2], gp[:, 0:2], wp[:, 0:2], ALU.mult))
            then(nc.vector.tensor_scalar(pw.bitcast(I32)[:, 0:2], r.bitcast(I32)[:, 0:2], 0x7F800000, None,
                                         ALU.bitwise_and))
            then(nc.vector.scalar_tensor_tensor(out=cs[:, 0:2], in0=pw[:, 0:2], scalar=1.5, in1=r[:, 0:2],
                                                op0=ALU.mult, op1=ALU.is_lt))
            then(nc.vector.scalar_tensor_tensor(out=cs[:, 0:2], in0=cs[:, 0:2], scalar=1.0, in1=pw[:, 0:2],
                                                op0=ALU.add, op1=ALU.mult))
            nc.vector.reciprocal(inv[:, 0:2], cs[:, 0:2]).then_inc(smoothed, 1)
            then(nc.vector.memset(cs[64:P, 2:3], 1.0))
            then(nc.vector.tensor_copy(cs[0:64, 2:3], cs[0:64, 1:2]))
            for i, c in enumerate((0, 0, 1, 2)):
                nc.vector.tensor_scalar(wqkv[:, i], wqkv[:, i], cs[:, c:c + 1], None, ALU.mult).then_inc(smoothed, 1)
            def low_x(p, b, c):
                dve.wait_ge(x_high, 3 * p + 1 + c)
                at_least(dve, v_done, 2 * p - 2)
                rws, into = ((slice(0, P), 2), (slice(64, P), 1))[c]
                nc.vector.scalar_tensor_tensor(
                    out=xs[rws, b, into], in0=xT[rws, c, bass.ds(2 * TOK * p, 2 * TOK)], scalar=inv[rws, c:c + 1],
                    in1=xs[rws, b, c], op0=ALU.mult, op1=ALU.subtract).then_inc(x_low, 1)

            def leave(p, u, b):
                j = 3 * p + u
                dve.wait_ge(first_done, j + 1)
                at_least(dve, third_done, j - 1)
                nc.vector.tensor_tensor(rest[:, b], p_qkv[:, 0:2 * TOK], part[:, 0, u, :],
                                        ALU.subtract).then_inc(rest_done, 1)

            dve.wait_ge(smoothed, 5)
            for c in range(2):
                low_x(0, 0, c)
            for u in range(3):
                leave(0, u, u % 2)
            dve.wait_ge(const, FILLS)
            then(nc.vector.tensor_tensor(gate_b[:], gate_b[:], gate_c[:], ALU.subtract))
            for e in range(EXPERTS):
                then(nc.vector.memset(prefer[:, e:e + 1], float(EXPERTS - e)))
                then(nc.vector.memset(region[:, e:e + 1], float(e * REGION)))
            then(nc.vector.tensor_copy(base[:], region[:]))
            then(nc.vector.tensor_copy(lane[:], token_i[:, 0, 0:1]))

            def biggest(n, k, u):
                half, head = unit(u, False)
                dve.wait_ge(s_done, UNITS * n + u + 1)
                nc.vector.tensor_reduce(mx[0:HALF, k % 2, half, head:head + 2],
                                        p_s[u % 2][0:HALF, 0:2 * TOK].rearrange("p (h t) -> p h t", h=2),
                                        AX.X, ALU.max).then_inc(max_done, 1)

            def negate(n, b):
                dve.wait_ge(max_done, UNITS * (n + 1))
                at_least(dve, negmT_done, n)
                nc.vector.tensor_scalar(negm[0:HALF, :, 0, :], mx[0:HALF, b], -1.0, None, ALU.mult)\
                    .then_inc(negm1_done, 1)

            def negate_rest(n, b):
                dve.wait_ge(negm1_done, n + 1)
                nc.vector.scalar_tensor_tensor(out=negm[0:HALF, :, 1, :], in0=mx[0:HALF, b], scalar=-1.0,
                                               in1=negm[0:HALF, :, 0, :], op0=ALU.mult, op1=ALU.subtract)\
                    .then_inc(negm_done, 1)

            def invert(m):
                dve.wait_ge(picked, m + 1)
                nc.vector.reciprocal(recip[0:HALF], p_picked[:, :, :, HD]).then_inc(recip_done, 1)

            def multiply(m):
                dve.wait_ge(recip_done, m + 1)
                at_least(dve, oT_done, m)
                for t in range(2):
                    nc.vector.tensor_tensor(
                        o[0:HALF, t, 0:C].rearrange("p (h d) -> p h d", d=HD), p_picked[:, t, :, 0:HD],
                        recip[0:HALF, t].rearrange("p (h o) -> p h o", o=1).broadcast_to([HALF, HEADS, HD]),
                        ALU.mult).then_inc(norm_done, 1)

            def residual(m, b, earlier, hbuf, loads):
                dve.wait_ge(proj_done, m + 1)
                dve.wait_ge(h_loaded[hbuf], loads)
                at_least(dve, scattered[b], 32 * earlier)
                nc.vector.tensor_tensor(rows[0:HALF, b, :, 0:C], p_proj
                                        .rearrange("p (t c) -> p t c", t=2), hb[0:HALF, hbuf], ALU.add).then_inc(h2_done, 1)

            def statistics(m, b):
                dve.wait_ge(h2_done, m + 1)
                for t in range(2):
                    nc.vector.bn_stats(stats[0:HALF, t], rows[0:HALF, b, t, 0:C]).then_inc(stats_done, 1)

            def aggregate(m, b):
                dve.wait_ge(stats_done, 2 * m + 2)
                settled(dve, waited_dve)
                for t in range(2):
                    nc.vector.bn_aggr(rows[0:HALF, b, t, MEAN:VAR + 1], stats[0:HALF, t]).then_inc(mv_done, 1)

            def normalise(m, b):
                dve.wait_ge(rstd_done, m + 1)
                at_least(dve, zT_done, m)
                for t in range(2):
                    nc.vector.tensor_scalar(z[0:HALF, t, 0:C], rows[0:HALF, b, t, 0:C],
                                            rows[0:HALF, b, t, MEAN:MEAN + 1], rows[0:HALF, b, t, RSTD:RSTD + 1],
                                            ALU.subtract, ALU.mult).then_inc(z_done, 1)

            def over_halves(t, n):
                return t.rearrange("p (o e) -> p o e", o=1).broadcast_to([n, 2, EXPERTS])

            def over_experts(t):
                return t.rearrange("p (t o) -> p t o", o=1).broadcast_to([HALF, 2, EXPERTS])

            H = slice(0, HALF)

            def score_experts(m, k):
                dve.wait_ge(gate_done, m + 1)
                if live(k, 2):
                    dve.wait_ge(picked, m + 2)
                nc.vector.tensor_tensor(score[H], p_gate.rearrange("p (t e) -> p t e", t=2),
                                        over_halves(gate_b[H], HALF), ALU.add).then_inc(chosen_done, 1)

            def best_score(m):
                dve.wait_ge(chosen_done, CHOOSE * m + 1)
                nc.vector.tensor_reduce(best[H], score[H], AX.X, ALU.max).then_inc(chosen_done, 1)

            def like(m):
                dve.wait_ge(chosen_done, CHOOSE * m + 2)
                nc.vector.tensor_tensor(liked[H], score[H], over_experts(best[H]), ALU.is_ge).then_inc(chosen_done, 1)

            def prefer_first(m):
                dve.wait_ge(chosen_done, CHOOSE * m + 3)
                nc.vector.tensor_tensor(liked[H], liked[H], over_halves(prefer[H], HALF), ALU.mult)\
                    .then_inc(chosen_done, 1)

            def like_most(m):
                dve.wait_ge(chosen_done, CHOOSE * m + 4)
                nc.vector.tensor_reduce(likedest[H], liked[H], AX.X, ALU.max).then_inc(chosen_done, 1)

            def choose(m):
                dve.wait_ge(chosen_done, CHOOSE * m + 5)
                at_least(dve, ranked, m)
                nc.vector.tensor_tensor(chosen[H], liked[H], over_experts(likedest[H]), ALU.is_equal)\
                    .then_inc(chosen_done, 1)

            def rows_of_experts(m, k):
                dve.wait_ge(ranked, m + 1)
                if live(k, 3):
                    dve.wait_ge(proj_done, m + 2)
                nc.vector.tensor_tensor(place[H], p_place.rearrange("p (t e) -> p t e", t=2),
                                        over_halves(base[H], HALF), ALU.add).then_inc(placed, 1)

            def next_rows(m):
                dve.wait_ge(placed, PLACE * m + 1)
                nc.vector.tensor_tensor(base[:], p_total, base[:], ALU.add).then_inc(placed, 1)

            def row_of_chosen(m, b, part):
                dve.wait_ge(placed, PLACE * m + 2 + part)
                if part == 0:
                    nc.vector.tensor_tensor(place[H], place[H], chosen[H], ALU.mult).then_inc(placed, 1)
                if part == 1:
                    nc.vector.tensor_reduce(where_f[H], place[H], AX.X, ALU.add).then_inc(placed, 1)
                if part == 2:
                    nc.vector.tensor_copy(where_i[H, b], where_f[H]).then_inc(placed, 1)

            def slot(n, k, pair, quad):
                m, b = n - 3, (k - 3) % 2
                for u in range(UNITS):
                    if live(k, 4) and u == 0:
                        choose(n - 4)
                    if live(k, 3) and u == 11:
                        best_score(m)
                    if live(k, 0):
                        biggest(n, k, u)
                    if makes_pair(k) and u in (3, 6, 9):
                        leave(pair + 1, (u - 3) // 3, (k // 2 + u // 3) % 2)
                    if makes_pair(k) and u in (0, 1):
                        low_x(pair + 1, (k // 2 + 1) % 2, u)
                    if live(k, 3) and u == 2:
                        residual(m, b, pair + (k - 3) // 2 - k // 2, (k - 3) % 4,
                                 16 * (quad + (k - 3) // 4 - k // 4 + 1))
                    if live(k, 4) and u == 2:
                        rows_of_experts(n - 4, k)
                    if live(k, 3) and u == 3:
                        statistics(m, b)
                    if live(k, 4) and u == 3:
                        next_rows(n - 4)
                    if live(k, 3) and u == 4:
                        aggregate(m, b)
                    if live(k, 4) and u in (4, 5, 6):
                        row_of_chosen(n - 4, k % 2, u - 4)
                    if live(k, 3) and u == 5:
                        normalise(m, b)
                    if live(k, 2) and u == 10:
                        invert(n - 2)
                        multiply(n - 2)
                    if live(k, 3) and u == 10:
                        score_experts(m, k)
                if live(k, 3):
                    like(m)
                if live(k, 0):
                    negate(n, k % 2)
                if live(k, 3):
                    prefer_first(m)
                if live(k, 0):
                    negate_rest(n, k % 2)
                if live(k, 3):
                    like_most(m)
            over_slots(dve, slot)

            dve.wait_ge(placed, PLACE * IMAGES)
            then(nc.vector.memset(padding[:, 0:TOKEN], 0.0))
            nc.vector.tensor_scalar(padding[:, TOKEN:ROW], lane[:], float(ALL), None, ALU.add).then_inc(pad_ready, 1)
            nc.vector.tensor_scalar(pad_i[:], base[:], lane[:], None, ALU.add).then_inc(pad_ready, 1)
            tiles_f, ends, gaps = few[:, 0], few[:, 1], few[:, 2]
            then(nc.vector.tensor_tensor(few[:, 3], base[:], region[:], ALU.subtract))
            then(nc.vector.tensor_scalar(few_i[:, 0], few[:, 3], float(P - 1), None, ALU.add))
            then(nc.vector.tensor_scalar(few_i[:, 1], few_i[:, 0], 7, None, ALU.arith_shift_right))
            then(nc.vector.tensor_copy(tiles_f, few_i[:, 1]))
            then(nc.vector.tensor_copy(ends[:, 0:1], tiles_f[:, 0:1]))
            for e in range(1, EXPERTS):
                then(nc.vector.tensor_tensor(ends[:, e:e + 1], ends[:, e - 1:e], tiles_f[:, e:e + 1], ALU.add))
            then(nc.vector.tensor_scalar(gaps, tiles_f, -float(P), float(REGION), ALU.mult, ALU.add))
            number, expert, row, past = (table[:, i] for i in range(4))
            then(nc.vector.tensor_scalar(row, number, float(P), None, ALU.mult))
            then(nc.vector.memset(expert, 0.0))
            for e in range(EXPERTS - 1):
                then(nc.vector.tensor_scalar(past, number, ends[:, e:e + 1], None, ALU.is_ge))
                then(nc.vector.tensor_tensor(expert, expert, past, ALU.add))
                then(nc.vector.scalar_tensor_tensor(out=row, in0=past, scalar=gaps[:, e:e + 1], in1=row,
                                                    op0=ALU.mult, op1=ALU.add))
            then(nc.vector.tensor_scalar(past, number, ends[:, 3:4], None, ALU.is_lt))
            then(nc.vector.scalar_tensor_tensor(out=row, in0=row, scalar=-float(SPARE), in1=past,
                                                op0=ALU.add, op1=ALU.mult))
            nc.vector.tensor_scalar(tile_row[:], row, float(SPARE), None, ALU.add).then_inc(tables, 1)
            nc.vector.tensor_copy(tile_expert[:], expert).then_inc(tables, 1)
            dve.wait_ge(tables, 2)

        @block.scalar
        def _(act):
            def first_part(p, u):
                act.wait_ge(qk_done, 3 * p + u + 1)
                if u == 0:
                    for late in range(2):
                        at_least(act, stacked[late], STACK * p)
                nc.scalar.copy(part[:, 0, u, :], p_qkv[:, 0:2 * TOK]).then_inc(first_done, 1)

            def high_x(p, b):
                at_least(act, v_done, 2 * p - 2)
                for c in range(2):
                    nc.scalar.activation(xs[:, b, c], xT[:, c, bass.ds(2 * TOK * p, 2 * TOK)], ACT.Copy,
                                         scale=smooth[:, 7, c:c + 1]).then_inc(x_high, 1)
                act.wait_ge(x_high, 3 * p + 2)
                nc.scalar.copy(xs[0:64, b, 3], xs[0:64, b, 1]).then_inc(x_high, 1)

            for b in range(2):
                for at in range(0, 2 * TOK, P):
                    end = min(at + P, 2 * TOK)
                    nc.scalar.activation(xs[64:P, b, 3, at:end], ident[64:P, 0:end - at], ACT.Copy, scale=0.0,
                                         bias=1.0).then_inc(x_ones, 1)
            act.wait_ge(smoothed, 1)
            high_x(0, 0)
            for u in range(3):
                first_part(0, u)

            def exps(n, v):
                act.wait_ge(t_done, UNITS * n + v + 1)
                nc.scalar.activation(probs[0:HALF, v % PROB_SLOTS, :], p_t[v % 2][0:HALF, 0:2 * TOK], ACT.Exp,
                                     scale=SCALE).then_inc(exp_done, 1)

            def take_max(m):
                act.wait_ge(negmT_done, m + 1)
                at_least(act, negm_placed, 16 * m)
                nc.scalar.copy(negmT[:], p_negmT).then_inc(negmT_taken, 1)

            def take_outputs(m, bank):
                act.wait_ge(pv_done, 6 * m + 4 + 2 * bank)
                at_least(act, picked, m)
                if bank == 0:
                    nc.scalar.copy(o_raw[:, 0:2].rearrange("p g t -> p (g t)"), p_o[0][:, 0:2 * TOK]).then_inc(o_taken, 1)
                else:
                    nc.scalar.copy(o_raw[:, 2], p_o[1][:, 0:TOK]).then_inc(o_taken, 1)

            def slot(n, k, pair, quad):
                for u in range(UNITS):
                    if live(k, 3) and u == 0:
                        act.wait_ge(oT_done, n - 2)
                        at_least(act, proj_done, n - 3)
                        nc.scalar.copy(oT[:].rearrange("p c t -> p (c t)"), p_oT).then_inc(oT_taken, 1)
                    if makes_pair(k) and u == 0:
                        high_x(pair + 1, (k // 2 + 1) % 2)
                    if makes_pair(k) and u in (3, 6, 9):
                        first_part(pair + 1, (u - 3) // 3)
                    if u < TLAG and live(k, 2):
                        exps(n - 2, u - TLAG + UNITS)
                    if u >= TLAG and live(k, 1):
                        exps(n - 1, u - TLAG)
                    if u == 2 and live(k, 1):
                        take_max(n - 1)
                    if live(k, 2) and u in (TLAG - 1, TLAG + 2):
                        take_outputs(n - 2, (u - TLAG + 1) // 3)
                    if live(k, 3) and u == 8:
                        act.wait_ge(zT_done, n - 2)
                        at_least(act, gate_done, n - 3)
                        nc.scalar.copy(zT[:], p_zT.rearrange("p (c t) -> p c t", c=2)).then_inc(zT_taken, 1)
                    if live(k, 1) and u == 0:
                        act.wait_ge(v_done, n)
                        at_least(act, pv_done, 6 * (n - 2))
                        nc.scalar.copy(vs[0:HALF, (k - 1) % 2, :, :, 0:HD],
                                       p_qkv[0:HALF, 0:2 * C].rearrange("p (t h d) -> p t h d", t=2, d=HD))\
                            .then_inc(v_taken, 1)
            over_slots(act, slot)

        @block.tensor
        def _(pe):
            pe.wait_ge(smoothed, 5)
            pe.wait_ge(x_ones, 8)

            def queries_keys(p, b, u):
                pe.wait_ge(x_high, 3 * p + 3)
                pe.wait_ge(x_low, 2 * p + 2)
                at_least(pe, rest_done, 3 * p + u)
                if u == 0:
                    at_least(pe, v_taken, 2 * p - 2)
                for i, (c, w) in enumerate(PRODUCTS):
                    last = nc.tensor.matmul(p_qkv[:, 0:2 * TOK], wqkv[:, w, P * u:P * (u + 1)],
                                            xs[:, b, c], start=(i == 0), stop=(i == len(PRODUCTS) - 1))
                last.then_inc(qk_done, 1)

            def values(n, k, pair):
                if makes_pair(k):
                    pe.wait_ge(rest_done, 3 * pair + 6)
                else:
                    pe.wait_ge(v_taken, n)
                at = TOK * (k % 2)
                for t in range(2):
                    for i, (c, w) in enumerate(PRODUCTS):
                        last = nc.tensor.matmul(p_qkv[0:HALF, C * t:C * (t + 1)],
                                                xs[:, (k // 2) % 2, c, at + HALF * t:at + HALF * (t + 1)],
                                                wqkv[:, w, 2 * C:3 * C], start=(i == 0), stop=(i == len(PRODUCTS) - 1))
                last.then_inc(v_done, 1)

            def scores(n, k, u, pair):
                half, head = unit(u, False)
                b, at = (k // 2) % 2, TOK * (k % 2)
                if u in (0, 4) and k % 2 == 0:
                    pe.wait_ge(stacked[u // 4], STACK * (pair + 1))
                at_least(pe, max_done, UNITS * n + u - 1)
                for i in range(2):
                    last = nc.tensor.matmul(p_s[u % 2][0:HALF, TOK * i:TOK * (i + 1)],
                                            qs[0:SPLIT_ROWS, b, head + i, at + HALF * half:at + HALF * (half + 1)],
                                            ks[0:SPLIT_ROWS, b, head + i, at:at + TOK], start=True, stop=True)
                last.then_inc(s_done, 1)

            def scores_turned(n, k, v):
                half, head = unit(v, True)
                b, at = (k // 2) % 2, TOK * (k % 2)
                if v == 0:
                    pe.wait_ge(negm_placed, 16 * (n + 1))
                at_least(pe, exp_done, UNITS * n + v - 1)
                for i in range(2):
                    last = nc.tensor.matmul(p_t[v % 2][0:HALF, TOK * i:TOK * (i + 1)],
                                            ks[0:SPLIT_ROWS + 2, b, head + i, at + HALF * half:at + HALF * (half + 1)],
                                            qs[0:SPLIT_ROWS + 2, b, head + i, at:at + TOK], start=True, stop=True)
                last.then_inc(t_done, 1)

            def outputs(m, k, s, more):
                g, half = s // 2, s % 2
                pe.wait_ge(exp_done, UNITS * m + 2 * s + 2)
                if s == 0:
                    pe.wait_ge(v_taken, m + 1)
                    at_least(pe, o_taken, 2 * m - 1)
                if s == 4:
                    at_least(pe, o_taken, 2 * m)
                    if more:
                        pe.wait_ge(negmT_taken, m + 2)
                for j in range(4):
                    last = nc.tensor.matmul(p_o[g // 2][32 * j:32 * j + 32, TOK * (g % 2):TOK * (g % 2 + 1)],
                                            vs[:, k % 2, half, 4 * g + j, :],
                                            probs[:, (2 * s + j // 2) % PROB_SLOTS, TOK * (j % 2):TOK * (j % 2 + 1)],
                                            start=(half == 0), stop=(half == 1), skip_group_check=True)
                last.then_inc(pv_done, 1)

            def turn_max(m, k):
                if live(k, 3):
                    pe.wait_ge(o_taken, 2 * m - 2)
                pe.wait_ge(negm_done, m + 1)
                at_least(pe, negmT_taken, m)
                for t in range(2):
                    last = nc.tensor.transpose(p_negmT[:, HALVES[t]],
                                               negm[0:HALF, t].rearrange("p a h -> p (a h)"), identb[0:HALF, 0:HALF])
                last.then_inc(negmT_done, 1)

            def pick_outputs(m):
                pe.wait_ge(o_taken, 2 * m + 2)
                for t in range(2):
                    for g in range(3):
                        last = nc.tensor.matmul(p_picked[:, t, 4 * g:4 * g + 4].rearrange("p h d -> p (h d)"),
                                                o_raw[:, g, HALVES[t]], pick[:].rearrange("p h d -> p (h d)"),
                                                start=True, stop=True)
                last.then_inc(picked, 1)

            def turn_outputs(m, k):
                pe.wait_ge(norm_done, 2 * m + 2)
                if live(k, 3):
                    pe.wait_ge(chosen_done, CHOOSE * (m - 1) + 1)
                for c in range(2):
                    for t in range(2):
                        last = nc.tensor.transpose(p_oT[:, TOK * c + HALF * t:TOK * c + HALF * (t + 1)],
                                                   o[0:HALF, t, P * c:P * (c + 1)], ident[0:HALF, 0:HALF])
                last.then_inc(oT_done, 1)

            def project(m):
                pe.wait_ge(oT_taken, m + 1)
                for t in range(2):
                    for c in range(2):
                        last = nc.tensor.matmul(p_proj[:, C * t:C * (t + 1)], oT[:, c, HALVES[t]],
                                                wproj[:, c, :], start=(c == 0), stop=(c == 1))
                last.then_inc(proj_done, 1)

            def turn_z(m, k):
                pe.wait_ge(z_done, 2 * m + 2)
                pe.wait_ge(h2_done, m + 1)
                if live(k, 4):
                    pe.wait_ge(placed, PLACE * (m - 1) + 2)
                for t in range(2):
                    for c in range(2):
                        last = nc.tensor.transpose(p_zT[:, TOK * c + HALF * t:TOK * c + HALF * (t + 1)],
                                                   z[0:HALF, t, P * c:P * (c + 1)], ident[0:HALF, 0:HALF])
                last.then_inc(zT_done, 1)

            def gate(m):
                pe.wait_ge(zT_taken, m + 1)
                for t in range(2):
                    for c in range(2):
                        last = nc.tensor.matmul(p_gate[:, EXPERTS * t:EXPERTS * (t + 1)], zT[:, c, HALVES[t]],
                                                gate_w[:, c, :], start=(c == 0), stop=(c == 1))
                last.then_inc(gate_done, 1)

            def rank(m, k):
                pe.wait_ge(chosen_done, CHOOSE * (m + 1))
                if live(k, 3):
                    pe.wait_ge(oT_taken, m + 2)
                H = slice(0, HALF)
                nc.tensor.matmul(p_place[:, 0:EXPERTS], before[H, H], chosen[H, 0], start=True, stop=True)
                nc.tensor.matmul(p_place[:, EXPERTS:2 * EXPERTS], before[H, H], chosen[H, 1], start=True, stop=False)
                nc.tensor.matmul(p_place[:, EXPERTS:2 * EXPERTS], ones[H, H], chosen[H, 0], start=False, stop=True)
                nc.tensor.matmul(p_total, ones[H, :], chosen[H, 0], start=True, stop=False)
                nc.tensor.matmul(p_total, ones[H, :], chosen[H, 1], start=False, stop=True).then_inc(ranked, 1)

            for u in range(3):
                queries_keys(0, 0, u)
            pe.wait_ge(const, FILLS)

            def slot(n, k, pair, quad):
                for u in range(UNITS):
                    if live(k, 0):
                        scores(n, k, u, pair)
                    if u < TLAG and live(k, 2):
                        scores_turned(n - 2, k - 2, u - TLAG + UNITS)
                    if u >= TLAG and live(k, 1):
                        scores_turned(n - 1, k - 1, u - TLAG)
                    if u % 2 == 1:
                        s = (u - TLAG - 3) // 2
                        if s >= 0 and live(k, 1):
                            outputs(n - 1, k - 1, s, False)
                        if s < 0 and live(k, 2):
                            outputs(n - 2, k - 2, s + 6, live(k, 1))
                    if live(k, 1) and u == 1:
                        turn_max(n - 1, k)
                    if live(k, 4) and u == 1:
                        rank(n - 4, k)
                    if live(k, 3) and u == 1:
                        project(n - 3)
                    if makes_pair(k) and u in (2, 5, 8):
                        queries_keys(pair + 1, (k // 2 + 1) % 2, (u - 2) // 3)
                    if live(k, 3) and u == 7:
                        turn_z(n - 3, k)
                    if live(k, 3) and u == 9:
                        gate(n - 3)
                    if live(k, 2) and u == 9:
                        pick_outputs(n - 2)
                    if live(k, 0) and u == 11:
                        values(n, k, pair)
                    if live(k, 2) and u == 11:
                        turn_outputs(n - 2, k)
            over_slots(pe, slot)


def shared_by_phase_c(shared):
    at = [0]

    def take(pattern, **sizes):
        n = prod(sizes.values())
        at[0] += n
        return shared[:, at[0] - n:at[0]].rearrange(pattern, **sizes)

    w1_raw = take("p (e k h) -> p e k h", e=EXPERTS, k=3, h=HID)
    w2_raw = take("p (e k c) -> p e k c", e=EXPERTS, k=KH, c=C)
    b2 = take("p (e c) -> p e c", e=EXPERTS, c=C)
    rows = take("p (b r) -> p b r", b=RING, r=ROW)
    z, hid, y, result = (take("p (b c) -> p b c", b=2, c=n) for n in (C, HID, C, C))
    return w1_raw, w2_raw, b2, rows, z, hid, y, result


def phase_c(nc, a, sb, ps, sem, shared, raw_loaded, ident, rows_dram, tile_expert, tile_row):
    with ExitStack() as st:
        w1_raw, w2_raw, b2, rows, z, hid, y, result = shared_by_phase_c(shared)
        w1 = sb(st, "w1", [P, EXPERTS, 4, HID], F32R)
        w2 = sb(st, "w2", [P, EXPERTS, KH, 2, C], F32R)
        identr = sb(st, "identr", [P, P], F32R)
        zz = sb(st, "z_parts", [P, 2, 2 * C], F32R)
        zT = sb(st, "zT_c", [P, 2, 4, P], F32R)
        hidT = sb(st, "hidT", [P, 2, 2, HID], F32R)
        token = sb(st, "token", [P, RING, 1], I32)
        p_z = ps(st, "p_z", [P, 3, P])
        p_h = [ps(st, f"p_hid{i}", [P, 512]) for i in range(2)]
        p_hT = [ps(st, f"p_hidT{i}", [P, 512]) for i in range(2)]
        p_y = [ps(st, f"p_y{i}", [P, 512]) for i in range(2)]
        HH = HID // 2

        w1_high, w1_done, w2_high, w2_done, const = (
            sem("c_" + n) for n in ("w1_high", "w1_done", "w2_high", "w2_done", "const"))
        loaded = [sem(f"c_rows{i}") for i in range(RING)]
        z_done, zhigh_done, zlow_done, zT_done, zT_taken, h_done, gelu_done, hT_done, hT_high, hT_low = (
            sem("c_" + n) for n in ("z", "z_high", "z_low", "zT", "zT_taken", "hid", "gelu", "hidT", "hidT_high",
                                    "hidT_low"))
        y_done, summed, token_done, result_done = (sem("c_" + n) for n in ("y", "summed", "token", "result"))
        stored = [sem(f"c_stored{i}") for i in range(2)]
        waited_pool = sem("c_waited_pool")
        block = st.enter_context(nc.Block())

        def over_steps(eng, step):
            for t in range(RING):
                step(t, t, t // 2, 0)
            with eng.Fori(1, TILES // RING - 1) as i:
                for k in range(RING, 2 * RING):
                    step(RING * i + k - RING, k, RING // 2 * i + (k - RING) // 2, i)
            for t in range(TILES - RING, TILES + 2):
                step(t, t, t // 2, t // RING)

        def live(k, behind):
            return 0 <= k - behind < TILES

        @block.sync
        def _(sp):
            def step(t, k, half, rnd):
                if live(k, 0):
                    if k >= RING:
                        sp.wait_ge(result_done, t - RING + 1)
                    first = sp.value_load(tile_row[0:1, bass.ds(t, 1)], min_val=0, max_val=SPARE)
                    sp.dma_start(rows[:, k % RING, :], rows_dram[bass.ds(first, P), :]).then_inc(loaded[k % RING], 16)
            over_steps(sp, step)

        @block.gpsimd
        def _(pool):
            pool.wait_ge(raw_loaded, RAW_LOADS)
            for e in range(EXPERTS):
                nc.gpsimd.tensor_copy(w2[:, e, :, 0], w2_raw[:, e]).then_inc(w2_high, 1)
            def step(t, k, half, rnd):
                if live(k, 2):
                    pool.wait_ge(result_done, t - 1)
                    pool.wait_ge(token_done, t - 1)
                    settled(pool, waited_pool)
                    nc.gpsimd.indirect_dma_start(
                        out=a["out"], out_offset=bass.IndirectOffsetOnAxis(ap=token[:, (k - 2) % RING, :], axis=0),
                        in_=result[:, k % 2, :], in_offset=None, bounds_check=ALL - 1, oob_is_err=False)\
                        .then_inc(stored[k % 2], 16)
            over_steps(pool, step)
            for b in range(2):
                pool.wait_ge(stored[b], 16 * TILES // 2)

        @block.vector
        def _(dve):
            dve.wait_ge(raw_loaded, RAW_LOADS)
            for e in range(EXPERTS):
                dve.wait_ge(w1_high, 3 * e + 1)
                nc.vector.tensor_tensor(w1[:, e, 1], w1_raw[:, e, 0], w1[:, e, 0], ALU.subtract).then_inc(w1_done, 1)
                dve.wait_ge(w1_high, 3 * e + 3)
                nc.vector.tensor_tensor(w1[0:96, e, 3], w1_raw[0:96, e, 2], w1[0:96, e, 3], ALU.subtract).then_inc(w1_done, 1)

            def normalise(t, k, half, rnd):
                slot = k % RING
                dve.wait_ge(loaded[slot], 16 * (rnd + 1))
                at_least(dve, zlow_done, 2 * t - 2)
                row = rows[:, slot, :]
                nc.vector.tensor_scalar(z[:, k % 2], row[:, 0:C], row[:, MEAN:MEAN + 1], row[:, RSTD:RSTD + 1],
                                        ALU.subtract, ALU.mult).then_inc(z_done, 1)
                at_least(dve, stored[k % 2], 16 * (half - RING // 2 + 1))
                nc.vector.tensor_copy(token[:, slot, :], row[:, TOKEN:ROW]).then_inc(token_done, 1)

            def low_z(t, b):
                dve.wait_ge(zhigh_done, t + 1)
                for into, features in ((slice(C, C + 64), slice(P, C)), (slice(C + 64, 2 * C), slice(0, P))):
                    nc.vector.tensor_tensor(zz[:, b, into], z[:, b, features], zz[:, b, features],
                                            ALU.subtract).then_inc(zlow_done, 1)

            def low_hidden(t, b, part):
                dve.wait_ge(hT_high, 2 * t + part + 1)
                at = slice(HH * part, HH * (part + 1))
                nc.vector.tensor_tensor(hidT[:, b, 1, at], p_hT[part][:, 0:HH], hidT[:, b, 0, at],
                                        ALU.subtract).then_inc(hT_low, 1)

            def finish(t, k, half):
                dve.wait_ge(y_done, t + 1)
                at_least(dve, result_done, t)
                expert = dve.value_load(tile_expert[0:1, bass.ds(t, 1)], min_val=0, max_val=EXPERTS - 1)
                nc.vector.tensor_tensor(y[:, 0], p_y[k % 2][:, 0:C], b2[:, bass.ds(expert, 1), :]
                                        .rearrange("p e c -> p (e c)"), ALU.add).then_inc(summed, 1)
                nc.vector.tensor_tensor(y[:, 1], p_y[k % 2][:, C:2 * C], rows[:, k % RING, 0:C],
                                        ALU.add).then_inc(summed, 1)
                dve.wait_ge(summed, 2 * t + 2)
                at_least(dve, stored[k % 2], 16 * half)
                nc.vector.tensor_tensor(result[:, k % 2], y[:, 0], y[:, 1], ALU.add).then_inc(result_done, 1)

            def step(t, k, half, rnd):
                def after(n):
                    return t + n, k + n, half + (k + n) // 2 - k // 2, rnd + (k + n) // RING - k // RING

                if k == 0:
                    normalise(*after(0))
                    low_z(t, 0)
                    normalise(*after(1))
                    for e in range(EXPERTS):
                        dve.wait_ge(w2_high, e + 1)
                        nc.vector.tensor_tensor(w2[:, e, :, 1], w2_raw[:, e], w2[:, e, :, 0], ALU.subtract).then_inc(w2_done, 1)
                if live(k, -1):
                    low_z(t + 1, (k + 1) % 2)
                if live(k, 1):
                    for part in range(2):
                        low_hidden(t - 1, (k - 1) % 2, part)
                if live(k, 2):
                    finish(t - 2, k - 2, half - 1)
                if live(k, -2):
                    normalise(*after(2))
            over_steps(dve, step)

        @block.scalar
        def _(act):
            nc.scalar.copy(identr[:], ident[:]).then_inc(const, 1)
            for b in range(2):
                nc.scalar.activation(zT[:, b, 3], ident[:], ACT.Copy, scale=0.0, bias=1.0).then_inc(const, 1)
            act.wait_ge(raw_loaded, RAW_LOADS)
            for e in range(EXPERTS):
                for into, chunk in ((0, 0), (2, 1), (3, 2)):
                    nc.scalar.copy(w1[:, e, into], w1_raw[:, e, chunk]).then_inc(w1_high, 1)

            def high_z(t, b):
                act.wait_ge(z_done, t + 1)
                at_least(act, zT_done, t - 1)
                nc.scalar.copy(zz[:, b, 0:C], z[:, b]).then_inc(zhigh_done, 1)

            def take_z(t, b):
                act.wait_ge(zT_done, t + 1)
                at_least(act, h_done, 2 * t - 2)
                nc.scalar.copy(zT[:, b, 0:3], p_z[:]).then_inc(zT_taken, 1)
                nc.scalar.copy(zT[0:64, b, 3], p_z[0:64, 1]).then_inc(zT_taken, 1)

            def high_hidden(t, b, part):
                act.wait_ge(hT_done, 2 * t + part + 1)
                at_least(act, y_done, t - 1)
                nc.scalar.copy(hidT[:, b, 0, HH * part:HH * (part + 1)], p_hT[part][:, 0:HH]).then_inc(hT_high, 1)

            def step(t, k, half, rnd):
                if k == 0:
                    high_z(t, 0)
                    take_z(t, 0)
                    high_z(t + 1, 1)
                if live(k, 1):
                    for part in range(2):
                        high_hidden(t - 1, (k - 1) % 2, part)
                if live(k, 0):
                    for part in range(2):
                        act.wait_ge(h_done, 2 * t + part + 1)
                        at_least(act, hT_done, 2 * t - 2)
                        nc.scalar.activation(hid[:, k % 2, HH * part:HH * (part + 1)], p_h[part][:, 0:HH],
                                             ACT.Gelu).then_inc(gelu_done, 1)
                if live(k, -2):
                    high_z(t + 2, k % 2)
                if live(k, -1):
                    take_z(t + 1, (k + 1) % 2)
            over_steps(act, step)

        @block.tensor
        def _(pe):
            pe.wait_ge(const, 3)

            def turn_z(t, b):
                pe.wait_ge(zlow_done, 2 * t + 2)
                at_least(pe, zT_taken, 2 * t)
                for c in range(3):
                    last = nc.tensor.transpose(p_z[:, c, :].bitcast(F32R), zz[:, b, P * c:P * (c + 1)], identr[:])
                last.then_inc(zT_done, 1)

            def first_layer(t, b, part, expert):
                pe.wait_ge(zT_taken, 2 * t + 2)
                at_least(pe, gelu_done, 2 * t + part - 1)
                for i, (c, w) in enumerate(PRODUCTS):
                    last = nc.tensor.matmul(p_h[part][:, 0:HH], zT[:, b, c, :],
                                            w1[:, bass.ds(expert, 1), w, HH * part:HH * (part + 1)]
                                            .rearrange("p e h -> p (e h)"), start=(i == 0),
                                            stop=(i == len(PRODUCTS) - 1))
                last.then_inc(h_done, 1)

            def turn_hidden(t, b, part):
                pe.wait_ge(gelu_done, 2 * t + part + 1)
                at_least(pe, hT_low, 2 * t + part - 1)
                for m in range(3):
                    at = HH * part + P * m
                    last = nc.tensor.transpose(p_hT[part][:, P * m:P * (m + 1)], hid[:, b, at:at + P], ident[:])
                last.then_inc(hT_done, 1)

            def second_layer(t, b, expert):
                at_least(pe, summed, 2 * t - 2)
                for m in range(KH):
                    if m % 3 == 0:
                        pe.wait_ge(hT_high, 2 * t + m // 3 + 1)
                    nc.tensor.matmul(p_y[b][:, 0:2 * C], hidT[:, b, 0, P * m:P * (m + 1)],
                                     w2[:, bass.ds(expert, 1), m].rearrange("p e i c -> p (e i c)"),
                                     start=(m == 0), stop=False)
                for m in range(KH):
                    if m % 3 == 0:
                        pe.wait_ge(hT_low, 2 * t + m // 3 + 1)
                    last = nc.tensor.matmul(p_y[b][:, 0:C], hidT[:, b, 1, P * m:P * (m + 1)],
                                            w2[:, bass.ds(expert, 1), m, 0].rearrange("p e c -> p (e c)"),
                                            start=False, stop=(m == KH - 1))
                last.then_inc(y_done, 1)

            experts = {}

            def expert_of(t, k):
                if k not in experts:
                    experts[k] = pe.value_load(tile_expert[0:1, bass.ds(t, 1)], min_val=0, max_val=EXPERTS - 1)
                return experts[k]

            def step(t, k, half, rnd):
                if k == RING:
                    experts.clear()
                if k == 0:
                    turn_z(t, 0)
                    pe.wait_ge(w1_done, 2 * EXPERTS)
                if live(k, 1):
                    last_expert = expert_of(t - 1, k - 1)
                    for part in range(2):
                        turn_hidden(t - 1, (k - 1) % 2, part)
                if live(k, 0):
                    for part in range(2):
                        first_layer(t, k % 2, part, expert_of(t, k))
                if live(k, -1):
                    turn_z(t + 1, (k + 1) % 2)
                if k == 1:
                    pe.wait_ge(w2_done, EXPERTS)
                if live(k, 1):
                    second_layer(t - 1, (k - 1) % 2, last_expert)
                if live(k, -1) and (isinstance(t, int) or k < 2 * RING - 1):
                    expert_of(t + 1, k + 1)
            over_steps(pe, step)


def kernel(x, L0_tok_W, L0_tok_b, L0_attn_qkv_weight, L0_attn_qkv_bias, L0_attn_proj_weight, L0_attn_proj_bias,
           L0_ffn_gate_w, L0_ffn_gate_b, L0_ffn_gate_center, L0_ffn_w1, L0_ffn_b1, L0_ffn_w2, L0_ffn_b2):
    import numpy as np
    from concourse import bacc
    from concourse.bass_utils import run_bass_kernel_spmd

    x = np.asarray(x).reshape(IMAGES, CHANNELS, GRID, PATCH, GRID, PATCH)
    patches = np.ascontiguousarray(x.transpose(1, 3, 5, 0, 2, 4).reshape(D_IN, ALL))

    def with_bias(w, b):
        out = np.zeros((3 * P, w.shape[1]), np.float32)
        out[:C] = w
        out[C:2 * P] = out[2 * P:2 * P + 64] = w[P:C]
        out[2 * P + 64] = out[2 * P + 96] = b
        return out

    def by_dim(first, heads):
        return [first + h * HD + d for d in range(HD) for h in heads]

    order = (by_dim(0, range(8)) + by_dim(C, range(8)) + by_dim(0, range(8, 12)) + by_dim(C, range(8, 12))
             + list(range(2 * C, 3 * C)))
    qkv_w = with_bias(np.asarray(L0_attn_qkv_weight).T[:, order], np.asarray(L0_attn_qkv_bias)[order])
    proj_w = np.zeros((2 * P, C), np.float32)
    proj_w[:C] = np.asarray(L0_attn_proj_weight).T
    proj_w[C] = np.asarray(L0_attn_proj_bias)
    w1 = np.stack([with_bias(w, b) for w, b in zip(np.asarray(L0_ffn_w1), np.asarray(L0_ffn_b1))])
    gate_w = np.zeros((2 * P, EXPERTS), np.float32)
    gate_w[:C] = np.asarray(L0_ffn_gate_w)
    arrays = {
        "patches": patches,
        "tok_w": np.ascontiguousarray(np.asarray(L0_tok_W).T),
        "tok_b": np.asarray(L0_tok_b),
        "qkv_w": qkv_w,
        "proj_w": proj_w,
        "gate_w": gate_w,
        "gate_b": np.asarray(L0_ffn_gate_b),
        "gate_c": np.asarray(L0_ffn_gate_center),
        "w1": w1,
        "w2": np.asarray(L0_ffn_w2),
        "b2": np.asarray(L0_ffn_b2).reshape(-1),
    }
    nc = bacc.Bacc("TRN2", target_bir_lowering=False, num_devices=1)
    a = {n: nc.dram_tensor("in_" + n, v.shape, F32, kind="ExternalInput").ap() for n, v in arrays.items()}
    a["out"] = nc.dram_tensor("out", [ALL, C], F32, kind="ExternalOutput").ap()
    vit_block(nc, a)
    r = run_bass_kernel_spmd(nc, [{"in_" + n: v for n, v in arrays.items()}], core_ids=[0])
    return r.results[0]["out"].reshape(IMAGES, TOK, C)
```
